# Optimizing a Trainium2 kernel written in Bass

```python
import numpy as np
import jax
import jax.numpy as jnp

def _softmax(x, axis=-1):
    return jax.nn.softmax(x, axis=axis)

def _gelu(x):
    return jax.nn.gelu(x, approximate=True)

def _silu(x):
    return jax.nn.silu(x)

def _sigmoid(x):
    return jax.nn.sigmoid(x)

def _layernorm(x, axis=-1, eps=1e-05):
    m = jnp.mean(x, axis=axis, keepdims=True)
    v = jnp.var(x, axis=axis, keepdims=True)
    return (x - m) / jnp.sqrt(v + eps)

def _scatter_add(tgt, idx, src, axis=0):
    return tgt.at[idx].add(src)

def _segment_sum(src, seg, n):
    return jax.ops.segment_sum(src, seg, n)
kernel_name = 'mk_perceiver_d2_seqx_r2_bcb535'

def setup_inputs(seed: int=0):
    np.random.seed(seed)
    _w = jnp.asarray

    def _rec_inputs():
        import jax
        import jax.numpy as jnp
        _rk = jax.random.key(seed)
        x = -0.0002928 + 1 * jax.random.normal(jax.random.fold_in(_rk, 1), (32, 32, 512), jnp.float32)
        _lenS = 32 - jax.random.randint(jax.random.fold_in(_rk, 7), (32,), 0, max(1, 32 // 4) + 1, jnp.int32)
        _lenS2 = 257 - jax.random.randint(jax.random.fold_in(_rk, 8), (32,), 0, max(1, 257 // 4) + 1, jnp.int32)
        _ctx_1024P = jax.random.normal(jax.random.fold_in(_rk, 11), (32, 16, 512), jnp.float32)
        _ctx_1024c = jax.random.dirichlet(jax.random.fold_in(_rk, 511), 0.3 * jnp.ones((16,), jnp.float32), (32, 257))
        _ctx_1024t = jnp.einsum('bsk,bkd->bsd', _ctx_1024c, _ctx_1024P)
        _ctx_1024t = _ctx_1024t * jax.lax.rsqrt(jnp.mean(jnp.square(_ctx_1024t)) + 1e-12) * 0.953939
        ctx_1024 = -1.39393e-06 + 0.999914 * (_ctx_1024t + 0.3 * jax.random.normal(jax.random.fold_in(_rk, 611), (32, 257, 512), jnp.float32))
        _validS = jnp.arange(32)[None, :] < _lenS[:, None]
        _validS2 = jnp.arange(257)[None, :] < _lenS2[:, None]
        _causal = jnp.tril(jnp.ones((32, 32), dtype=bool))
        mask_Bx1xS2_if1 = jnp.where(jnp.ones((32, 1, 257), dtype=bool), 1, 0).astype(jnp.int32)
        return (x, ctx_1024, mask_Bx1xS2_if1)
    x, ctx_1024, mask_Bx1xS2_if1 = _rec_inputs()

    def _L0_xattn_setup():
        import jax, jax.numpy as jnp
        import numpy as np
        H = 16
        D_MODEL = 512
        D_K = D_MODEL // H
        NEG = -1000000000.0

        def _split_heads(x):
            B, S, _ = x.shape
            return x.reshape(B, S, H, D_K).transpose(0, 2, 1, 3)
        key = jax.random.key(seed)
        ks = jax.random.split(key, 12)
        B, S = (2, 1024)
        inp = {'query': jax.random.normal(ks[0], (B, S, D_MODEL), jnp.float32), 'key': jax.random.normal(ks[1], (B, S, D_MODEL), jnp.float32), 'value': jax.random.normal(ks[2], (B, S, D_MODEL), jnp.float32), 'mask': jnp.ones((B, 1, S), jnp.int32)}
        s = 1.0 / np.sqrt(D_MODEL)
        for i, nm in enumerate(['Wq', 'Wk', 'Wv', 'Wo']):
            inp[nm] = jax.random.normal(ks[3 + i], (D_MODEL, D_MODEL), jnp.float32) * s
            inp['b' + nm[1]] = jax.random.normal(ks[7 + i], (D_MODEL,), jnp.float32) * s
        return inp
    _L0_xattn_all = _L0_xattn_setup()
    _L0_xattn_in = {k: v for k, v in _L0_xattn_all.items() if k in ('Wq', 'bq', 'Wk', 'bk', 'Wv', 'bv', 'Wo', 'bo')}
    del _L0_xattn_all

    def _L0_attn_setup():
        import jax, jax.numpy as jnp
        import numpy as np
        NUM_HEADS = 16
        USE_MASKING = True
        NEG_INF = -1000000000.0
        key = jax.random.key(seed)
        k1, k2 = jax.random.split(key)
        B, S, D = (2, 1024, 512)
        x = jax.random.normal(k1, (B, S, D), dtype=jnp.float32)
        qkv_weights = jax.random.normal(k2, (D, 3 * D), dtype=jnp.float32) * (1.0 / np.sqrt(D))
        return {'x': x, 'qkv_weights': qkv_weights}
    _L0_attn_all = _L0_attn_setup()
    _L0_attn_in = {k: v for k, v in _L0_attn_all.items() if k in ('qkv_weights',)}
    del _L0_attn_all

    def _L0_ffn_setup():
        import jax, jax.numpy as jnp
        import numpy as np
        import math
        D = 512
        H = 16
        E = 8
        TOPK = 2
        LAT = D // 2
        KPH = LAT // H
        HD = D // H

        def _forward(hs, q_w, q_b, k_w, k_b, v_w, v_b, o_w, o_b, router_w, router_b, w1, b1, w2, b2):
            B, S, _ = hs.shape
            Q = (hs @ q_w + q_b).reshape(B, S, H, HD).transpose(0, 2, 1, 3)
            K = (hs @ k_w + k_b).reshape(B, S, H, KPH).transpose(0, 2, 1, 3)
            V = (hs @ v_w + v_b).reshape(B, S, H, KPH).transpose(0, 2, 1, 3)
            scores = jnp.einsum('bhsk,bhtk->bhst', Q[..., :KPH], K) / math.sqrt(KPH)
            attn = jax.nn.softmax(scores, axis=-1)
            ao = jnp.einsum('bhst,bhtv->bhsv', attn, V)
            ao = ao.transpose(0, 2, 1, 3).reshape(B, S, H * KPH)
            ao = jnp.concatenate([ao, jnp.zeros((B, S, D - LAT), ao.dtype)], axis=-1)
            mla_out = ao @ o_w + o_b
            probs = jax.nn.softmax(mla_out @ router_w + router_b, axis=-1)
            topw, topi = jax.lax.top_k(probs, TOPK)
            topw = topw / (topw.sum(-1, keepdims=True) + 1e-08)
            combine = jnp.sum(jax.nn.one_hot(topi, E, dtype=probs.dtype) * topw[..., None], axis=-2)
            h1 = jnp.einsum('bsd,edf->ebsf', mla_out, w1) + b1[:, None, None, :]
            h1 = jax.nn.gelu(h1, approximate=False)
            h2 = jnp.einsum('ebsf,efd->ebsd', h1, w2) + b2[:, None, None, :]
            moe_out = jnp.einsum('bse,ebsd->bsd', combine, h2)
            return hs + 0.3 * moe_out
        key = jax.random.key(seed)
        ks = jax.random.split(key, 16)
        s = 0.02
        inp = {'hidden_states': jax.random.normal(ks[0], (2, 1024, D), jnp.float32), 'q_w': jax.random.normal(ks[1], (D, D), jnp.float32) * s, 'q_b': jnp.zeros((D,), jnp.float32), 'k_w': jax.random.normal(ks[2], (D, LAT), jnp.float32) * s, 'k_b': jnp.zeros((LAT,), jnp.float32), 'v_w': jax.random.normal(ks[3], (D, LAT), jnp.float32) * s, 'v_b': jnp.zeros((LAT,), jnp.float32), 'o_w': jax.random.normal(ks[4], (D, D), jnp.float32) * s, 'o_b': jnp.zeros((D,), jnp.float32), 'router_w': jax.random.normal(ks[5], (D, E), jnp.float32) * s, 'router_b': jnp.zeros((E,), jnp.float32), 'w1': jax.random.normal(ks[6], (E, D, 2 * D), jnp.float32) * s, 'b1': jnp.zeros((E, 2 * D), jnp.float32), 'w2': jax.random.normal(ks[7], (E, 2 * D, D), jnp.float32) * s, 'b2': jnp.zeros((E, D), jnp.float32)}
        return inp
    _L0_ffn_all = _L0_ffn_setup()
    _L0_ffn_in = {k: v for k, v in _L0_ffn_all.items() if k in ('q_w', 'q_b', 'k_w', 'k_b', 'v_w', 'v_b', 'o_w', 'o_b', 'router_w', 'router_b', 'w1', 'b1', 'w2', 'b2')}
    del _L0_ffn_all

    def _L1_xattn_setup():
        import jax, jax.numpy as jnp
        import numpy as np
        B, S, D = (8, 1024, 512)
        key = jax.random.key(seed)
        kq, kk, kv = jax.random.split(key, 3)
        qm = jax.random.normal(kq, (B, S, D), dtype=jnp.float32)
        km = jax.random.normal(kk, (B, S, D), dtype=jnp.float32)
        vm = jax.random.normal(kv, (B, S, D), dtype=jnp.float32)
        return {'qm': qm, 'km': km, 'vm': vm}
    _L1_xattn_all = _L1_xattn_setup()
    _L1_xattn_in = {k: v for k, v in _L1_xattn_all.items() if k in ()}
    del _L1_xattn_all

    def _L1_attn_setup():
        import jax, jax.numpy as jnp
        import numpy as np
        D = 512
        HS = 128
        NKV = 2

        def apply_rope(x):
            d = x.shape[-1]
            T = x.shape[-2]
            positions = jnp.arange(0, d, 2, dtype=jnp.float32)
            theta = 10000.0 ** (-2.0 * positions / d)
            angles = jnp.arange(T, dtype=jnp.float32)[:, None] * theta[None, :]
            cos, sin = (jnp.cos(angles), jnp.sin(angles))
            xr = x.reshape(x.shape[:-1] + (d // 2, 2))
            out = jnp.stack([xr[..., 0] * cos - xr[..., 1] * sin, xr[..., 1] * cos + xr[..., 0] * sin], axis=-1)
            return out.reshape(x.shape)
        key = jax.random.key(seed)
        k1, k2, k3, k4, k5 = jax.random.split(key, 5)
        B, T = (4, 1024)
        x = jax.random.normal(k1, (B, T, D), dtype=jnp.float32)
        s = 1.0 / np.sqrt(D)
        Wq = jax.random.normal(k2, (NKV, HS, D), dtype=jnp.float32) * s
        Wk = jax.random.normal(k3, (HS, D), dtype=jnp.float32) * s
        Wv = jax.random.normal(k4, (HS, D), dtype=jnp.float32) * s
        Wo = jax.random.normal(k5, (D, NKV * HS), dtype=jnp.float32) * (1.0 / np.sqrt(NKV * HS))
        return {'x': x, 'Wq': Wq, 'Wk': Wk, 'Wv': Wv, 'Wo': Wo}
    _L1_attn_all = _L1_attn_setup()
    _L1_attn_in = {k: v for k, v in _L1_attn_all.items() if k in ('Wq', 'Wk', 'Wv', 'Wo')}
    del _L1_attn_all

    def _L1_ffn_setup():
        import jax, jax.numpy as jnp
        import numpy as np
        N_EXPERTS = 8
        TOP_K = 2
        key = jax.random.key(seed)
        k1, k2, k3, k4 = jax.random.split(key, 4)
        B, T, C, H, E = (2, 1024, 512, 2048, N_EXPERTS)
        x = jax.random.normal(k1, (B, T, C), dtype=jnp.float32)
        router_w = jax.random.normal(k2, (E, C), dtype=jnp.float32) * 0.02
        w1 = jax.random.normal(k3, (E, C, H), dtype=jnp.float32) * (1.0 / np.sqrt(C))
        w2 = jax.random.normal(k4, (E, H, C), dtype=jnp.float32) * (1.0 / np.sqrt(H))
        return {'x': x, 'router_w': router_w, 'w1': w1, 'w2': w2}
    _L1_ffn_all = _L1_ffn_setup()
    _L1_ffn_in = {k: v for k, v in _L1_ffn_all.items() if k in ('router_w', 'w1', 'w2')}
    del _L1_ffn_all
    return {'x': x, 'ctx_1024': ctx_1024, 'mask_Bx1xS2_if1': mask_Bx1xS2_if1, 'L0_xattn_Wq': _L0_xattn_in['Wq'], 'L0_xattn_bq': _L0_xattn_in['bq'], 'L0_xattn_Wk': _L0_xattn_in['Wk'], 'L0_xattn_bk': _L0_xattn_in['bk'], 'L0_xattn_Wv': _L0_xattn_in['Wv'], 'L0_xattn_bv': _L0_xattn_in['bv'], 'L0_xattn_Wo': _L0_xattn_in['Wo'], 'L0_xattn_bo': _L0_xattn_in['bo'], 'L0_attn_qkv_weights': _L0_attn_in['qkv_weights'], 'L0_ffn_q_w': _L0_ffn_in['q_w'], 'L0_ffn_q_b': _L0_ffn_in['q_b'], 'L0_ffn_k_w': _L0_ffn_in['k_w'], 'L0_ffn_k_b': _L0_ffn_in['k_b'], 'L0_ffn_v_w': _L0_ffn_in['v_w'], 'L0_ffn_v_b': _L0_ffn_in['v_b'], 'L0_ffn_o_w': _L0_ffn_in['o_w'], 'L0_ffn_o_b': _L0_ffn_in['o_b'], 'L0_ffn_router_w': _L0_ffn_in['router_w'], 'L0_ffn_router_b': _L0_ffn_in['router_b'], 'L0_ffn_w1': _L0_ffn_in['w1'], 'L0_ffn_b1': _L0_ffn_in['b1'], 'L0_ffn_w2': _L0_ffn_in['w2'], 'L0_ffn_b2': _L0_ffn_in['b2'], 'L1_attn_Wq': _L1_attn_in['Wq'], 'L1_attn_Wk': _L1_attn_in['Wk'], 'L1_attn_Wv': _L1_attn_in['Wv'], 'L1_attn_Wo': _L1_attn_in['Wo'], 'L1_ffn_router_w': _L1_ffn_in['router_w'], 'L1_ffn_w1': _L1_ffn_in['w1'], 'L1_ffn_w2': _L1_ffn_in['w2']}

def reference(x, ctx_1024, mask_Bx1xS2_if1, L0_xattn_Wq, L0_xattn_bq, L0_xattn_Wk, L0_xattn_bk, L0_xattn_Wv, L0_xattn_bv, L0_xattn_Wo, L0_xattn_bo, L0_attn_qkv_weights, L0_ffn_q_w, L0_ffn_q_b, L0_ffn_k_w, L0_ffn_k_b, L0_ffn_v_w, L0_ffn_v_b, L0_ffn_o_w, L0_ffn_o_b, L0_ffn_router_w, L0_ffn_router_b, L0_ffn_w1, L0_ffn_b1, L0_ffn_w2, L0_ffn_b2, L1_attn_Wq, L1_attn_Wk, L1_attn_Wv, L1_attn_Wo, L1_ffn_router_w, L1_ffn_w1, L1_ffn_w2):
    import jax
    import jax.numpy as jnp

    def _L0_xattn_ref(query, key, value, mask, Wq, bq, Wk, bk, Wv, bv, Wo, bo):
        import jax, jax.numpy as jnp
        import numpy as np
        H = 16
        D_MODEL = 512
        D_K = D_MODEL // H
        NEG = -1000000000.0

        def _split_heads(x):
            B, S, _ = x.shape
            return x.reshape(B, S, H, D_K).transpose(0, 2, 1, 3)
        q = _split_heads(query @ Wq + bq)
        k = _split_heads(key @ Wk + bk)
        v = _split_heads(value @ Wv + bv)
        scores = jnp.einsum('bhqd,bhkd->bhqk', q, k) / jnp.sqrt(jnp.float32(D_K))
        scores = jnp.where(mask[:, None, :, :] == 0, NEG, scores)
        attn = jax.nn.softmax(scores, axis=-1)
        out = jnp.einsum('bhqk,bhkd->bhqd', attn, v)
        B, _, Sq, _ = out.shape
        out = out.transpose(0, 2, 1, 3).reshape(B, Sq, H * D_K)
        return out @ Wo + bo

    def _L0_attn_ref(x, qkv_weights):
        import jax, jax.numpy as jnp
        import numpy as np
        NUM_HEADS = 16
        USE_MASKING = True
        NEG_INF = -1000000000.0
        B, S, D = x.shape
        H = NUM_HEADS
        Dh = D // H
        qkv = jnp.einsum('bsd,de->bse', x, qkv_weights)
        qkv = qkv.reshape(-1, 3 * D)
        pre_q = qkv[:, 0 * D:1 * D].reshape(-1, S, H, Dh)
        pre_k = qkv[:, 1 * D:2 * D].reshape(-1, S, H, Dh)
        pre_v = qkv[:, 2 * D:3 * D].reshape(-1, S, H, Dh)
        q = jnp.transpose(pre_q, (0, 2, 1, 3)).reshape(-1, S, Dh)
        v = jnp.transpose(pre_v, (0, 2, 1, 3)).reshape(-1, S, Dh)
        k = jnp.transpose(pre_k, (0, 2, 3, 1)).reshape(-1, S, Dh)
        scale = jnp.asarray(np.sqrt(Dh), dtype=x.dtype)
        a = jnp.einsum('aib,ajb->aij', q, k) / scale
        if USE_MASKING:
            tril = jnp.tril(jnp.ones((S, S), dtype=x.dtype))[None]
            a = tril * a + NEG_INF * (1.0 - tril)
        a = jax.nn.softmax(a, axis=-1)
        heads = jnp.einsum('aij,ajb->aib', a, v)
        heads = heads.reshape(-1, H, S, Dh)
        heads = jnp.transpose(heads, (0, 2, 1, 3)).reshape(-1, S, D)
        return heads

    def _L0_ffn_ref(hidden_states, q_w, q_b, k_w, k_b, v_w, v_b, o_w, o_b, router_w, router_b, w1, b1, w2, b2):
        import jax, jax.numpy as jnp
        import numpy as np
        import math
        D = 512
        H = 16
        E = 8
        TOPK = 2
        LAT = D // 2
        KPH = LAT // H
        HD = D // H

        def _forward(hs, q_w, q_b, k_w, k_b, v_w, v_b, o_w, o_b, router_w, router_b, w1, b1, w2, b2):
            B, S, _ = hs.shape
            Q = (hs @ q_w + q_b).reshape(B, S, H, HD).transpose(0, 2, 1, 3)
            K = (hs @ k_w + k_b).reshape(B, S, H, KPH).transpose(0, 2, 1, 3)
            V = (hs @ v_w + v_b).reshape(B, S, H, KPH).transpose(0, 2, 1, 3)
            scores = jnp.einsum('bhsk,bhtk->bhst', Q[..., :KPH], K) / math.sqrt(KPH)
            attn = jax.nn.softmax(scores, axis=-1)
            ao = jnp.einsum('bhst,bhtv->bhsv', attn, V)
            ao = ao.transpose(0, 2, 1, 3).reshape(B, S, H * KPH)
            ao = jnp.concatenate([ao, jnp.zeros((B, S, D - LAT), ao.dtype)], axis=-1)
            mla_out = ao @ o_w + o_b
            probs = jax.nn.softmax(mla_out @ router_w + router_b, axis=-1)
            topw, topi = jax.lax.top_k(probs, TOPK)
            topw = topw / (topw.sum(-1, keepdims=True) + 1e-08)
            combine = jnp.sum(jax.nn.one_hot(topi, E, dtype=probs.dtype) * topw[..., None], axis=-2)
            h1 = jnp.einsum('bsd,edf->ebsf', mla_out, w1) + b1[:, None, None, :]
            h1 = jax.nn.gelu(h1, approximate=False)
            h2 = jnp.einsum('ebsf,efd->ebsd', h1, w2) + b2[:, None, None, :]
            moe_out = jnp.einsum('bse,ebsd->bsd', combine, h2)
            return hs + 0.3 * moe_out
        return _forward(hidden_states, q_w, q_b, k_w, k_b, v_w, v_b, o_w, o_b, router_w, router_b, w1, b1, w2, b2)

    def _L1_xattn_ref(qm, km, vm):
        import jax, jax.numpy as jnp
        import numpy as np
        B, S, D = (8, 1024, 512)
        scale = 1.0 / jnp.sqrt(jnp.asarray(qm.shape[-1], dtype=qm.dtype))
        qkm = jnp.einsum('bqd,bkd->bqk', qm, km) * scale
        out = jnp.einsum('bqk,bkd->bqd', qkm, vm)
        return jax.nn.softmax(out, axis=-1)

    def _L1_attn_ref(x, Wq, Wk, Wv, Wo):
        import jax, jax.numpy as jnp
        import numpy as np
        D = 512
        HS = 128
        NKV = 2

        def apply_rope(x):
            d = x.shape[-1]
            T = x.shape[-2]
            positions = jnp.arange(0, d, 2, dtype=jnp.float32)
            theta = 10000.0 ** (-2.0 * positions / d)
            angles = jnp.arange(T, dtype=jnp.float32)[:, None] * theta[None, :]
            cos, sin = (jnp.cos(angles), jnp.sin(angles))
            xr = x.reshape(x.shape[:-1] + (d // 2, 2))
            out = jnp.stack([xr[..., 0] * cos - xr[..., 1] * sin, xr[..., 1] * cos + xr[..., 0] * sin], axis=-1)
            return out.reshape(x.shape)
        B, T, _ = x.shape
        k = apply_rope(x @ Wk.T)
        v = x @ Wv.T
        q = jnp.einsum('btd,hkd->bhtk', x, Wq)
        q = apply_rope(q)
        scale = HS ** (-0.5)
        scores = jnp.einsum('bhtk,bsk->bhts', q, k) * scale
        causal = jnp.tril(jnp.ones((T, T), dtype=bool))
        scores = jnp.where(causal, scores, -jnp.inf)
        w = jax.nn.softmax(scores, axis=-1)
        out = jnp.einsum('bhts,bsk->bhtk', w, v)
        out = out.transpose(0, 2, 1, 3).reshape(B, T, NKV * HS)
        return out @ Wo.T

    def _L1_ffn_ref(x, router_w, w1, w2):
        import jax, jax.numpy as jnp
        import numpy as np
        N_EXPERTS = 8
        TOP_K = 2
        B, T, C = x.shape
        E = N_EXPERTS
        xf = x.reshape(-1, C)
        logits = jnp.einsum('nc,ec->ne', xf, router_w)
        probs = jax.nn.softmax(logits, axis=-1)
        top_w, top_i = jax.lax.top_k(probs, TOP_K)
        top_w = top_w / jnp.sum(top_w, axis=-1, keepdims=True)
        comb = jnp.einsum('nk,nke->ne', top_w, jax.nn.one_hot(top_i, E, dtype=xf.dtype))
        h = jax.nn.gelu(jnp.einsum('nc,ech->enh', xf, w1), approximate=False)
        y = jnp.einsum('enh,ehc->enc', h, w2)
        out = jnp.einsum('ne,enc->nc', comb, y)
        return out.reshape(B, T, C)
    x = x + _L0_xattn_ref(_layernorm(x, axis=-1), ctx_1024, ctx_1024, mask_Bx1xS2_if1, L0_xattn_Wq, L0_xattn_bq, L0_xattn_Wk, L0_xattn_bk, L0_xattn_Wv, L0_xattn_bv, L0_xattn_Wo, L0_xattn_bo)
    x = x + _L0_attn_ref(_layernorm(x, axis=-1), L0_attn_qkv_weights)
    x = x + _L0_ffn_ref(_layernorm(x, axis=-1), L0_ffn_q_w, L0_ffn_q_b, L0_ffn_k_w, L0_ffn_k_b, L0_ffn_v_w, L0_ffn_v_b, L0_ffn_o_w, L0_ffn_o_b, L0_ffn_router_w, L0_ffn_router_b, L0_ffn_w1, L0_ffn_b1, L0_ffn_w2, L0_ffn_b2)
    x = x + _L1_xattn_ref(_layernorm(x, axis=-1), ctx_1024, ctx_1024)
    x = x + _L1_attn_ref(_layernorm(x, axis=-1), L1_attn_Wq, L1_attn_Wk, L1_attn_Wv, L1_attn_Wo)
    x = x + _L1_ffn_ref(_layernorm(x, axis=-1), L1_ffn_router_w, L1_ffn_w1, L1_ffn_w2)
    return x

_drawn_inputs = setup_inputs


def setup_inputs(seed=0):
    import zlib

    import numpy as np

    out = dict(_drawn_inputs(seed))
    spreads = {'L0_ffn_q_b': (0.0, 0.8),
     'L0_ffn_k_b': (0.0, 2.0),
     'L0_ffn_v_b': (0.0, 0.8),
     'L0_ffn_o_b': (0.0, 0.388),
     'L0_ffn_router_b': (0.0, 0.454),
     'L0_ffn_b1': (0.0, 0.764),
     'L0_ffn_b2': (0.0, 2.0)}
    factors = {'L0_xattn_bq': 3.122,
     'L0_xattn_bk': 64.0,
     'L0_ffn_q_w': 8.0,
     'L0_ffn_k_w': 8.0,
     'L0_ffn_v_w': 8.0,
     'L0_ffn_o_w': 4.811,
     'L0_ffn_router_w': 5.048,
     'L0_ffn_w1': 8.0,
     'L0_ffn_w2': 8.0,
     'L1_attn_Wq': 4.001,
     'L1_attn_Wk': 4.12,
     'L1_ffn_router_w': 2.871,
     'L1_ffn_w1': 2.669}
    for name, (base, spread) in spreads.items():
        noise = np.random.default_rng([zlib.crc32(name.encode()), seed]).standard_normal(out[name].shape)
        drawn = base * np.exp(spread * noise) if base else spread * noise
        out[name] = jnp.asarray(drawn.astype(out[name].dtype))
    for name, factor in factors.items():
        out[name] = (out[name] * factor).astype(out[name].dtype)
    return out
```

```python
from contextlib import ExitStack

import numpy as np

import concourse.bass as bass
from concourse import mybir

F32 = mybir.dt.float32
I32 = mybir.dt.int32
U32 = mybir.dt.uint32
ALU = mybir.AluOpType
ACT = mybir.ActivationFunctionType
X = mybir.AxisListType.X
ds = bass.ds

P = 128
B, S, D = 32, 32, 512
SK = 257
K = D // P
T = B * S // P
NB = P // S
H, DH = 16, 32
G = 4
LAT, KPH = 256, 16
E = 8
ST = 2 * B * S // P + E - 1
F0, F1 = 1024, 2048
HS = 128
EPS = 1e-5
NEG = -1e9
BIG = 3e38

TABLES = {}
_at = 0
for _name, _n in (("ident", P), ("ones", P), ("before", P), ("eye32", 32 * 32), ("eye_tile", T * 32),
                  ("tril", S), ("untril", S), ("cos", HS), ("sin", HS), ("block_causal", P),
                  ("expert_id", E), ("step128", E), ("upto", E * E), ("tile_id", ST)):
    TABLES[_name] = (_at, _n)
    _at += _n
TABLE = _at


def tables():
    p = np.arange(P)
    t = {}
    t["ident"] = np.eye(P)
    t["ones"] = np.ones((P, P))
    t["before"] = p[:, None] < p[None, :]
    t["eye32"] = np.broadcast_to(np.eye(32).reshape(1, -1), (P, 1024))
    t["eye_tile"] = (np.arange(32)[None, None] == NB * np.arange(T)[None, :, None] + (p // S)[:, None, None])
    low = np.tril(np.ones((S, S)))[p % S]
    t["tril"] = low * float(DH) ** -0.5
    t["untril"] = NEG * (1 - low)
    theta = np.float32(10000.0) ** (np.float32(-2.0) * np.arange(0, HS, 2, dtype=np.float32) / np.float32(HS))
    angle = (p % S).astype(np.float32)[:, None] * theta[None]
    t["cos"] = np.repeat(np.cos(angle), 2, axis=1)
    t["sin"] = np.stack([-np.sin(angle), np.sin(angle)], -1)
    t["block_causal"] = np.where((p[:, None] // S == p[None] // S) & (p[None] <= p[:, None]), 0.0, -1e30)
    t["expert_id"] = np.broadcast_to(np.arange(E), (P, E))
    t["step128"] = np.broadcast_to(P * np.arange(E), (P, E))
    t["upto"] = np.broadcast_to(np.tril(np.ones((E, E))).reshape(1, -1), (P, E * E))
    t["tile_id"] = np.broadcast_to(np.arange(ST), (P, ST))
    return np.concatenate([np.asarray(t[n], np.float32).reshape(P, -1) for n in TABLES], axis=1)


def semaphores(nc, ctx, prefix):
    taken = []

    def give_back():
        nc.clear_and_free_semaphores(taken)
        nc.all_engine_barrier()
    ctx.callback(give_back)

    def sem(name):
        taken.append(nc.alloc_semaphore(prefix + name))
        return taken[-1]
    return sem


class Core:

    def __init__(self, nc, ctx, A):
        self.nc, self.A = nc, A
        self.sb = lambda name, shape, dt=F32: ctx.enter_context(nc.sbuf_tensor(name, shape, dt))
        self.x = self.sb("x", [P, T, D])
        self.rows = self.sb("rows", [P, T, D])
        self.probs = self.sb("probs", [P, T, E])
        self.table = self.sb("table", [P, TABLE])
        self.come = [ctx.enter_context(nc.semaphore(f"come{t}")) for t in range(T)]
        self.slot = self.sb("slot", [P, 2, T], U32)
        self.gate = self.sb("gate", [P, T, 2])
        self.expert_of = self.sb("expert_of", [1, ST], I32)
        self.tiles_before = self.sb("tiles_before", [1, E], I32)
        dram = lambda name, rows: nc.dram_tensor(name, [rows, D], F32, kind="Internal").ap()
        self.sent = [dram(f"sent{n}", ST * P) for n in range(2)]
        self.back = [dram(f"back{n}", ST * P) for n in range(2)]

    def tab(self, name):
        a, n = TABLES[name]
        return self.table[:, a:a + n]


def setup_phase(nc, core):
    with ExitStack() as ctx:
        loaded = ctx.enter_context(nc.semaphore("setup_loaded"))
        cleared = ctx.enter_context(nc.semaphore("setup_cleared"))
        zero_made = ctx.enter_context(nc.semaphore("zero_made"))
        zero = ctx.enter_context(nc.sbuf_tensor("zero", [P, D], F32))
        block = ctx.enter_context(nc.Block())

        @block.vector
        def _(dve):
            dve.memset(zero[:], 0.0).then_inc(zero_made, 1)

        @block.sync
        def _(sp):
            sp.dma_start(core.table[:], core.A["tables"]).then_inc(loaded, 16)
            sp.dma_start(core.x[:], core.A["x"].rearrange("(t p) d -> p t d", p=P)).then_inc(loaded, 16)
            sp.wait_ge(zero_made, 1)
            for sent in core.sent:
                sp.dma_start(sent.rearrange("(t p) d -> p t d", p=P),
                             zero[:].unsqueeze(1).to_broadcast([P, ST, D])).then_inc(cleared, 16)
            sp.wait_ge(loaded, 32)
            sp.wait_ge(cleared, 32)


def phase_cross0(nc, core):
    A = core.A
    x, tab = core.x, core.tab
    with ExitStack() as ctx:
        sb = lambda name, shape, dt=F32: ctx.enter_context(nc.sbuf_tensor("c0_" + name, shape, dt))
        sem = semaphores(nc, ctx, "c0_")
        pb = lambda name, banks: ctx.enter_context(nc.psum_tensor("c0_" + name, [P, banks, 512], F32))

        wq, wk, wv, wo = (sb(n, [P, K, D]) for n in ("wq", "wk", "wv", "wo"))
        bq, bk = sb("bq", [P, G]), sb("bk", [P, G])
        bv, bo = sb("bv", [P, D]), sb("bo", [P, D])
        ctxT = sb("ctxT", [P, NB, K, SK])
        lastT = sb("lastT", [P, K, NB, B])
        maskt = sb("maskt", [P, NB, SK], I32)
        keep = sb("keep", [P, NB, SK])
        bound = sb("bound", [P, NB, SK])
        stats = sb("stats", [P, 6])
        mv = sb("mv", [P, 2])
        mhalf = sb("mhalf", [P, 1])
        veps = sb("veps", [P, 1])
        rstd = sb("rstd", [P, 1])
        xn = sb("xn", [P, D])
        xT = sb("xT", [P, K, P])
        qbd = sb("qbd", [P, NB, G, NB, S])
        kT = sb("kT", [P, 2, G, SK])
        v = sb("v", [P, 2, 2, D])
        vlast = sb("vlast", [P, G, P])
        sm = sb("sm", [P, 2, G, SK])
        nmax = sb("nmax", [P, 2, G])
        rsum = sb("rsum", [P, 2, G])
        rinv = sb("rinv", [P, 2, G])
        plast = sb("plast", [P, G, 32])
        pT = sb("pT", [P, 2 * G, P])
        plastT = sb("plastT", [P, P])
        o = sb("o", [P, D])
        oT = sb("oT", [P, K, P])

        KV = pb("KV", 3)
        SC = pb("SC", 2)
        TB = pb("TB", 2)
        O = pb("O", 1)

        weights_in = sem("weights_in")
        ctx_in = [sem(f"ctx_in{b}") for b in range(NB)]
        mask_in = sem("mask_in")
        keep_made = sem("keep_made")
        bound_made = sem("bound_made")
        cleared = sem("cleared")
        mhalf_set = sem("mhalf_set")
        var_ready = sem("var_ready")
        rstd_ready = sem("rstd_ready")
        xn_ready = sem("xn_ready")
        t_ready = sem("t_ready")
        t_free = [sem("t_free0"), sem("t_free1")]
        kv_ready = sem("kv_ready")
        kT_ready = sem("kT_ready")
        v_ready = sem("v_ready")
        vlast_done = sem("vlast_done")
        vlast_ready = sem("vlast_ready")
        scores_ready = sem("scores_ready")
        masked = sem("masked")
        max_ready = sem("max_ready")
        exp_done = sem("exp_done")
        plast_ready = sem("plast_ready")
        pv_ready = sem("pv_ready")
        o_ready = sem("o_ready")

        PT_USE = (0, 3, 6, 11)
        XT_USE, Q_USE, OT_USE, OUT_USE, USES = 9, 10, 14, 15, 16
        FIRST_USES = 2

        def use(n, last):
            return n - 2 if last and n > Q_USE else n

        block = ctx.enter_context(nc.Block())

        @block.sync
        def _(sp):
            sp.dma_start(wv[:], A["wv"].rearrange("(k p) n -> p k n", p=P)).then_inc(weights_in, 16)
            sp.dma_start(wq[:], A["wq"].rearrange("(k p) n -> p k n", p=P)).then_inc(weights_in, 16)
            sp.dma_start(wk[:], A["wk"].rearrange("(k p) n -> p k n", p=P)).then_inc(weights_in, 16)
            for r in range(NB):
                sp.dma_start(lastT[:, :, r, :], A["ctx_lastT"]).then_inc(weights_in, 16)
            for t, a in ((bq, "bqT"), (bk, "bkT")):
                sp.dma_start(t[:], A[a]).then_inc(weights_in, 16)
            for t, a in ((bv, "bv"), (bo, "bo")):
                sp.dma_start(t[:], A[a].partition_broadcast(P)).then_inc(weights_in, 16)
            sp.dma_start(wo[:], A["wo"].rearrange("(k p) n -> p k n", p=P)).then_inc(weights_in, 16)

            def loads(j, first):
                if not first:
                    sp.wait_ge(bound_made, j)
                sp.dma_start(maskt[:], A["mask"][ds(j, 1), :].partition_broadcast(P)
                             .rearrange("p a (b k) -> p (a b) k", b=NB)).then_inc(mask_in, 16)
                for b in range(NB):
                    if not first:
                        sp.wait_ge(kv_ready, 24 * j - 24 + 6 * b + 6)
                    sp.dma_start(ctxT[:, b], A["ctxT"][ds(j * NB + b, 1), :, :]
                                 .rearrange("a p n -> p (a n)").rearrange("p (k n) -> p k n", k=K)).then_inc(ctx_in[b], 16)
            loads(0, True)
            with sp.Fori(1, T) as j:
                loads(j, False)

        WEIGHTS = 16 * 12

        @block.gpsimd
        def _(pool):
            pool.memset(mhalf[:], -0.5).then_inc(mhalf_set, 1)
            pool.wait_ge(mhalf_set, 1)

            def rsqrt(j):
                pool.drain()
                pool.wait_ge(var_ready, j + 1)
                pool.tensor_tensor(rstd[:], veps[:], mhalf[:], ALU.pow).then_inc(rstd_ready, 1)
            with pool.Fori(0, T) as j:
                rsqrt(j)

        @block.vector
        def _(dve):
            dve.wait_ge(weights_in, WEIGHTS)
            def norm(j):
                dve.drain()
                dve.bn_stats(stats[:], x[:, ds(j, 1), :].rearrange("p a d -> p (a d)"))
                dve.drain()
                dve.bn_aggr(mv[:], stats[:])
                dve.drain()
                dve.tensor_scalar(veps[:], mv[:, 1:2], EPS, None, ALU.add).then_inc(var_ready, 1)

            def normed(j):
                dve.drain()
                dve.wait_ge(rstd_ready, j + 1)
                dve.tensor_scalar(xn[:], x[:, ds(j, 1), :].rearrange("p a d -> p (a d)"), mv[:, 0:1],
                                  rstd[:, 0:1], ALU.subtract, ALU.mult).then_inc(xn_ready, 1)

            def spread_q(u):
                dve.drain()
                dve.wait_ge(t_ready, u)
                for h in range(NB):
                    rows = slice(S * h, S * h + S)
                    last = dve.tensor_tensor(
                        qbd[rows, :, :, h, :].rearrange("p b g q -> p g b q"),
                        TB[rows, 0, :].rearrange("p (g b q) -> p g b q", g=G, b=NB),
                        bq[rows, :].unsqueeze(2).unsqueeze(3).to_broadcast([S, G, NB, S]), ALU.add)
                last.then_inc(t_free[0], 1)

            def copy_v(i, p, kt):
                dve.wait_ge(kv_ready, 6 * i + G + kt + 1)
                dve.tensor_tensor(v[:, p, kt, :], KV[:, 1 + kt, :], bv[:], ALU.add).then_inc(v_ready, 1)

            dve.sem_inc(masked, 1)
            dve.sem_inc(o_ready, 1)
            dve.memset(qbd[:], 0.0)
            dve.memset(vlast[:], 0.0).then_inc(cleared, 1)
            norm(0)
            normed(0)
            dve.wait_ge(vlast_done, 1)
            for g in range(G):
                rows = slice(S * g, S * g + S)
                last = dve.tensor_tensor(vlast[rows, g, :], O[rows, 0, P * g:P * g + P], bv[rows, P * g:P * g + P], ALU.add)
            last.then_inc(vlast_ready, 1)
            spread_q(2)
            copy_v(0, 0, 0)
            copy_v(0, 0, 1)

            def tile(j, last):
                dve.drain()
                dve.wait_ge(mask_in, 16 * j + 16)
                dve.tensor_scalar(keep[:], maskt[:], 0, BIG, ALU.not_equal, ALU.mult).then_inc(keep_made, 1)
                dve.drain()
                dve.tensor_scalar(bound[:], keep[:], NEG, None, ALU.add).then_inc(bound_made, 1)
                for b in range(NB):
                    i = NB * j + b
                    for hf in range(2):
                        groups = slice(2 * hf, 2 * hf + 2)
                        dve.drain()
                        dve.wait_ge(scores_ready, 2 * i + hf + 1)
                        dve.scalar_tensor_tensor(sm[:, b % 2, groups, :], SC[:, :, 0:SK], float(DH) ** -0.5,
                                                 bound[:, b:b + 1, :].to_broadcast([P, 2, SK]), ALU.mult, ALU.min)\
                           .then_inc(masked, 1)
                        dve.drain()
                        dve.tensor_reduce(nmax[:, b % 2, groups], sm[:, b % 2, groups, :], X, ALU.max, negate=True)\
                           .then_inc(max_ready, 1)
                    if b == NB - 1 and not last:
                        spread_q(USES * j + FIRST_USES + Q_USE + 1)
                    dve.drain()
                    dve.wait_ge(exp_done, 2 * i + 2)
                    dve.tensor_tensor(plast[:], tab("eye32").rearrange("p (i n) -> p i n", n=32)[:, ds(i, 1), :].to_broadcast([P, G, 32]),
                                      sm[:, b % 2, :, SK - 1:SK].to_broadcast([P, G, 32]), ALU.mult).then_inc(plast_ready, 1)
                    dve.reciprocal(rinv[:, b % 2, :], rsum[:, b % 2, :])
                    if not (last and b == NB - 1):
                        copy_v(i + 1, (b + 1) % 2, 0)
                        copy_v(i + 1, (b + 1) % 2, 1)
                    if b == 0 and not last:
                        norm(j + 1)
                    if b == 1 and not last:
                        normed(j + 1)
                    dve.drain()
                    dve.wait_ge(pv_ready, i + 1)
                    if b == 0:
                        dve.wait_ge(t_ready, USES * j + 1)
                    for h in range(NB):
                        rows = slice(S * h, S * h + S)
                        op = dve.tensor_tensor(o[S * b:S * b + S, :].rearrange("p (g c) -> p g c", g=G)[:, :, S * h:S * h + S],
                                               O[rows, 0, :].rearrange("p (g c) -> p g c", g=G)[:, :, S * h:S * h + S],
                                               rinv[rows, b % 2, :].unsqueeze(2).to_broadcast([S, G, S]), ALU.mult)
                    op.then_inc(o_ready, 1)
                dve.drain()
                dve.wait_ge(t_ready, USES * j + FIRST_USES + use(OUT_USE, last) + 1)
                xt = x[:, ds(j, 1), :].rearrange("p a d -> p (a d)")
                dve.tensor_tensor(xt, xt, TB[:, 1, :], ALU.add).then_inc(t_free[1], 1)
                dve.drain()
                dve.tensor_tensor(xt, xt, bo[:], ALU.add)

            with dve.Fori(0, T - 1) as j:
                tile(j, False)
            tile(T - 1, True)

        @block.scalar
        def _(act):
            act.wait_ge(weights_in, WEIGHTS)
            def copy_k(i, p, g):
                act.wait_ge(kv_ready, 6 * i + g + 1)
                act.activation(kT[:, p, g, :], KV[:, g % 3, 0:SK], ACT.Identity, bias=bk[:, g:g + 1]).then_inc(kT_ready, 1)

            def copy_t(out, u, bank):
                act.wait_ge(t_ready, u)
                act.activation(out, TB[:, bank, 0:out.free_size()], ACT.Copy).then_inc(t_free[bank], 1)

            copy_t(xT[:].rearrange("p k n -> p (k n)"), 1, 1)
            for g in range(G):
                copy_k(0, 0, g)

            def tile(j, last):
                for b in range(NB):
                    i = NB * j + b
                    for hf in range(2):
                        if not (last and b == NB - 1):
                            copy_k(i + 1, (b + 1) % 2, 2 * hf)
                            copy_k(i + 1, (b + 1) % 2, 2 * hf + 1)
                        act.wait_ge(max_ready, 2 * i + hf + 1)
                        for g in range(2 * hf, 2 * hf + 2):
                            op = act.activation(sm[:, b % 2, g, :], sm[:, b % 2, g, :], ACT.Exp,
                                                bias=nmax[:, b % 2, g:g + 1], accum_out=rsum[:, b % 2, g:g + 1])
                        op.then_inc(exp_done, 1)
                    n = use(PT_USE[b], last)
                    for c in range(2):
                        copy_t(pT[:, 4 * c:4 * c + 4, :].rearrange("p a n -> p (a n)"),
                               USES * j + FIRST_USES + n + c + 1, (n + c) % 2)
                    copy_t(plastT[:], USES * j + FIRST_USES + n + 3, n % 2)
                    if b == 2 and not last:
                        copy_t(xT[:].rearrange("p k n -> p (k n)"), USES * j + FIRST_USES + XT_USE + 1, 1)
                copy_t(oT[:].rearrange("p k n -> p (k n)"), USES * j + FIRST_USES + use(OT_USE, last) + 1, 0)

            with act.Fori(0, T - 1) as j:
                tile(j, False)
            tile(T - 1, True)

        @block.tensor
        def _(pe):
            pe.wait_ge(weights_in, WEIGHTS)
            def free(bank, v):
                pe.wait_ge(t_free[bank], v)

            def make_xT(j):
                pe.wait_ge(xn_ready, j + 1)
                for k in range(K):
                    op = pe.transpose(TB[:, 1, P * k:P * k + P], xn[:, P * k:P * k + P], tab("ident"))
                op.then_inc(t_ready, 1)

            def make_q(v):
                free(1, v)
                for g in range(G):
                    for k in range(K):
                        op = pe.matmul(TB[:, 0, P * g:P * g + P], wq[:, k, P * g:P * g + P], xT[:, k, :],
                                       start=(k == 0), stop=(k == K - 1))
                op.then_inc(t_ready, 1)

            def make_k(i, j, b, g, first=False):
                if g == 0:
                    pe.wait_ge(ctx_in[b], 16 * j + 16)
                    if not first:
                        pe.wait_ge(kT_ready, 4 * i)
                if g == 1 and not first:
                    pe.wait_ge(v_ready, 2 * i - 1)
                if g == 2 and not first:
                    pe.wait_ge(v_ready, 2 * i)
                if g == 3:
                    pe.wait_ge(kT_ready, 4 * i + 1)
                for k in range(K):
                    op = pe.matmul(KV[:, g % 3, 0:SK], wk[:, k, P * g:P * g + P], ctxT[:, b, k, :],
                                   start=(k == 0), stop=(k == K - 1))
                op.then_inc(kv_ready, 1)

            def make_v(i, b, kt):
                pe.wait_ge(kT_ready, 4 * i + 2 + kt)
                for k in range(K):
                    op = pe.matmul(KV[:, 1 + kt, :], ctxT[:, b, k, P * kt:P * kt + P], wv[:, k, :],
                                   start=(k == 0), stop=(k == K - 1))
                op.then_inc(kv_ready, 1)

            def scores(i, b, hf):
                pe.wait_ge(kT_ready, 4 * i + 2 * hf + 2)
                pe.wait_ge(masked, 2 * i + hf + 1)
                for g in range(2 * hf, 2 * hf + 2):
                    op = pe.matmul(SC[:, g % 2, 0:SK], qbd[:, b, g].rearrange("p h q -> p (h q)"), kT[:, b % 2, g, :],
                                   start=True, stop=True)
                op.then_inc(scores_ready, 1)

            for k in range(K):
                op = pe.matmul(O[:, 0, :], lastT[:, k].rearrange("p r b -> p (r b)"), wv[:, k, :], start=(k == 0), stop=(k == K - 1))
            op.then_inc(vlast_done, 1)
            make_xT(0)
            make_q(1)
            pe.wait_ge(t_free[0], 1)
            for g in range(G):
                make_k(0, 0, 0, g, first=True)
            make_v(0, 0, 0)
            make_v(0, 0, 1)

            def tile(j, last):
                base = USES // 2 * j + 1
                for b in range(NB):
                    i = NB * j + b
                    nb = (b + 1) % NB
                    more = not (last and b == NB - 1)
                    nj = j + (b + 1) // NB
                    if b == NB - 1 and not last:
                        free(0, base + Q_USE // 2)
                        make_q(base + XT_USE // 2 + 1)
                    scores(i, b, 0)
                    if more:
                        make_k(i + 1, nj, nb, 0)
                        make_k(i + 1, nj, nb, 1)
                    scores(i, b, 1)
                    if more:
                        make_k(i + 1, nj, nb, 2)
                        make_k(i + 1, nj, nb, 3)
                        make_v(i + 1, nb, 0)
                        make_v(i + 1, nb, 1)
                    n = use(PT_USE[b], last)
                    pe.wait_ge(exp_done, 2 * i + 2)
                    for c in range(2):
                        free((n + c) % 2, base + (n + c) // 2)
                        for m in range(4):
                            g, kt = 2 * c + m // 2, m % 2
                            op = pe.transpose(TB[:, (n + c) % 2, P * m:P * m + P], sm[:, b % 2, g, P * kt:P * kt + P], tab("ident"))
                        op.then_inc(t_ready, 1)
                    pe.wait_ge(plast_ready, i + 1)
                    free(n % 2, base + (n + 2) // 2)
                    pe.transpose(TB[:, n % 2, 0:P], plast[:].rearrange("p g n -> p (g n)"), tab("ident")).then_inc(t_ready, 1)
                    pe.wait_ge(v_ready, 2 * i + 2)
                    pe.wait_ge(vlast_ready, 1)
                    pe.wait_ge(o_ready, i + 1)
                    free(n % 2, base + (n + 2) // 2 + 1)
                    free((n + 1) % 2, base + (n + 1) // 2 + 1)
                    for g in range(G):
                        for kt in range(2):
                            pe.matmul(O[:, 0, P * g:P * g + P], pT[:, 2 * g + kt, :], v[:, b % 2, kt, P * g:P * g + P],
                                      start=(g == 0 and kt == 0), stop=False, skip_group_check=True)
                    op = pe.matmul(O[:, 0, :], plastT[:], vlast[:].rearrange("p g n -> p (g n)"),
                                   start=False, stop=True, skip_group_check=True)
                    op.then_inc(pv_ready, 1)
                    if b == 2 and not last:
                        free(1, base + XT_USE // 2)
                        make_xT(j + 1)
                n = use(OT_USE, last)
                pe.wait_ge(o_ready, NB * j + NB + 1)
                free(0, base + n // 2)
                for k in range(K):
                    op = pe.transpose(TB[:, 0, P * k:P * k + P], o[:, P * k:P * k + P], tab("ident"))
                op.then_inc(t_ready, 1)
                free(1, base + n // 2)
                free(0, base + n // 2 + 1)
                for k in range(K):
                    op = pe.matmul(TB[:, 1, :], oT[:, k, :], wo[:, k, :], start=(k == 0), stop=(k == K - 1))
                op.then_inc(t_ready, 1)

            with pe.Fori(0, T - 1) as j:
                tile(j, False)
            tile(T - 1, True)


def phase_self0(nc, core):
    A, x, tab = core.A, core.x, core.tab
    with ExitStack() as ctx:
        sb = lambda name, shape, dt=F32: ctx.enter_context(nc.sbuf_tensor("s0_" + name, shape, dt))
        sem = semaphores(nc, ctx, "s0_")
        sems = lambda name: [sem(f"{name}{s}") for s in range(2)]
        LC = 3 * LAT

        wqkv = sb("wqkv", [P, K, 3 * D])
        latw = sb("latw", [P, K, LC])
        latb = sb("latb", [P, LC])
        latow = sb("latow", [P, 2, D])
        latob = sb("latob", [P, D])
        rw = sb("rw", [P, K, E])
        rb = sb("rb", [P, E])
        two = lambda name, shape: [sb(f"{name}{s}", shape) for s in range(2)]
        stats, mv, veps, rstd = two("stats", [P, 6]), two("mv", [P, 2]), two("veps", [P, 1]), two("rstd", [P, 1])
        mhalf = sb("mhalf", [P, 1])
        xn, xT = two("xn", [P, D]), two("xT", [P, K, P])
        qT, kT, kn, vn = two("qT", [P, H, 32]), two("kT", [P, LAT]), two("kn", [P, D]), two("vn", [P, D])
        qpad = two("qpad", [P, H, 32])
        sm, pT = two("sm", [P, H, S]), two("pT", [P, H, S])
        nm, rs, ri = two("nm", [P, H]), two("rs", [P, H]), two("ri", [P, H])
        ao, aoT = two("ao", [P, LAT]), two("aoT", [P, 2, P])
        lg, lmax, lsum, linv = two("lg", [P, E]), two("lmax", [P, 1]), two("lsum", [P, 1]), two("linv", [P, 1])

        R = [[ctx.enter_context(nc.psum_tensor(f"s0_R{s}{k}", [P, 512], F32)) for k in range(2)] for s in range(2)]
        AT = ctx.enter_context(nc.psum_tensor("s0_AT", [P, NB, 512], F32))

        weights_in = sem("weights_in")
        WEIGHTS = 16 * 7
        mhalf_set, qpad_zero = sem("mhalf_set"), sem("qpad_zero")
        var_ready, rstd_ready, xn_ready = sems("var_ready"), sems("rstd_ready"), sems("xn_ready")
        r_ready = sems("r_ready")
        r_free = [sems(f"r_free{s}_") for s in range(2)]
        qT_ready, kv_ready = sems("qT_ready"), sems("kv_ready")
        heads_begun = sem("heads_begun")
        at_ready, at_free = sem("at_ready"), sem("at_free")
        raw_ready = sems("raw_ready")
        shifted, exp_done, pT_ready = sems("shifted"), sems("exp_done"), sems("pT_ready")
        ao_ready = sems("ao_ready")
        rows_kept = sems("rows_kept")
        lshift, lexp = sems("lshift"), sems("lexp")

        XT0, UQ, UK, UV, XT1, ULQK, ULV, UAO, UO, XT2, ULOG = range(11)
        USES, READS = 11, 5
        SCORE0, PV0, SCORE1, PV1 = range(4)

        block = ctx.enter_context(nc.Block())

        def ready(eng, s, it, n):
            eng.wait_ge(r_ready[s], USES * it + n + 1)

        def at_use(it, n, s):
            return 8 * it + 2 * n + s

        @block.sync
        def _(sp):
            for t, a in ((wqkv, "wqkv"), (latw, "lat_w"), (latow, "lat_ow"), (rw, "rw0")):
                sp.dma_start(t[:], A[a].rearrange("(k p) n -> p k n", p=P)).then_inc(weights_in, 16)
            for t, a in ((latb, "lat_b"), (latob, "lat_ob"), (rb, "rb0")):
                sp.dma_start(t[:], A[a].partition_broadcast(P)).then_inc(weights_in, 16)

        @block.gpsimd
        def _(pool):
            pool.memset(mhalf[:], -0.5).then_inc(mhalf_set, 1)
            pool.wait_ge(mhalf_set, 1)

            def rsqrt(n):
                for s in range(2):
                    pool.drain()
                    pool.wait_ge(var_ready[s], n)
                    pool.tensor_tensor(rstd[s][:], veps[s][:], mhalf[:], ALU.pow).then_inc(rstd_ready[s], 1)
            for kept in rows_kept:
                pool.sem_inc(kept, 1)
            with pool.Fori(0, T // 2) as it:
                rsqrt(2 * it + 1)
                rsqrt(2 * it + 2)
                for s in range(2):
                    pool.wait_ge(xn_ready[s], 3 * it + 3)
                    pool.wait_ge(mhalf_set, 1)
                    pool.tensor_copy(core.rows[:, ds(2 * it + s, 1), :].rearrange("p a d -> p (a d)"), xn[s][:])\
                        .then_inc(rows_kept[s], 1)

        @block.vector
        def _(dve):
            dve.wait_ge(weights_in, WEIGHTS)
            def tile(it, s):
                return x[:, ds(2 * it + s, 1), :].rearrange("p a d -> p (a d)")

            def norm(it, k):
                for s in range(2):
                    dve.drain()
                    dve.bn_stats(stats[s][:], tile(it, s))
                for s in range(2):
                    dve.drain()
                    dve.bn_aggr(mv[s][:], stats[s][:])
                for s in range(2):
                    dve.drain()
                    dve.tensor_scalar(veps[s][:], mv[s][:, 1:2], EPS, None, ALU.add).then_inc(var_ready[s], 1)
                for s in range(2):
                    dve.wait_ge(rstd_ready[s], 2 * it + k + 1)
                    if k == 0:
                        dve.wait_ge(rows_kept[s], it + 1)
                    if k > 0:
                        ready(dve, s, it, XT0)
                    dve.tensor_scalar(xn[s][:], tile(it, s), mv[s][:, 0:1], rstd[s][:, 0:1],
                                      ALU.subtract, ALU.mult).then_inc(xn_ready[s], 1)

            def softmax(it, k):
                for s in range(2):
                    if k == 1:
                        dve.wait_ge(raw_ready[s], it + 1)
                    dve.tensor_reduce(nm[s][:], sm[s][:], X, ALU.max, negate=True)
                for s in range(2):
                    dve.drain()
                    dve.tensor_tensor(sm[s][:], sm[s][:], nm[s][:].unsqueeze(2).to_broadcast([P, H, S]), ALU.add)\
                       .then_inc(shifted[s], 1)
                for s in range(2):
                    dve.drain()
                    dve.wait_ge(exp_done[s], 2 * it + k + 1)
                    dve.tensor_reduce(rs[s][:], sm[s][:], X, ALU.add)
                    dve.drain()
                    dve.reciprocal(ri[s][:], rs[s][:])
                    dve.drain()
                    dve.tensor_tensor(sm[s][:], sm[s][:], ri[s][:].unsqueeze(2).to_broadcast([P, H, S]), ALU.mult)
                    dve.drain()
                    dve.transpose(pT[s][:].rearrange("p h q -> p (h q)"), sm[s][:].rearrange("p h q -> p (h q)")).then_inc(pT_ready[s], 1)

            for s in range(2):
                last = dve.memset(qpad[s][:], 0.0)
            last.then_inc(qpad_zero, 1)
            for free in r_free[0] + r_free[1] + [at_free]:
                dve.sem_inc(free, 1)
            with dve.Fori(0, T // 2) as it:
                norm(it, 0)
                for s in range(2):
                    dve.drain()
                    ready(dve, s, it, UQ)
                    dve.transpose(qT[s][:].rearrange("p h q -> p (h q)"), R[s][UQ % 2][:]).then_inc(r_free[s][UQ % 2], 1)
                for s in range(2):
                    dve.wait_ge(at_ready, at_use(it, SCORE0, s) + 1)
                    for b in range(NB):
                        rows = slice(S * b, S * b + S)
                        op = dve.tensor_tensor(sm[s][rows], AT[rows, b, :].rearrange("p (h k) -> p h k", h=H),
                                               tab("tril")[rows].unsqueeze(1).to_broadcast([S, H, S]), ALU.mult)
                    op.then_inc(at_free, 1)
                for s in range(2):
                    dve.drain()
                    dve.tensor_tensor(sm[s][:], sm[s][:], tab("untril").unsqueeze(1).to_broadcast([P, H, S]), ALU.add)
                dve.drain()
                softmax(it, 0)
                for s in range(2):
                    dve.drain()
                    dve.wait_ge(at_ready, at_use(it, PV0, s) + 1)
                    for b in range(NB):
                        rows = slice(S * b, S * b + S)
                        xt = x[rows, ds(2 * it + s, 1), :].rearrange("p a d -> p (a d)")
                        op = dve.tensor_tensor(xt, xt, AT[rows, b, :], ALU.add)
                    op.then_inc(at_free, 1)
                norm(it, 1)
                for s in range(2):
                    dve.drain()
                    dve.tensor_tensor(tile(it, s), tile(it, s), xn[s][:], ALU.add)
                for s in range(2):
                    ready(dve, s, it, ULQK)
                    q = R[s][ULQK % 2][:, 0:LAT].rearrange("p (h e k) -> p h e k", e=2, k=KPH)
                    bias = latb[:, 0:LAT].rearrange("p (h e k) -> p h e k", e=2, k=KPH)
                    pad = qpad[s][:].rearrange("p (h e) k -> p h e k", e=2)
                    for e in range(2):
                        dve.tensor_tensor(pad[:, :, e, KPH * e:KPH * e + KPH], q[:, :, e, :], bias[:, :, e, :], ALU.add)
                    dve.tensor_tensor(kn[s][:, 0:LAT], R[s][ULQK % 2][:, LAT:2 * LAT], latb[:, LAT:2 * LAT], ALU.add)\
                       .then_inc(r_free[s][ULQK % 2], 1)
                    dve.drain()
                    dve.transpose(qT[s][:].rearrange("p h q -> p (h q)"), qpad[s][:].rearrange("p h q -> p (h q)"))
                    dve.transpose(kT[s][:], kn[s][:, 0:LAT]).then_inc(qT_ready[s], 1)
                    ready(dve, s, it, ULV)
                    dve.tensor_tensor(vn[s][:, 0:LAT], R[s][ULV % 2][:, 0:LAT], latb[:, 2 * LAT:LC], ALU.add)\
                       .then_inc(r_free[s][ULV % 2], 1)
                softmax(it, 1)
                for s in range(2):
                    dve.drain()
                    dve.wait_ge(at_ready, at_use(it, PV1, s) + 1)
                    for b in range(NB):
                        rows = slice(S * b, S * b + S)
                        op = dve.tensor_copy(ao[s][rows], AT[rows, b, 0:LAT])
                    op.then_inc(at_free, 1)
                    dve.drain()
                    dve.sem_inc(ao_ready[s], 1)
                for s in range(2):
                    ready(dve, s, it, UO)
                    dve.tensor_tensor(xn[s][:], R[s][UO % 2][:], latob[:], ALU.add).then_inc(xn_ready[s], 1)
                for s in range(2):
                    dve.drain()
                    ready(dve, s, it, ULOG)
                    dve.tensor_tensor(lg[s][:], R[s][ULOG % 2][:, 0:E], rb[:], ALU.add).then_inc(r_free[s][ULOG % 2], 1)
                    dve.drain()
                    dve.tensor_reduce(lmax[s][:], lg[s][:], X, ALU.max, negate=True).then_inc(lshift[s], 1)
                for s in range(2):
                    dve.drain()
                    dve.wait_ge(lexp[s], it + 1)
                    dve.reciprocal(linv[s][:], lsum[s][:])
                    dve.drain()
                    dve.tensor_scalar(core.probs[:, ds(2 * it + s, 1), :].rearrange("p a e -> p (a e)"), lg[s][:],
                                      linv[s][:, 0:1], None, ALU.mult)

        @block.scalar
        def _(act):
            act.wait_ge(weights_in, WEIGHTS)
            def copy(s, it, n, out, w, free=True, done=None):
                ready(act, s, it, n)
                act.activation(out, R[s][n % 2][:, 0:w], ACT.Copy).then_inc(r_free[s][n % 2], 1)

            def exps(it, k):
                for s in range(2):
                    act.wait_ge(shifted[s], 2 * it + k + 1)
                    act.activation(sm[s][:], sm[s][:], ACT.Exp).then_inc(exp_done[s], 1)

            with act.Fori(0, T // 2) as it:
                for s in range(2):
                    copy(s, it, XT0, xT[s][:].rearrange("p k n -> p (k n)"), D)
                for s in range(2):
                    copy(s, it, UK, kn[s][:], D)
                    copy(s, it, UV, vn[s][:], D)
                exps(it, 0)
                for s in range(2):
                    copy(s, it, XT1, xT[s][:].rearrange("p k n -> p (k n)"), D)
                for s in range(2):
                    act.wait_ge(at_ready, at_use(it, SCORE1, s) + 1)
                    for b in range(NB):
                        rows = slice(S * b, S * b + S)
                        op = act.activation(sm[s][rows], AT[rows, b, :].rearrange("p (h k) -> p h k", h=H), ACT.Copy,
                                            scale=float(KPH) ** -0.5)
                    op.then_inc(at_free, 1)
                    act.drain()
                    act.sem_inc(raw_ready[s], 1)
                exps(it, 1)
                for s in range(2):
                    copy(s, it, UAO, aoT[s][:].rearrange("p k n -> p (k n)"), LAT)
                for s in range(2):
                    copy(s, it, XT2, xT[s][:].rearrange("p k n -> p (k n)"), D)
                for s in range(2):
                    act.wait_ge(lshift[s], it + 1)
                    act.activation(lg[s][:], lg[s][:], ACT.Exp, bias=lmax[s][:, 0:1], accum_out=lsum[s][:]).then_inc(lexp[s], 1)

        @block.tensor
        def _(pe):
            pe.wait_ge(weights_in, WEIGHTS)
            def free(s, it, n):
                pe.wait_ge(r_free[s][n % 2], READS * it + n // 2 - (n == ULOG) + 1)

            def read(s, it, n):
                pe.wait_ge(r_free[s][n % 2], READS * it + n // 2 - (n == ULOG) + 2)

            def transposes(s, it, n, src, count):
                free(s, it, n)
                for k in range(count):
                    op = pe.transpose(R[s][n % 2][:, P * k:P * k + P], src[:, P * k:P * k + P], tab("ident"))
                op.then_inc(r_ready[s], 1)

            def product(s, it, n, lhs, rhs, w):
                free(s, it, n)
                for k in range(len(lhs)):
                    op = pe.matmul(R[s][n % 2][:, 0:w], lhs[k], rhs[k], start=(k == 0), stop=(k == len(lhs) - 1))
                op.then_inc(r_ready[s], 1)

            def heads(use, lhs, rhs, w):
                pe.wait_ge(at_free, use + 1)
                pe.sem_inc(heads_begun, 1)
                for h in range(H):
                    for b in range(NB):
                        rows = slice(S * b, S * b + S)
                        op = pe.matmul(AT[rows, b, w * h:w * h + w], lhs(rows, h), rhs(rows, h), start=(h == 0), stop=(h == H - 1),
                                       skip_group_check=True)
                op.then_inc(at_ready, 1)

            with pe.Fori(0, T // 2) as it:
                for s in range(2):
                    pe.wait_ge(xn_ready[s], 3 * it + 1)
                    transposes(s, it, XT0, xn[s], K)
                for s in range(2):
                    read(s, it, XT0)
                    for n, c in ((UQ, 0), (UK, 1), (UV, 2)):
                        product(s, it, n, [xT[s][:, k, :] for k in range(K)],
                                [wqkv[:, k, D * c:D * c + D] for k in range(K)], D)
                for s in range(2):
                    read(s, it, UQ)
                    read(s, it, UK)
                    heads(at_use(it, SCORE0, s), lambda r, h: qT[s][r, h, :], lambda r, h: kn[s][r, 32 * h:32 * h + 32], 32)
                for s in range(2):
                    read(s, it, UV)
                    pe.wait_ge(pT_ready[s], 2 * it + 1)
                    heads(at_use(it, PV0, s), lambda r, h: pT[s][r, h, :], lambda r, h: vn[s][r, 32 * h:32 * h + 32], 32)
                for s in range(2):
                    pe.wait_ge(xn_ready[s], 3 * it + 2)
                    transposes(s, it, XT1, xn[s], K)
                for s in range(2):
                    read(s, it, XT1)
                    for n, c, w in ((ULQK, 0, 2 * LAT), (ULV, 2 * LAT, LAT)):
                        product(s, it, n, [xT[s][:, k, :] for k in range(K)],
                                [latw[:, k, c:c + w] for k in range(K)], w)
                for s in range(2):
                    pe.wait_ge(qT_ready[s], it + 1)
                    heads(at_use(it, SCORE1, s), lambda r, h: qT[s][r, h, :], lambda r, h: kT[s][r, 32 * (h // 2):32 * (h // 2) + 32], 32)
                for s in range(2):
                    read(s, it, ULV)
                    pe.wait_ge(pT_ready[s], 2 * it + 2)
                    heads(at_use(it, PV1, s), lambda r, h: pT[s][r, h, :], lambda r, h: vn[s][r, KPH * h:KPH * h + KPH], KPH)
                for s in range(2):
                    pe.wait_ge(ao_ready[s], it + 1)
                    transposes(s, it, UAO, ao[s], 2)
                for s in range(2):
                    read(s, it, UAO)
                    product(s, it, UO, [aoT[s][:, k, :] for k in range(2)], [latow[:, k, :] for k in range(2)], D)
                for s in range(2):
                    pe.wait_ge(xn_ready[s], 3 * it + 3)
                    transposes(s, it, XT2, xn[s], K)
                for s in range(2):
                    read(s, it, XT2)
                    product(s, it, ULOG, [xT[s][:, k, :] for k in range(K)], [rw[:, k, :] for k in range(K)], E)


def phase_route(nc, core, n, eps):
    tab, probs = core.tab, core.probs
    TE = T * E
    with ExitStack() as ctx:
        sb = lambda name, shape, dt=F32: ctx.enter_context(nc.sbuf_tensor(f"r{n}_{name}", shape, dt))
        sem = semaphores(nc, ctx, f"r{n}_")
        top, idx = sb("top", [P, T, E]), sb("idx", [P, T, E], U32)
        idxf = sb("idxf", [P, T, 2])
        pick = sb("pick", [P, 2, T, E])
        both = sb("both", [P, T, E])
        wsum, winv = sb("wsum", [P, T]), sb("winv", [P, T])
        off = sb("off", [P, T + 1, E])
        over = sb("over", [P, E, E])
        tiles = sb("tiles", [P, E])
        upto, first = sb("upto", [P, E]), sb("first", [P, E])
        pos, posk = sb("pos", [P, T, E]), sb("posk", [P, T, E])
        slotf = sb("slotf", [P, 2, T])
        cmp = sb("cmp", [1, ST, E])
        owner = sb("owner", [1, ST])
        ps = ctx.enter_context(nc.psum_tensor(f"r{n}_ps", [P, 2, 512], F32))
        picked, counted, slots_ready, sent = sem("picked"), sem("counted"), sem("slots_ready"), sem("sent")
        block = ctx.enter_context(nc.Block())

        @block.vector
        def _(dve):
            for t in range(T):
                dve.max(top[:, t, :], probs[:, t, :])
            dve.drain()
            for t in range(T):
                dve.max_index(idx[:, t, :], top[:, t, :], probs[:, t, :])
            dve.drain()
            dve.tensor_copy(idxf[:], idx[:, :, 0:2])
            dve.tensor_tensor(wsum[:], top[:, :, 0], top[:, :, 1], ALU.add)
            dve.drain()
            if eps:
                dve.tensor_scalar(wsum[:], wsum[:], eps, None, ALU.add)
                dve.drain()
            dve.reciprocal(winv[:], wsum[:])
            for k in range(2):
                dve.tensor_tensor(pick[:, k], tab("expert_id").unsqueeze(1).to_broadcast([P, T, E]),
                                  idxf[:, :, k:k + 1].to_broadcast([P, T, E]), ALU.is_equal)
            dve.drain()
            dve.tensor_tensor(core.gate[:], top[:, :, 0:2], winv[:].unsqueeze(2).to_broadcast([P, T, 2]), ALU.mult)
            dve.tensor_tensor(both[:], pick[:, 0], pick[:, 1], ALU.add).then_inc(picked, 1)
            dve.memset(off[:, 0, :], 0.0)
            dve.wait_ge(counted, 1)
            for t in range(T):
                dve.drain()
                dve.tensor_tensor(off[:, t + 1, :], off[:, t, :], ps[:, 1, E * t:E * t + E], ALU.add)
            dve.drain()
            dve.tensor_tensor(over[:], off[:, T, :].unsqueeze(2).to_broadcast([P, E, E]),
                              tab("step128").unsqueeze(1).to_broadcast([P, E, E]), ALU.is_gt)
            dve.tensor_tensor(pos[:], off[:, 0:T, :], ps[:, 0, 0:TE].rearrange("p (t e) -> p t e", e=E), ALU.add)
            dve.drain()
            dve.tensor_reduce(tiles[:], over[:], X, ALU.add)
            dve.drain()
            dve.tensor_tensor(over[:], tab("upto").rearrange("p (a b) -> p a b", a=E),
                              tiles[:].unsqueeze(1).to_broadcast([P, E, E]), ALU.mult)
            dve.drain()
            dve.tensor_reduce(upto[:], over[:], X, ALU.add)
            dve.drain()
            dve.tensor_tensor(first[:], upto[:], tiles[:], ALU.subtract)
            dve.tensor_tensor(cmp[:], upto[0:1, :].unsqueeze(1).to_broadcast([1, ST, E]),
                              tab("tile_id")[0:1, :].unsqueeze(2).to_broadcast([1, ST, E]), ALU.is_le)
            dve.drain()
            dve.tensor_reduce(owner[:], cmp[:], X, ALU.add)
            dve.tensor_copy(core.tiles_before[:], first[0:1, :])
            dve.drain()
            dve.tensor_scalar(first[:], first[:], float(P), None, ALU.mult)
            dve.tensor_scalar(core.expert_of[:], owner[:], float(E - 1), None, ALU.min)
            dve.drain()
            dve.tensor_tensor(pos[:], pos[:], first[:].unsqueeze(1).to_broadcast([P, T, E]), ALU.add)
            for k in range(2):
                dve.drain()
                dve.tensor_tensor(posk[:], pos[:], pick[:, k], ALU.mult)
                dve.drain()
                dve.tensor_reduce(slotf[:, k, :], posk[:], X, ALU.add)
            dve.drain()
            dve.tensor_copy(core.slot[:], slotf[:]).then_inc(slots_ready, 1)

        @block.tensor
        def _(pe):
            pe.wait_ge(picked, 1)
            m = both[:].rearrange("p t e -> p (t e)")
            pe.matmul(ps[:, 0, 0:TE], tab("before"), m, start=True, stop=True)
            pe.matmul(ps[:, 1, 0:TE], tab("ones"), m, start=True, stop=True).then_inc(counted, 1)

        @block.gpsimd
        def _(pool):
            pool.wait_ge(slots_ready, 1)
            for t in range(T):
                for k in range(2):
                    pool.indirect_dma_start(core.sent[n], bass.IndirectOffsetOnAxis(ap=core.slot[:, k, t:t + 1], axis=0),
                                            core.rows[:, t, :], None).then_inc(sent, 16)
            pool.wait_ge(sent, 16 * 2 * T)


def phase_experts(nc, core, n, F, biased):
    A, tab = core.A, core.tab
    NF, NC = F // P, F // 512
    w1d, w2d = A[f"w1_{n}"], A[f"w2_{n}"]
    with ExitStack() as ctx:
        sb = lambda name, shape, dt=F32: ctx.enter_context(nc.sbuf_tensor(f"e{n}_{name}", shape, dt))
        sem = semaphores(nc, ctx, f"e{n}_")
        w1, w2 = sb("w1", [P, 2, K, F]), sb("w2", [P, 2, NF, D])
        if biased:
            b1, b2 = sb("b1", [P, 2, F]), sb("b2", [P, 2, D])
        xg, xT = sb("xg", [P, D]), sb("xT", [P, K, P])
        h, hT = sb("h", [P, F]), sb("hT", [P, NF, P])
        y = sb("y", [P, D])
        HP = ctx.enter_context(nc.psum_tensor(f"e{n}_HP", [P, 4, 512], F32))
        TP = ctx.enter_context(nc.psum_tensor(f"e{n}_TP", [P, 2, 512], F32))
        XP = ctx.enter_context(nc.psum_tensor(f"e{n}_XP", [P, 512], F32))
        YP = ctx.enter_context(nc.psum_tensor(f"e{n}_YP", [P, 512], F32))
        w_in = sem("w_in")
        rows_in, xT_made, xT_copied = sem("rows_in"), sem("xT_made"), sem("xT_copied")
        h_made, h_read, act_done = sem("h_made"), sem("h_read"), sem("act_done")
        hT_made, hT_copied = sem("hT_made"), [sem("hT_copied0"), sem("hT_copied1")]
        y_made, y_stored = sem("y_made"), sem("y_stored")
        y_copied = sem("y_copied")
        PER = 16 * (4 if biased else 2)

        block = ctx.enter_context(nc.Block())

        def parity(eng, m):
            e = eng.value_load(core.expert_of[0:1, ds(m, 1)], min_val=0, max_val=E - 1)
            return e, e & 1

        def peel(eng, step):
            step(0, True, False)
            with eng.Fori(1, ST - 1) as m:
                step(m, False, False)
            step(ST - 1, False, True)

        @block.sync
        def _(sp):
            def load(e):
                sp.dma_start(w1[:, e % 2], w1d[e].rearrange("(k p) f -> p k f", p=P)).then_inc(w_in, 16)
                sp.dma_start(w2[:, e % 2], w2d[e].rearrange("(k p) d -> p k d", p=P)).then_inc(w_in, 16)
                if biased:
                    sp.dma_start(b1[:, e % 2], A["b1_0"][e:e + 1, :].partition_broadcast(P).rearrange("p a f -> p (a f)")).then_inc(w_in, 16)
                    sp.dma_start(b2[:, e % 2], A["b2_0"][e:e + 1, :].partition_broadcast(P).rearrange("p a f -> p (a f)")).then_inc(w_in, 16)
            load(0)
            for e in range(1, E):
                sp.wait_ge(w_in, PER * e)
                if e >= 2:
                    before = sp.value_load(core.tiles_before[0:1, e - 1:e], min_val=0, max_val=ST)
                    sp.wait_ge(y_copied, before + 1)
                load(e)

        @block.gpsimd
        def _(pool):
            def store(m):
                pool.wait_ge(y_copied, m + 2)
                pool.dma_start(core.back[n][ds(m * P, P), :], y[:]).then_inc(y_stored, 16)

            def fetch(m):
                pool.wait_ge(xT_made, m)
                pool.dma_start(xg[:], core.sent[n][ds(m * P, P), :]).then_inc(rows_in, 16)
            pool.dma_start(xg[:], core.sent[n][0:P, :]).then_inc(rows_in, 16)
            fetch(1)
            with pool.Fori(2, ST) as m:
                fetch(m)
                store(m - 2)
            store(ST - 2)
            store(ST - 1)
            pool.wait_ge(y_stored, 16 * ST)

        @block.vector
        def _(dve):
            dve.memset(y[:], 0.0).then_inc(y_copied, 1)

            def step(m, first, last):
                dve.drain()
                if biased:
                    _, p = parity(dve, m)
                    for c in range(NC):
                        dve.wait_ge(h_made, NC * m + c + 1)
                        dve.tensor_tensor(h[:, 512 * c:512 * c + 512].unsqueeze(1), HP[:, c, :].unsqueeze(1),
                                          b1[:, ds(p, 1), 512 * c:512 * c + 512], ALU.add).then_inc(h_read, 1)
                for c in range(1, NC, 2):
                    dve.wait_ge(hT_made, NC * m + c + 1)
                    dve.tensor_copy(hT[:, 4 * c:4 * c + 4, :].rearrange("p a n -> p (a n)"), TP[:, 1, :]).then_inc(hT_copied[1], 1)
                dve.drain()
                if not first:
                    dve.wait_ge(y_stored, 16 * m)
                dve.wait_ge(y_made, m + 1)
                if biased:
                    dve.tensor_tensor(y[:].unsqueeze(1), YP[:].unsqueeze(1), b2[:, ds(p, 1), :], ALU.add).then_inc(y_copied, 1)
                else:
                    dve.tensor_copy(y[:], YP[:]).then_inc(y_copied, 1)
            peel(dve, step)

        @block.scalar
        def _(act):
            def copy_xT(m):
                act.wait_ge(xT_made, m + 1)
                act.activation(xT[:].rearrange("p k n -> p (k n)"), XP[:], ACT.Copy).then_inc(xT_copied, 1)

            copy_xT(0)

            def step(m, first, last):
                for c in range(NC):
                    act.wait_ge(h_read if biased else h_made, NC * m + c + 1)
                    act.activation(h[:, 512 * c:512 * c + 512], h[:, 512 * c:512 * c + 512] if biased else HP[:, c, :], ACT.Gelu)\
                       .then_inc(act_done, 1)
                    if c % 2:
                        act.wait_ge(hT_made, NC * m + c)
                        act.activation(hT[:, 4 * c - 4:4 * c, :].rearrange("p a n -> p (a n)"), TP[:, 0, :], ACT.Copy)\
                           .then_inc(hT_copied[0], 1)
                if not last:
                    copy_xT(m + 1)
            peel(act, step)

        @block.tensor
        def _(pe):
            def rows_T(m):
                pe.wait_ge(rows_in, 16 * m + 16)
                for k in range(K):
                    op = pe.transpose(XP[:, P * k:P * k + P], xg[:, P * k:P * k + P], tab("ident"))
                op.then_inc(xT_made, 1)

            def hidden(m, p, c, first):
                if not first:
                    pe.wait_ge(h_read if biased else act_done, NC * m - NC + c + 1)
                for k in range(K):
                    op = pe.matmul(HP[:, c, :], xT[:, k, :], w1[:, ds(p, 1), k, 512 * c:512 * c + 512],
                                   start=(k == 0), stop=(k == K - 1))
                op.then_inc(h_made, 1)

            def hidden_T(m, c, first):
                pe.wait_ge(act_done, NC * m + c + 1)
                if not (first and c < 2):
                    pe.wait_ge(hT_copied[c % 2], NC // 2 * m + c // 2)
                for k in range(4):
                    op = pe.transpose(TP[:, c % 2, P * k:P * k + P], h[:, 512 * c + P * k:512 * c + P * k + P], tab("ident"))
                op.then_inc(hT_made, 1)

            def step(m, first, last):
                e, p = parity(pe, m)
                pe.wait_ge(w_in, e * PER + PER)
                pe.wait_ge(xT_copied, m + 1)
                hidden(m, p, 0, first)
                for c in range(1, NC):
                    hidden(m, p, c, first)
                    hidden_T(m, c - 1, first)
                if not last:
                    rows_T(m + 1)
                hidden_T(m, NC - 1, first)
                pe.wait_ge(y_copied, m + 1)
                for c in range(NC):
                    pe.wait_ge(hT_copied[c % 2], NC // 2 * m + c // 2 + 1)
                    for k in range(4 * c, 4 * c + 4):
                        op = pe.matmul(YP[:], hT[:, k, :], w2[:, ds(p, 1), k, :], start=(k == 0), stop=(k == NF - 1))
                op.then_inc(y_made, 1)
            rows_T(0)
            peel(pe, step)


def phase_combine(nc, core, n, scale):
    with ExitStack() as ctx:
        got = ctx.enter_context(nc.sbuf_tensor(f"m{n}_got", [P, T, 2, D], F32))
        come = core.come
        block = ctx.enter_context(nc.Block())

        @block.gpsimd
        def _(pool):
            for t in range(T):
                for k in range(2):
                    pool.indirect_dma_start(got[:, t, k, :], None, core.back[n],
                                            bass.IndirectOffsetOnAxis(ap=core.slot[:, k, t:t + 1], axis=0)).then_inc(come[t], 16)

        @block.vector
        def _(dve):
            if scale != 1.0:
                dve.tensor_scalar(core.gate[:], core.gate[:], scale, None, ALU.mult)
            for t in range(T):
                for k in range(2):
                    dve.drain()
                    dve.wait_ge(come[t], 32 * n + 32)
                    dve.scalar_tensor_tensor(core.x[:, t, :], got[:, t, k, :], core.gate[:, t, k:k + 1], core.x[:, t, :],
                                             ALU.mult, ALU.add)


def phase_layer1(nc, core):
    A, x, tab = core.A, core.x, core.tab
    with ExitStack() as ctx:
        sb = lambda name, shape, dt=F32: ctx.enter_context(nc.sbuf_tensor("l1_" + name, shape, dt))
        sem = semaphores(nc, ctx, "l1_")
        sems = lambda name: [sem(f"{name}{s}") for s in range(2)]
        two = lambda name, shape: [sb(f"{name}{s}", shape) for s in range(2)]
        W3 = 3 * HS

        wqkv, wo, rw = sb("wqkv", [P, K, 4 * HS]), sb("wo", [P, 2, D]), sb("rw", [P, K, E])
        ctxT = sb("ctxT", [P, NB, K, SK])
        ctxn = sb("ctxn", [P, NB, 2, D])
        ctxl = sb("ctxl", [B, D])
        stats, mv, veps, rstd = two("stats", [P, 6]), two("mv", [P, 2]), two("veps", [P, 1]), two("rstd", [P, 1])
        mhalf = sb("mhalf", [P, 1])
        xn, xT = two("xn", [P, D]), two("xT", [P, K, P])
        ls, lsl, lT = two("ls", [P, SK]), two("lsl", [P, 32]), two("lT", [P, 3, P])
        nm, rs, ri = two("nm", [P, 2]), two("rs", [P, 2]), two("ri", [P, 2])
        ex = two("ex", [P, D])
        t1, t2, r, v, rT = (two(a, s) for a, s in (("t1", [P, W3]), ("t2", [P, W3]), ("r", [P, W3]), ("v", [P, HS]), ("rT", [P, 3, P])))
        sm, pT = two("sm", [P, 2, P]), two("pT", [P, 2, P])
        o, oT = two("o", [P, 2 * HS]), two("oT", [P, 2, P])
        lg = two("lg", [P, E])

        R = [[ctx.enter_context(nc.psum_tensor(f"l1_R{s}{k}", [P, 512], F32)) for k in range(2)] for s in range(2)]
        LS = ctx.enter_context(nc.psum_tensor("l1_LS", [P, NB, 512], F32))

        weights_in, ctxl_in = sem("weights_in"), sem("ctxl_in")
        WEIGHTS = 16 * 4
        ctxT_in, ctxn_in = [sem(f"ctxT_in{b}") for b in range(NB)], [sem(f"ctxn_in{b}") for b in range(NB)]
        mhalf_set = sem("mhalf_set")
        var_ready, rstd_ready, xn_ready, rows_kept = sems("var_ready"), sems("rstd_ready"), sems("xn_ready"), sems("rows_kept")
        r_ready = sems("r_ready")
        r_free = [sems(f"r_free{s}_") for s in range(2)]
        ls_ready, ls_free, lin_used = sem("ls_ready"), sem("ls_free"), sem("lin_used")
        lsl_ready = sems("lsl_ready")
        fmax, fexp = sems("fmax"), sems("fexp")
        r_made, p_made, shifted, exp_done = sems("r_made"), sems("p_made"), sems("shifted"), sems("exp_done")
        o_made = sems("o_made")
        lshift, lexp = sems("lshift"), sems("lexp")

        XT0, LT, LO, XT1, QKV, RT, SC, PTT, PV, OT, WO, XT2, LOG = range(13)
        USES, OF_BANK = 13, (7, 6)
        block = ctx.enter_context(nc.Block())

        def ready(eng, s, it, n):
            eng.wait_ge(r_ready[s], USES * it + n + 1)

        @block.sync
        def _(sp):
            sp.dma_start(wqkv[:], A["wqkv1"].rearrange("(k p) n -> p k n", p=P)).then_inc(weights_in, 16)
            sp.dma_start(wo[:], A["wo1"].rearrange("(k p) n -> p k n", p=P)).then_inc(weights_in, 16)
            sp.dma_start(rw[:], A["rw1"].rearrange("(k p) n -> p k n", p=P)).then_inc(weights_in, 16)
            sp.dma_start(ctxl[:], A["ctx"].rearrange("b k d -> b (k d)")[:, (SK - 1) * D:SK * D]).then_inc(weights_in, 16)

            def loads(j, first):
                for b in range(NB):
                    if not first:
                        sp.wait_ge(ls_ready, NB * j - NB + b + 1)
                    sp.dma_start(ctxT[:, b], A["ctxT"][ds(j * NB + b, 1), :, :]
                                 .rearrange("a p n -> p (a n)").rearrange("p (k n) -> p k n", k=K)).then_inc(ctxT_in[b], 16)
                for b in range(NB):
                    if not first:
                        sp.wait_ge(lin_used, NB * j - NB + b + 1)
                    sp.dma_start(ctxn[:, b], A["ctx"][ds(j * NB + b, 1), 0:2 * P, :]
                                 .rearrange("a (k p) d -> p (a k) d", p=P)).then_inc(ctxn_in[b], 16)
            loads(0, True)
            with sp.Fori(1, T) as j:
                loads(j, False)

        @block.gpsimd
        def _(pool):
            pool.memset(mhalf[:], -0.5).then_inc(mhalf_set, 1)
            pool.wait_ge(mhalf_set, 1)
            for kept in rows_kept:
                pool.sem_inc(kept, 1)
            with pool.Fori(0, T // 2) as it:
                for k in range(3):
                    for s in range(2):
                        pool.drain()
                        pool.wait_ge(var_ready[s], 3 * it + k + 1)
                        pool.tensor_tensor(rstd[s][:], veps[s][:], mhalf[:], ALU.pow).then_inc(rstd_ready[s], 1)
                for s in range(2):
                    pool.wait_ge(xn_ready[s], 3 * it + 3)
                    pool.wait_ge(mhalf_set, 1)
                    pool.tensor_copy(core.rows[:, ds(2 * it + s, 1), :].rearrange("p a d -> p (a d)"), xn[s][:])\
                        .then_inc(rows_kept[s], 1)

        @block.vector
        def _(dve):
            dve.wait_ge(weights_in, WEIGHTS)
            def tile(it, s):
                return x[:, ds(2 * it + s, 1), :].rearrange("p a d -> p (a d)")

            def norm(it, k):
                for s in range(2):
                    dve.drain()
                    dve.bn_stats(stats[s][:], tile(it, s))
                for s in range(2):
                    dve.drain()
                    dve.bn_aggr(mv[s][:], stats[s][:])
                for s in range(2):
                    dve.drain()
                    dve.tensor_scalar(veps[s][:], mv[s][:, 1:2], EPS, None, ALU.add).then_inc(var_ready[s], 1)
                for s in range(2):
                    dve.wait_ge(rstd_ready[s], 3 * it + k + 1)
                    if k == 0:
                        dve.wait_ge(rows_kept[s], it + 1)
                    if k > 0:
                        ready(dve, s, it, (XT0, XT1)[k - 1])
                    dve.tensor_scalar(xn[s][:], tile(it, s), mv[s][:, 0:1], rstd[s][:, 0:1],
                                      ALU.subtract, ALU.mult).then_inc(xn_ready[s], 1)

            for free in r_free[0] + r_free[1]:
                dve.sem_inc(free, 1)
            with dve.Fori(0, T // 2) as it:
                norm(it, 0)
                for s in range(2):
                    dve.drain()
                    dve.wait_ge(ls_free, NB * (2 * it + s) + NB)
                    dve.tensor_scalar(lsl[s][:], tab("eye_tile").rearrange("p (t n) -> p t n", n=32)[:, ds(2 * it + s, 1), :]
                                      .rearrange("p a n -> p (a n)"), ls[s][:, SK - 1:SK], None, ALU.mult).then_inc(lsl_ready[s], 1)
                for s in range(2):
                    dve.drain()
                    ready(dve, s, it, LO)
                    dve.tensor_reduce(nm[s][:, 0:1], R[s][LO % 2][:], X, ALU.max, negate=True).then_inc(fmax[s], 1)
                for s in range(2):
                    dve.wait_ge(fexp[s], it + 1)
                    dve.reciprocal(ri[s][:, 0:1], rs[s][:, 0:1])
                    dve.drain()
                    dve.scalar_tensor_tensor(tile(it, s), ex[s][:], ri[s][:, 0:1], tile(it, s), ALU.mult, ALU.add)
                norm(it, 1)
                for s in range(2):
                    dve.drain()
                    ready(dve, s, it, QKV)
                    q = R[s][QKV % 2][:, 0:W3]
                    pair = lambda a: a.rearrange("p (h i c) -> p h i c", h=3, c=2)
                    wide = lambda name: tab(name).rearrange("p (i c) -> p i c", c=2).unsqueeze(1)
                    dve.tensor_tensor(t1[s][:].rearrange("p (h i) -> p h i", h=3), q.rearrange("p (h i) -> p h i", h=3),
                                      tab("cos").unsqueeze(1).to_broadcast([P, 3, HS]), ALU.mult)
                    for c in range(2):
                        dve.tensor_tensor(pair(t2[s][:])[:, :, :, c], pair(q)[:, :, :, 1 - c],
                                               wide("sin")[:, :, :, c].to_broadcast([P, 3, HS // 2]), ALU.mult)
                    dve.tensor_copy(v[s][:], R[s][QKV % 2][:, W3:W3 + HS]).then_inc(r_free[s][QKV % 2], 1)
                    dve.drain()
                    dve.tensor_tensor(r[s][:], t1[s][:], t2[s][:], ALU.add).then_inc(r_made[s], 1)
                for s in range(2):
                    dve.drain()
                    ready(dve, s, it, SC)
                    dve.scalar_tensor_tensor(sm[s][:], R[s][SC % 2][:, 0:2 * P].rearrange("p (h k) -> p h k", h=2), float(HS) ** -0.5,
                                             tab("block_causal").unsqueeze(1).to_broadcast([P, 2, P]), ALU.mult, ALU.add)\
                       .then_inc(r_free[s][SC % 2], 1)
                    dve.drain()
                    dve.tensor_reduce(nm[s][:], sm[s][:], X, ALU.max, negate=True)
                    dve.drain()
                    dve.tensor_tensor(sm[s][:], sm[s][:], nm[s][:].unsqueeze(2).to_broadcast([P, 2, P]), ALU.add)\
                       .then_inc(shifted[s], 1)
                for s in range(2):
                    dve.drain()
                    dve.wait_ge(exp_done[s], it + 1)
                    dve.tensor_reduce(rs[s][:], sm[s][:], X, ALU.add)
                    dve.drain()
                    dve.reciprocal(ri[s][:], rs[s][:])
                    dve.drain()
                    dve.tensor_tensor(sm[s][:], sm[s][:], ri[s][:].unsqueeze(2).to_broadcast([P, 2, P]), ALU.mult).then_inc(p_made[s], 1)
                for s in range(2):
                    ready(dve, s, it, PV)
                    dve.tensor_copy(o[s][:], R[s][PV % 2][:, 0:2 * HS]).then_inc(r_free[s][PV % 2], 1)
                for s in range(2):
                    ready(dve, s, it, WO)
                    dve.tensor_tensor(tile(it, s), tile(it, s), R[s][WO % 2][:], ALU.add).then_inc(r_free[s][WO % 2], 1)
                norm(it, 2)
                for s in range(2):
                    dve.drain()
                    ready(dve, s, it, LOG)
                    dve.tensor_copy(lg[s][:], R[s][LOG % 2][:, 0:E]).then_inc(r_free[s][LOG % 2], 1)
                    dve.drain()
                    dve.tensor_reduce(nm[s][:, 0:1], lg[s][:], X, ALU.max, negate=True).then_inc(lshift[s], 1)
                for s in range(2):
                    dve.drain()
                    dve.wait_ge(lexp[s], it + 1)
                    dve.reciprocal(ri[s][:, 0:1], rs[s][:, 0:1])
                    dve.drain()
                    dve.tensor_scalar(core.probs[:, ds(2 * it + s, 1), :].rearrange("p a e -> p (a e)"), lg[s][:],
                                      ri[s][:, 0:1], None, ALU.mult)

        @block.scalar
        def _(act):
            act.wait_ge(weights_in, WEIGHTS)
            def copy(s, it, n, out, w):
                ready(act, s, it, n)
                act.activation(out, R[s][n % 2][:, 0:w], ACT.Copy).then_inc(r_free[s][n % 2], 1)

            flat = lambda a: a[:].rearrange("p k n -> p (k n)")
            with act.Fori(0, T // 2) as it:
                for s in range(2):
                    copy(s, it, XT0, flat(xT[s]), D)
                for s in range(2):
                    for b in range(NB):
                        rows = slice(S * b, S * b + S)
                        act.wait_ge(ls_ready, NB * (2 * it + s) + b + 1)
                        act.activation(ls[s][rows], LS[rows, b, 0:SK], ACT.Copy, scale=float(D) ** -0.5).then_inc(ls_free, 1)
                for s in range(2):
                    ready(act, s, it, LT)
                    act.activation(lT[s][0:32, 2, :], R[s][LT % 2][0:32, 2 * P:3 * P], ACT.Copy)
                    act.activation(lT[s][:, 0:2, :].rearrange("p k n -> p (k n)"), R[s][LT % 2][:, 0:2 * P], ACT.Copy)\
                       .then_inc(r_free[s][LT % 2], 1)
                for s in range(2):
                    act.wait_ge(fmax[s], it + 1)
                    act.activation(ex[s][:], R[s][LO % 2][:], ACT.Exp, bias=nm[s][:, 0:1], accum_out=rs[s][:, 0:1]).then_inc(r_free[s][LO % 2], 1)
                    act.drain()
                    act.sem_inc(fexp[s], 1)
                for s in range(2):
                    copy(s, it, XT1, flat(xT[s]), D)
                for s in range(2):
                    copy(s, it, RT, flat(rT[s]), 3 * P)
                for s in range(2):
                    act.wait_ge(shifted[s], it + 1)
                    act.activation(sm[s][:], sm[s][:], ACT.Exp).then_inc(exp_done[s], 1)
                for s in range(2):
                    copy(s, it, PTT, flat(pT[s]), 2 * P)
                for s in range(2):
                    copy(s, it, OT, flat(oT[s]), 2 * P)
                for s in range(2):
                    copy(s, it, XT2, flat(xT[s]), D)
                for s in range(2):
                    act.wait_ge(lshift[s], it + 1)
                    act.activation(lg[s][:], lg[s][:], ACT.Exp, bias=nm[s][:, 0:1], accum_out=rs[s][:, 0:1]).then_inc(lexp[s], 1)

        @block.tensor
        def _(pe):
            pe.wait_ge(weights_in, WEIGHTS)
            def free(s, it, n):
                pe.wait_ge(r_free[s][n % 2], OF_BANK[n % 2] * it + n // 2 + 1)

            def read(s, it, n):
                pe.wait_ge(r_free[s][n % 2], OF_BANK[n % 2] * it + n // 2 + 2)

            def transposes(s, it, n, src, count):
                free(s, it, n)
                for k in range(count):
                    op = pe.transpose(R[s][n % 2][:, P * k:P * k + P], src[:, P * k:P * k + P], tab("ident"))
                op.then_inc(r_ready[s], 1)

            def product(s, it, n, lhs, rhs, w):
                free(s, it, n)
                for k in range(len(lhs)):
                    op = pe.matmul(R[s][n % 2][:, 0:w], lhs[k], rhs[k], start=(k == 0), stop=(k == len(lhs) - 1))
                op.then_inc(r_ready[s], 1)

            with pe.Fori(0, T // 2) as it:
                for s in range(2):
                    pe.wait_ge(xn_ready[s], 3 * it + 1)
                    transposes(s, it, XT0, xn[s][:], K)
                for s in range(2):
                    read(s, it, XT0)
                    for b in range(NB):
                        pe.wait_ge(ctxT_in[b], 16 * (2 * it + s) + 16)
                        if s:
                            pe.wait_ge(ls_free, 8 * it + b + 1)
                        for k in range(K):
                            op = pe.matmul(LS[:, b, 0:SK], xT[s][:, k, :], ctxT[:, b, k, :], start=(k == 0), stop=(k == K - 1))
                        op.then_inc(ls_ready, 1)
                for s in range(2):
                    pe.wait_ge(lsl_ready[s], it + 1)
                    free(s, it, LT)
                    for k in range(2):
                        pe.transpose(R[s][LT % 2][:, P * k:P * k + P], ls[s][:, P * k:P * k + P], tab("ident"))
                    pe.transpose(R[s][LT % 2][0:32, 2 * P:3 * P], lsl[s][:], tab("ident")).then_inc(r_ready[s], 1)
                for s in range(2):
                    free(s, it, LO)
                    read(s, it, LT)
                    pe.matmul(R[s][LO % 2][:], lT[s][0:32, 2, :], ctxl[:], start=True, stop=True, skip_group_check=True)
                    for b in range(NB):
                        rows = slice(S * b, S * b + S)
                        pe.wait_ge(ctxn_in[b], 16 * (2 * it + s) + 16)
                        for k in range(2):
                            op = pe.matmul(R[s][LO % 2][rows, :], lT[s][:, k, rows], ctxn[:, b, k, :], start=False, stop=(k == 1),
                                           skip_group_check=True)
                        op.then_inc(lin_used, 1)
                    pe.drain()
                    pe.sem_inc(r_ready[s], 1)
                for s in range(2):
                    pe.wait_ge(xn_ready[s], 3 * it + 2)
                    transposes(s, it, XT1, xn[s][:], K)
                for s in range(2):
                    read(s, it, XT1)
                    product(s, it, QKV, [xT[s][:, k, :] for k in range(K)], [wqkv[:, k, :] for k in range(K)], 4 * HS)
                for s in range(2):
                    pe.wait_ge(r_made[s], it + 1)
                    transposes(s, it, RT, r[s][:], 3)
                for s in range(2):
                    read(s, it, RT)
                    free(s, it, SC)
                    for hd in range(2):
                        op = pe.matmul(R[s][SC % 2][:, P * hd:P * hd + P], rT[s][:, hd, :], rT[s][:, 2, :], start=True, stop=True)
                    op.then_inc(r_ready[s], 1)
                for s in range(2):
                    pe.wait_ge(p_made[s], it + 1)
                    transposes(s, it, PTT, sm[s][:].rearrange("p h k -> p (h k)"), 2)
                for s in range(2):
                    read(s, it, PTT)
                    free(s, it, PV)
                    for hd in range(2):
                        op = pe.matmul(R[s][PV % 2][:, HS * hd:HS * hd + HS], pT[s][:, hd, :], v[s][:], start=True, stop=True)
                    op.then_inc(r_ready[s], 1)
                for s in range(2):
                    read(s, it, PV)
                    transposes(s, it, OT, o[s][:], 2)
                for s in range(2):
                    read(s, it, OT)
                    product(s, it, WO, [oT[s][:, k, :] for k in range(2)], [wo[:, k, :] for k in range(2)], D)
                for s in range(2):
                    pe.wait_ge(xn_ready[s], 3 * it + 3)
                    transposes(s, it, XT2, xn[s][:], K)
                for s in range(2):
                    read(s, it, XT2)
                    product(s, it, LOG, [xT[s][:, k, :] for k in range(K)], [rw[:, k, :] for k in range(K)], E)


def build(nc, A, out, stop=5):
    with ExitStack() as ctx:
        core = Core(nc, ctx, A)
        setup_phase(nc, core)
        phase_cross0(nc, core)
        if stop >= 1:
            phase_self0(nc, core)
        if stop >= 2:
            phase_route(nc, core, 0, 1e-8)
            phase_experts(nc, core, 0, F0, True)
            phase_combine(nc, core, 0, 0.3)
        if stop >= 3:
            phase_layer1(nc, core)
        if stop >= 5:
            phase_route(nc, core, 1, 0.0)
            phase_experts(nc, core, 1, F1, False)
            phase_combine(nc, core, 1, 1.0)
        finish(nc, core, out)


def finish(nc, core, out):
    with ExitStack() as ctx:
        stored = ctx.enter_context(nc.semaphore("stored"))
        block = ctx.enter_context(nc.Block())

        @block.sync
        def _(sp):
            sp.dma_start(out.rearrange("b s d -> (b s) d").rearrange("(t p) d -> p t d", p=P), core.x[:]).then_inc(stored, 16)
            sp.wait_ge(stored, 16)


def layout(**inputs):
    a = {k: np.asarray(v) for k, v in inputs.items()}
    c = np.ascontiguousarray
    rowvec = lambda v: c(v.reshape(1, -1))
    ctx = a["ctx_1024"]
    ctxT = ctx.transpose(0, 2, 1)
    heads = lambda w: w.reshape(w.shape[:-1] + (H, DH))[..., :KPH].reshape(w.shape[:-1] + (LAT,))
    d = {
        "tables": tables(),
        "x": c(a["x"].reshape(B * S, D)),
        "ctx": c(ctx),
        "ctxT": c(ctxT.reshape(B, K, P, SK).transpose(0, 2, 1, 3).reshape(B, P, K * SK)),
        "ctx_lastT": c(ctx[:, SK - 1, :].T.reshape(K, P, B).transpose(1, 0, 2)),
        "mask": c(a["mask_Bx1xS2_if1"].reshape(T, NB * SK)),
        "wq": a["L0_xattn_Wq"], "wk": a["L0_xattn_Wk"], "wv": a["L0_xattn_Wv"], "wo": a["L0_xattn_Wo"],
        "bqT": c(a["L0_xattn_bq"].reshape(G, P).T), "bkT": c(a["L0_xattn_bk"].reshape(G, P).T),
        "bv": a["L0_xattn_bv"], "bo": a["L0_xattn_bo"],
        "wqkv": a["L0_attn_qkv_weights"],
        "lat_w": c(np.concatenate([heads(a["L0_ffn_q_w"]), a["L0_ffn_k_w"], a["L0_ffn_v_w"]], axis=1)),
        "lat_b": c(np.concatenate([heads(a["L0_ffn_q_b"]), a["L0_ffn_k_b"], a["L0_ffn_v_b"]])),
        "lat_ow": c(a["L0_ffn_o_w"][:LAT]), "lat_ob": a["L0_ffn_o_b"],
        "rw0": a["L0_ffn_router_w"], "rb0": a["L0_ffn_router_b"],
        "w1_0": a["L0_ffn_w1"], "b1_0": a["L0_ffn_b1"], "w2_0": a["L0_ffn_w2"], "b2_0": a["L0_ffn_b2"],
        "wqkv1": c(np.concatenate([a["L1_attn_Wq"].reshape(2 * HS, D), a["L1_attn_Wk"], a["L1_attn_Wv"]], axis=0).T),
        "wo1": c(a["L1_attn_Wo"].T),
        "rw1": c(a["L1_ffn_router_w"].T),
        "w1_1": a["L1_ffn_w1"], "w2_1": a["L1_ffn_w2"],
    }
    return {k: c(v) for k, v in d.items()}


def kernel(**inputs):
    import concourse.bacc as bacc
    from concourse.bass_utils import run_bass_kernel_spmd

    nc = bacc.Bacc("TRN2", target_bir_lowering=False, num_devices=1)
    arrays = {f"in_{k}": v for k, v in layout(**inputs).items()}
    A = {k[3:]: nc.dram_tensor(k, v.shape, mybir.dt.from_np(v.dtype), kind="ExternalInput").ap() for k, v in arrays.items()}
    out = nc.dram_tensor("out", (B, S, D), F32, kind="ExternalOutput").ap()
    build(nc, A, out)
    r = run_bass_kernel_spmd(nc, [arrays], core_ids=[0])
    return r.results[0]["out"]
```

```python
from contextlib import ExitStack

import numpy as np

import concourse.bass as bass
from concourse import mybir

F32 = mybir.dt.float32
F32R = mybir.dt.float32r
I32 = mybir.dt.int32
U32 = mybir.dt.uint32
ALU = mybir.AluOpType
ACT = mybir.ActivationFunctionType
X = mybir.AxisListType.X
ds = bass.ds

P = 128
B, S, D = 32, 32, 512
SK = 257
SKP = SK + 1
K = D // P
T = B * S // P
NB = P // S
H, DH = 16, 32
G = 4
LAT, KPH = 256, 16
E = 8
ST = 2 * B * S // P + E - 1
F0, F1 = 1024, 2048
HS = 128
EPS = 1e-5
NEG = -1e9
BIG = 3e38

TABLES = {}
_at = 0
for _name, _n in (("ident", P), ("ones", P), ("before", P), ("one_at", 2 * B - 1), ("eye_tile", T * 32),
                  ("tril", S), ("untril", S), ("cos", HS), ("sin", HS), ("block_causal", P),
                  ("expert_id", E), ("step128", E), ("upto", E * E), ("tile_id", ST)):
    TABLES[_name] = (_at, _n)
    _at += _n
TABLE = _at


def tables():
    p = np.arange(P)
    t = {}
    t["ident"] = np.eye(P)
    t["ones"] = np.ones((P, P))
    t["before"] = p[:, None] < p[None, :]
    t["one_at"] = np.broadcast_to(np.arange(2 * B - 1) == B - 1, (P, 2 * B - 1))
    t["eye_tile"] = (np.arange(32)[None, None] == NB * np.arange(T)[None, :, None] + (p // S)[:, None, None])
    low = np.tril(np.ones((S, S)))[p % S]
    t["tril"] = low * float(DH) ** -0.5
    t["untril"] = NEG * (1 - low)
    theta = np.float32(10000.0) ** (np.float32(-2.0) * np.arange(0, HS, 2, dtype=np.float32) / np.float32(HS))
    angle = (p % S).astype(np.float32)[:, None] * theta[None]
    t["cos"] = np.repeat(np.cos(angle), 2, axis=1)
    t["sin"] = np.stack([-np.sin(angle), np.sin(angle)], -1)
    t["block_causal"] = np.where((p[:, None] // S == p[None] // S) & (p[None] <= p[:, None]), 0.0, -1e30)
    t["expert_id"] = np.broadcast_to(np.arange(E), (P, E))
    t["step128"] = np.broadcast_to(P * np.arange(E), (P, E))
    t["upto"] = np.broadcast_to(np.tril(np.ones((E, E))).reshape(1, -1), (P, E * E))
    t["tile_id"] = np.broadcast_to(np.arange(ST), (P, ST))
    return np.concatenate([np.asarray(t[n], np.float32).reshape(P, -1) for n in TABLES], axis=1)


def semaphores(nc, ctx, prefix):
    taken = []

    def give_back():
        nc.clear_and_free_semaphores(taken)
        nc.all_engine_barrier()
    ctx.callback(give_back)

    def sem(name):
        taken.append(nc.alloc_semaphore(prefix + name))
        return taken[-1]
    return sem


def passes(pe, out, xs, ws, first, last):
    (x_high, x_low), (w_high, w_low) = xs, ws
    pe.matmul(out, x_high, w_low, start=first, stop=False)
    pe.matmul(out, x_low, w_high, start=False, stop=False)
    return pe.matmul(out, x_high, w_high, start=False, stop=last)


class Core:

    def __init__(self, nc, ctx, A):
        self.nc, self.A = nc, A
        self.sb = lambda name, shape, dt=F32: ctx.enter_context(nc.sbuf_tensor(name, shape, dt))
        self.x = self.sb("x", [P, T, D])
        self.rows = self.sb("rows", [P, T, D])
        self.probs = self.sb("probs", [P, T, E])
        self.table = self.sb("table", [P, TABLE])
        self.slot = self.sb("slot", [P, 2, T], U32)
        self.gate = self.sb("gate", [P, T, 2])
        self.expert_of = self.sb("expert_of", [1, ST], I32)
        self.tiles_before = self.sb("tiles_before", [1, E], I32)
        dram = lambda name, rows: nc.dram_tensor(name, [rows, D], F32, kind="Internal").ap()
        self.sent = [dram(f"sent{n}", (ST + 1) * P) for n in range(2)]
        self.back = [dram(f"back{n}", ST * P) for n in range(2)]

    def tab(self, name):
        a, n = TABLES[name]
        return self.table[:, a:a + n]


def phase_cross0(nc, core):
    A = core.A
    x, tab = core.x, core.tab
    with ExitStack() as ctx:
        sb = lambda name, shape, dt=F32: ctx.enter_context(nc.sbuf_tensor("c0_" + name, shape, dt))
        sem = semaphores(nc, ctx, "c0_")
        pb = lambda name, banks: ctx.enter_context(nc.psum_tensor("c0_" + name, [P, banks, 512], F32))

        wq, wo = sb("wq", [P, K, D]), sb("wo", [P, K, D])
        wk, wv = core.rows[:, 0:K, :], core.rows[:, K:2 * K, :]
        wkh, wkl, wvh, wvl = (sb(n, [P, K, D], F32R) for n in ("wkh", "wkl", "wvh", "wvl"))
        zero = sb("zero", [P, D])
        bq, bk = sb("bq", [P, G]), sb("bk", [P, G])
        bv, bo = sb("bv", [P, D]), sb("bo", [P, D])
        ctxT = sb("ctxT", [P, NB, K, SKP])
        ctxh, ctxl = sb("ctxh", [P, 2, K, SKP], F32R), sb("ctxl", [P, 2, K, SKP], F32R)
        lastT = sb("lastT", [P, K, NB, B])
        maskt = sb("maskt", [P, NB, SK], I32)
        keep = sb("keep", [P, NB, SK])
        bound = sb("bound", [P, NB, SK])
        stats = sb("stats", [P, 6])
        mv = sb("mv", [P, 2])
        mhalf = sb("mhalf", [P, 1])
        veps = sb("veps", [P, 1])
        rstd = sb("rstd", [P, 1])
        xn = sb("xn", [P, D])
        xT = sb("xT", [P, K, P])
        qbd = sb("qbd", [P, NB, G, NB, S])
        kT = sb("kT", [P, 2, G, SK])
        v = sb("v", [P, 2, 2, D])
        vlast = sb("vlast", [P, G, P])
        sm = sb("sm", [P, 2, G, SK])
        nmax = sb("nmax", [P, 2, G])
        rsum = sb("rsum", [P, 2, G])
        rinv = sb("rinv", [P, 2, G])
        plast = sb("plast", [P, G, 32])
        pT = sb("pT", [P, 2 * G, P])
        plastT = sb("plastT", [P, P])
        o = sb("o", [P, D])
        oT = sb("oT", [P, K, P])

        KV = pb("KV", 3)
        SC = pb("SC", 2)
        TB = pb("TB", 2)
        O = pb("O", 1)

        weights_in, wo_in = sem("weights_in"), sem("wo_in")
        w_high, w_split = sem("w_high"), sem("w_split")
        ctx_high, ctx_split = sem("ctx_high"), sem("ctx_split")
        zero_made, rows_cleared = sem("zero_made"), sem("rows_cleared")
        ctx_in = [sem(f"ctx_in{b}") for b in range(NB)]
        mask_in = sem("mask_in")
        keep_made = sem("keep_made")
        bound_made = sem("bound_made")
        cleared = sem("cleared")
        mhalf_set = sem("mhalf_set")
        var_ready = sem("var_ready")
        rstd_ready = sem("rstd_ready")
        xn_ready = sem("xn_ready")
        t_ready = sem("t_ready")
        t_free = [sem("t_free0"), sem("t_free1")]
        kv_ready = sem("kv_ready")
        kT_ready = sem("kT_ready")
        v_ready = sem("v_ready")
        vlast_done = sem("vlast_done")
        vlast_ready = sem("vlast_ready")
        scores_ready = sem("scores_ready")
        masked = sem("masked")
        max_ready = sem("max_ready")
        exp_done = sem("exp_done")
        plast_ready = sem("plast_ready")
        pv_ready = sem("pv_ready")
        o_ready = sem("o_ready")

        PT_USE = (0, 3, 6, 11)
        XT_USE, Q_USE, OT_USE, OUT_USE, USES = 9, 10, 14, 15, 16
        FIRST_USES = 2

        def use(n, last):
            return n - 2 if last and n > Q_USE else n

        block = ctx.enter_context(nc.Block())

        @block.sync
        def _(sp):
            for t, a in ((wk, "wk"), (wv, "wv"), (wq[:], "wq")):
                sp.dma_start(t, A[a].rearrange("(k p) n -> p k n", p=P)).then_inc(weights_in, 16)
            sp.dma_start(core.table[:], A["tables"]).then_inc(weights_in, 16)
            sp.dma_start(x[:], A["x"].rearrange("(t p) d -> p t d", p=P)).then_inc(weights_in, 16)
            for r in range(NB):
                sp.dma_start(lastT[:, :, r, :], A["ctx_lastT"]).then_inc(weights_in, 16)
            for t, a in ((bq, "bqT"), (bk, "bkT")):
                sp.dma_start(t[:], A[a]).then_inc(weights_in, 16)
            sp.dma_start(bv[:], A["bv"].partition_broadcast(P)).then_inc(weights_in, 16)

            def loads(j, first):
                if not first:
                    sp.wait_ge(bound_made, j)
                sp.dma_start(maskt[:], A["mask"][ds(j, 1), :].partition_broadcast(P)
                             .rearrange("p a (b k) -> p (a b) k", b=NB)).then_inc(mask_in, 16)
                for b in range(NB):
                    if not first:
                        sp.wait_ge(ctx_split, NB * j - NB + b + 1)
                    sp.dma_start(ctxT[:, b], A["ctxT"][ds(j * NB + b, 1), :, :]
                                 .rearrange("a p n -> p (a n)").rearrange("p (k n) -> p k n", k=K)).then_inc(ctx_in[b], 16)
            loads(0, True)
            sp.dma_start(wo[:], A["wo"].rearrange("(k p) n -> p k n", p=P)).then_inc(wo_in, 16)
            sp.dma_start(bo[:], A["bo"].partition_broadcast(P)).then_inc(wo_in, 16)
            sp.wait_ge(zero_made, 1)
            for sent in core.sent:
                sp.dma_start(sent.rearrange("(t p) d -> p t d", p=P),
                             zero[:].unsqueeze(1).to_broadcast([P, ST + 1, D])).then_inc(rows_cleared, 16)
            with sp.Fori(1, T) as j:
                loads(j, False)
            sp.wait_ge(rows_cleared, 32)

        WEIGHTS = 16 * 12

        @block.gpsimd
        def _(pool):
            pool.memset(zero[:], 0.0).then_inc(zero_made, 1)
            pool.memset(mhalf[:], -0.5).then_inc(mhalf_set, 1)
            pool.wait_ge(mhalf_set, 1)

            def rsqrt(j):
                pool.drain()
                pool.wait_ge(var_ready, j + 1)
                pool.tensor_tensor(rstd[:], veps[:], mhalf[:], ALU.pow).then_inc(rstd_ready, 1)
            with pool.Fori(0, T) as j:
                rsqrt(j)

        @block.vector
        def _(dve):
            dve.wait_ge(weights_in, WEIGHTS)
            def norm(j):
                dve.drain()
                dve.bn_stats(stats[:], x[:, ds(j, 1), :].rearrange("p a d -> p (a d)"))
                dve.drain()
                dve.bn_aggr(mv[:], stats[:])
                dve.drain()
                dve.tensor_scalar(veps[:], mv[:, 1:2], EPS, None, ALU.add).then_inc(var_ready, 1)

            def normed(j):
                dve.drain()
                dve.wait_ge(rstd_ready, j + 1)
                dve.tensor_scalar(xn[:], x[:, ds(j, 1), :].rearrange("p a d -> p (a d)"), mv[:, 0:1],
                                  rstd[:, 0:1], ALU.subtract, ALU.mult).then_inc(xn_ready, 1)

            def spread_q(u):
                dve.drain()
                dve.wait_ge(t_ready, u)
                for h in range(NB):
                    rows = slice(S * h, S * h + S)
                    last = dve.tensor_tensor(
                        qbd[rows, :, :, h, :].rearrange("p b g q -> p g b q"),
                        TB[rows, 0, :].rearrange("p (g b q) -> p g b q", g=G, b=NB),
                        bq[rows, :].unsqueeze(2).unsqueeze(3).to_broadcast([S, G, NB, S]), ALU.add)
                last.then_inc(t_free[0], 1)

            def copy_v(i, p, kt):
                dve.wait_ge(kv_ready, 6 * i + G + kt + 1)
                dve.tensor_tensor(v[:, p, kt, :], KV[:, 1 + kt, :], bv[:], ALU.add).then_inc(v_ready, 1)

            def low_ctx(i, b):
                dve.wait_ge(ctx_high, i + 1)
                dve.tensor_tensor(ctxl[:, b % 2], ctxT[:, b], ctxh[:, b % 2].bitcast(F32), ALU.subtract).then_inc(ctx_split, 1)

            dve.sem_inc(masked, 1)
            dve.sem_inc(o_ready, 1)
            for n, (w, high, low) in enumerate(((wk, wkh, wkl), (wv, wvh, wvl))):
                dve.wait_ge(w_high, n + 1)
                dve.tensor_tensor(low[:], w, high[:].bitcast(F32), ALU.subtract).then_inc(w_split, 1)
            for b in range(2):
                low_ctx(b, b)
            dve.memset(qbd[:], 0.0)
            dve.memset(vlast[:], 0.0).then_inc(cleared, 1)
            norm(0)
            normed(0)
            dve.wait_ge(vlast_done, 1)
            for g in range(G):
                rows = slice(S * g, S * g + S)
                last = dve.tensor_tensor(vlast[rows, g, :], O[rows, 0, P * g:P * g + P], bv[rows, P * g:P * g + P], ALU.add)
            last.then_inc(vlast_ready, 1)
            spread_q(2)
            copy_v(0, 0, 0)
            copy_v(0, 0, 1)

            def tile(j, last):
                dve.drain()
                dve.wait_ge(mask_in, 16 * j + 16)
                dve.tensor_scalar(keep[:], maskt[:], 0, BIG, ALU.not_equal, ALU.mult).then_inc(keep_made, 1)
                dve.drain()
                dve.tensor_scalar(bound[:], keep[:], NEG, None, ALU.add).then_inc(bound_made, 1)
                for b in range(NB):
                    i = NB * j + b
                    for hf in range(2):
                        groups = slice(2 * hf, 2 * hf + 2)
                        dve.drain()
                        dve.wait_ge(scores_ready, 2 * i + hf + 1)
                        dve.scalar_tensor_tensor(sm[:, b % 2, groups, :], SC[:, :, 0:SK], float(DH) ** -0.5,
                                                 bound[:, b:b + 1, :].to_broadcast([P, 2, SK]), ALU.mult, ALU.min)\
                           .then_inc(masked, 1)
                        dve.drain()
                        dve.tensor_reduce(nmax[:, b % 2, groups], sm[:, b % 2, groups, :], X, ALU.max, negate=True)\
                           .then_inc(max_ready, 1)
                    if b == NB - 1 and not last:
                        spread_q(USES * j + FIRST_USES + Q_USE + 1)
                    dve.drain()
                    dve.wait_ge(exp_done, 2 * i + 2)
                    dve.tensor_tensor(plast[:], tab("one_at")[:, ds(i, 32)].unsqueeze(1).to_broadcast([P, G, 32]),
                                      sm[:, b % 2, :, SK - 1:SK].to_broadcast([P, G, 32]), ALU.mult).then_inc(plast_ready, 1)
                    dve.reciprocal(rinv[:, b % 2, :], rsum[:, b % 2, :])
                    if not (last and b == NB - 1):
                        copy_v(i + 1, (b + 1) % 2, 0)
                        copy_v(i + 1, (b + 1) % 2, 1)
                    if not (last and b + 2 >= NB):
                        low_ctx(i + 2, (b + 2) % NB)
                    if b == 0 and not last:
                        norm(j + 1)
                    if b == 1 and not last:
                        normed(j + 1)
                    dve.drain()
                    dve.wait_ge(pv_ready, i + 1)
                    if b == 0:
                        dve.wait_ge(t_ready, USES * j + 1)
                    for h in range(NB):
                        rows = slice(S * h, S * h + S)
                        op = dve.tensor_tensor(o[S * b:S * b + S, :].rearrange("p (g c) -> p g c", g=G)[:, :, S * h:S * h + S],
                                               O[rows, 0, :].rearrange("p (g c) -> p g c", g=G)[:, :, S * h:S * h + S],
                                               rinv[rows, b % 2, :].unsqueeze(2).to_broadcast([S, G, S]), ALU.mult)
                    op.then_inc(o_ready, 1)
                dve.drain()
                dve.wait_ge(t_ready, USES * j + FIRST_USES + use(OUT_USE, last) + 1)
                xt = x[:, ds(j, 1), :].rearrange("p a d -> p (a d)")
                dve.tensor_tensor(xt, xt, TB[:, 1, :], ALU.add).then_inc(t_free[1], 1)
                dve.drain()
                dve.wait_ge(wo_in, 32)
                dve.tensor_tensor(xt, xt, bo[:], ALU.add)

            with dve.Fori(0, T - 1) as j:
                tile(j, False)
            tile(T - 1, True)

        @block.scalar
        def _(act):
            act.wait_ge(weights_in, WEIGHTS)
            def copy_k(i, p, g):
                act.wait_ge(kv_ready, 6 * i + g + 1)
                act.activation(kT[:, p, g, :], KV[:, g % 3, 0:SK], ACT.Identity, bias=bk[:, g:g + 1]).then_inc(kT_ready, 1)

            def copy_t(out, u, bank):
                act.wait_ge(t_ready, u)
                act.activation(out, TB[:, bank, 0:out.free_size()], ACT.Copy).then_inc(t_free[bank], 1)

            def high_ctx(i, b, j, first=False):
                act.wait_ge(ctx_in[b], 16 * j + 16)
                if not first:
                    act.wait_ge(kv_ready, 6 * i - 6)
                act.activation(ctxh[:, b % 2], ctxT[:, b], ACT.Copy).then_inc(ctx_high, 1)

            for w, high in ((wk, wkh), (wv, wvh)):
                act.activation(high[:], w, ACT.Copy).then_inc(w_high, 1)
            for b in range(2):
                high_ctx(b, b, 0, first=True)
            copy_t(xT[:].rearrange("p k n -> p (k n)"), 1, 1)
            for g in range(G):
                copy_k(0, 0, g)

            def tile(j, last):
                for b in range(NB):
                    i = NB * j + b
                    for hf in range(2):
                        if not (last and b == NB - 1):
                            copy_k(i + 1, (b + 1) % 2, 2 * hf)
                            copy_k(i + 1, (b + 1) % 2, 2 * hf + 1)
                        act.wait_ge(max_ready, 2 * i + hf + 1)
                        for g in range(2 * hf, 2 * hf + 2):
                            op = act.activation(sm[:, b % 2, g, :], sm[:, b % 2, g, :], ACT.Exp,
                                                bias=nmax[:, b % 2, g:g + 1], accum_out=rsum[:, b % 2, g:g + 1])
                        op.then_inc(exp_done, 1)
                    if not (last and b + 2 >= NB):
                        high_ctx(i + 2, (b + 2) % NB, j + (b + 2) // NB)
                    n = use(PT_USE[b], last)
                    for c in range(2):
                        copy_t(pT[:, 4 * c:4 * c + 4, :].rearrange("p a n -> p (a n)"),
                               USES * j + FIRST_USES + n + c + 1, (n + c) % 2)
                    copy_t(plastT[:], USES * j + FIRST_USES + n + 3, n % 2)
                    if b == 2 and not last:
                        copy_t(xT[:].rearrange("p k n -> p (k n)"), USES * j + FIRST_USES + XT_USE + 1, 1)
                copy_t(oT[:].rearrange("p k n -> p (k n)"), USES * j + FIRST_USES + use(OT_USE, last) + 1, 0)

            with act.Fori(0, T - 1) as j:
                tile(j, False)
            tile(T - 1, True)

        @block.tensor
        def _(pe):
            pe.wait_ge(weights_in, WEIGHTS)
            def free(bank, v):
                pe.wait_ge(t_free[bank], v)

            def make_xT(j):
                pe.wait_ge(xn_ready, j + 1)
                for k in range(K):
                    op = pe.transpose(TB[:, 1, P * k:P * k + P], xn[:, P * k:P * k + P], tab("ident"))
                op.then_inc(t_ready, 1)

            def make_q(v):
                free(1, v)
                for g in range(G):
                    for k in range(K):
                        op = pe.matmul(TB[:, 0, P * g:P * g + P], wq[:, k, P * g:P * g + P], xT[:, k, :],
                                       start=(k == 0), stop=(k == K - 1))
                op.then_inc(t_ready, 1)

            def make_k(i, b, g, first=False):
                if g == 0:
                    pe.wait_ge(ctx_split, i + 1)
                    if not first:
                        pe.wait_ge(kT_ready, 4 * i)
                if g == 1 and not first:
                    pe.wait_ge(v_ready, 2 * i - 1)
                if g == 2 and not first:
                    pe.wait_ge(v_ready, 2 * i)
                if g == 3:
                    pe.wait_ge(kT_ready, 4 * i + 1)
                for k in range(K):
                    op = passes(pe, KV[:, g % 3, 0:SKP], [w[:, k, P * g:P * g + P] for w in (wkh, wkl)],
                                [c[:, b % 2, k, :] for c in (ctxh, ctxl)], k == 0, k == K - 1)
                op.then_inc(kv_ready, 1)

            def make_v(i, b, kt):
                pe.wait_ge(kT_ready, 4 * i + 2 + kt)
                for k in range(K):
                    op = passes(pe, KV[:, 1 + kt, :], [c[:, b % 2, k, P * kt:P * kt + P] for c in (ctxh, ctxl)],
                                [w[:, k, :] for w in (wvh, wvl)], k == 0, k == K - 1)
                op.then_inc(kv_ready, 1)

            def scores(i, b, hf):
                pe.wait_ge(kT_ready, 4 * i + 2 * hf + 2)
                pe.wait_ge(masked, 2 * i + hf + 1)
                for g in range(2 * hf, 2 * hf + 2):
                    op = pe.matmul(SC[:, g % 2, 0:SK], qbd[:, b, g].rearrange("p h q -> p (h q)"), kT[:, b % 2, g, :],
                                   start=True, stop=True)
                op.then_inc(scores_ready, 1)

            for k in range(K):
                op = pe.matmul(O[:, 0, :], lastT[:, k].rearrange("p r b -> p (r b)"), wv[:, k, :], start=(k == 0), stop=(k == K - 1))
            op.then_inc(vlast_done, 1)
            make_xT(0)
            make_q(1)
            pe.wait_ge(t_free[0], 1)
            pe.wait_ge(w_split, 2)
            for g in range(G):
                make_k(0, 0, g, first=True)
            make_v(0, 0, 0)
            make_v(0, 0, 1)

            def tile(j, last):
                base = USES // 2 * j + 1
                for b in range(NB):
                    i = NB * j + b
                    nb = (b + 1) % NB
                    more = not (last and b == NB - 1)
                    if b == NB - 1 and not last:
                        free(0, base + Q_USE // 2)
                        make_q(base + XT_USE // 2 + 1)
                    scores(i, b, 0)
                    if more:
                        make_k(i + 1, nb, 0)
                        make_k(i + 1, nb, 1)
                    scores(i, b, 1)
                    if more:
                        make_k(i + 1, nb, 2)
                        make_k(i + 1, nb, 3)
                        make_v(i + 1, nb, 0)
                        make_v(i + 1, nb, 1)
                    n = use(PT_USE[b], last)
                    pe.wait_ge(exp_done, 2 * i + 2)
                    for c in range(2):
                        free((n + c) % 2, base + (n + c) // 2)
                        for m in range(4):
                            g, kt = 2 * c + m // 2, m % 2
                            op = pe.transpose(TB[:, (n + c) % 2, P * m:P * m + P], sm[:, b % 2, g, P * kt:P * kt + P], tab("ident"))
                        op.then_inc(t_ready, 1)
                    pe.wait_ge(plast_ready, i + 1)
                    free(n % 2, base + (n + 2) // 2)
                    pe.transpose(TB[:, n % 2, 0:P], plast[:].rearrange("p g n -> p (g n)"), tab("ident")).then_inc(t_ready, 1)
                    pe.wait_ge(v_ready, 2 * i + 2)
                    pe.wait_ge(vlast_ready, 1)
                    pe.wait_ge(o_ready, i + 1)
                    free(n % 2, base + (n + 2) // 2 + 1)
                    free((n + 1) % 2, base + (n + 1) // 2 + 1)
                    for g in range(G):
                        for kt in range(2):
                            pe.matmul(O[:, 0, P * g:P * g + P], pT[:, 2 * g + kt, :], v[:, b % 2, kt, P * g:P * g + P],
                                      start=(g == 0 and kt == 0), stop=False, skip_group_check=True)
                    op = pe.matmul(O[:, 0, :], plastT[:], vlast[:].rearrange("p g n -> p (g n)"),
                                   start=False, stop=True, skip_group_check=True)
                    op.then_inc(pv_ready, 1)
                    if b == 2 and not last:
                        free(1, base + XT_USE // 2)
                        make_xT(j + 1)
                n = use(OT_USE, last)
                pe.wait_ge(o_ready, NB * j + NB + 1)
                free(0, base + n // 2)
                for k in range(K):
                    op = pe.transpose(TB[:, 0, P * k:P * k + P], o[:, P * k:P * k + P], tab("ident"))
                op.then_inc(t_ready, 1)
                free(1, base + n // 2)
                free(0, base + n // 2 + 1)
                pe.wait_ge(wo_in, 32)
                for k in range(K):
                    op = pe.matmul(TB[:, 1, :], oT[:, k, :], wo[:, k, :], start=(k == 0), stop=(k == K - 1))
                op.then_inc(t_ready, 1)

            with pe.Fori(0, T - 1) as j:
                tile(j, False)
            tile(T - 1, True)


def phase_self0(nc, core):
    A, x, tab = core.A, core.x, core.tab
    with ExitStack() as ctx:
        sb = lambda name, shape, dt=F32: ctx.enter_context(nc.sbuf_tensor("s0_" + name, shape, dt))
        sem = semaphores(nc, ctx, "s0_")
        sems = lambda name: [sem(f"{name}{s}") for s in range(2)]
        LC = 3 * LAT

        wqkv = sb("wqkv", [P, K, 3 * D])
        latw = sb("latw", [P, K, LC])
        latb = sb("latb", [P, LC])
        latow = sb("latow", [P, 2, D])
        latob = sb("latob", [P, D])
        rw = sb("rw", [P, K, E])
        rb = sb("rb", [P, E])
        two = lambda name, shape: [sb(f"{name}{s}", shape) for s in range(2)]
        stats, mv, veps, rstd = two("stats", [P, 6]), two("mv", [P, 2]), two("veps", [P, 1]), two("rstd", [P, 1])
        mhalf = sb("mhalf", [P, 1])
        xn, xT = two("xn", [P, D]), two("xT", [P, K, P])
        qT, kT, kn, vn = two("qT", [P, H, 32]), two("kT", [P, LAT]), two("kn", [P, D]), two("vn", [P, D])
        qpad = two("qpad", [P, H, 32])
        sm, pT = two("sm", [P, H, S]), two("pT", [P, H, S])
        nm, rs, ri = two("nm", [P, H]), two("rs", [P, H]), two("ri", [P, H])
        ao, aoT = two("ao", [P, LAT]), two("aoT", [P, 2, P])
        lg, lmax, lsum, linv = two("lg", [P, E]), two("lmax", [P, 1]), two("lsum", [P, 1]), two("linv", [P, 1])

        R = [[ctx.enter_context(nc.psum_tensor(f"s0_R{s}{k}", [P, 512], F32)) for k in range(2)] for s in range(2)]
        AT = ctx.enter_context(nc.psum_tensor("s0_AT", [P, 4, 512], F32))

        weights_in = sem("weights_in")
        WEIGHTS = 16 * 7
        mhalf_set, qpad_zero = sem("mhalf_set"), sem("qpad_zero")
        var_ready, rstd_ready, xn_ready = sems("var_ready"), sems("rstd_ready"), sems("xn_ready")
        r_ready = sems("r_ready")
        r_free = [sems(f"r_free{s}_") for s in range(2)]
        qT_ready, kv_ready = sems("qT_ready"), sems("kv_ready")
        heads_begun = sem("heads_begun")
        at_ready, at_free = sem("at_ready"), sem("at_free")
        raw_ready = sems("raw_ready")
        shifted, exp_done, pT_ready = sems("shifted"), sems("exp_done"), sems("pT_ready")
        ao_ready = sems("ao_ready")
        rows_kept = sems("rows_kept")
        lshift, lexp = sems("lshift"), sems("lexp")

        XT0, UQ, UK, UV, XT1, ULQK, ULV, UAO, UO, XT2, ULOG = range(11)
        USES, READS = 11, 5
        SCORE0, PV0, SCORE1, PV1 = range(4)

        block = ctx.enter_context(nc.Block())

        def ready(eng, s, it, n):
            eng.wait_ge(r_ready[s], USES * it + n + 1)

        def at_use(it, n, s):
            return 8 * it + 2 * n + s

        def AT_of(n, s):
            return AT[:, (2 * n + s) % 4, :]

        @block.sync
        def _(sp):
            for t, a in ((wqkv, "wqkv"), (latw, "lat_w"), (latow, "lat_ow"), (rw, "rw0")):
                sp.dma_start(t[:], A[a].rearrange("(k p) n -> p k n", p=P)).then_inc(weights_in, 16)
            for t, a in ((latb, "lat_b"), (latob, "lat_ob"), (rb, "rb0")):
                sp.dma_start(t[:], A[a].partition_broadcast(P)).then_inc(weights_in, 16)

        @block.gpsimd
        def _(pool):
            pool.memset(mhalf[:], -0.5).then_inc(mhalf_set, 1)
            pool.wait_ge(mhalf_set, 1)

            def rsqrt(n):
                for s in range(2):
                    pool.drain()
                    pool.wait_ge(var_ready[s], n)
                    pool.tensor_tensor(rstd[s][:], veps[s][:], mhalf[:], ALU.pow).then_inc(rstd_ready[s], 1)
            for kept in rows_kept:
                pool.sem_inc(kept, 1)
            with pool.Fori(0, T // 2) as it:
                rsqrt(2 * it + 1)
                rsqrt(2 * it + 2)
                for s in range(2):
                    pool.wait_ge(xn_ready[s], 3 * it + 3)
                    pool.wait_ge(mhalf_set, 1)
                    pool.tensor_copy(core.rows[:, ds(2 * it + s, 1), :].rearrange("p a d -> p (a d)"), xn[s][:])\
                        .then_inc(rows_kept[s], 1)

        @block.vector
        def _(dve):
            dve.wait_ge(weights_in, WEIGHTS)
            def tile(it, s):
                return x[:, ds(2 * it + s, 1), :].rearrange("p a d -> p (a d)")

            def norm(it, k):
                for s in range(2):
                    dve.drain()
                    dve.bn_stats(stats[s][:], tile(it, s))
                for s in range(2):
                    dve.drain()
                    dve.bn_aggr(mv[s][:], stats[s][:])
                for s in range(2):
                    dve.drain()
                    dve.tensor_scalar(veps[s][:], mv[s][:, 1:2], EPS, None, ALU.add).then_inc(var_ready[s], 1)
                for s in range(2):
                    dve.wait_ge(rstd_ready[s], 2 * it + k + 1)
                    if k == 0:
                        dve.wait_ge(rows_kept[s], it + 1)
                    if k > 0:
                        ready(dve, s, it, XT0)
                    dve.tensor_scalar(xn[s][:], tile(it, s), mv[s][:, 0:1], rstd[s][:, 0:1],
                                      ALU.subtract, ALU.mult).then_inc(xn_ready[s], 1)

            def softmax(it, k):
                for s in range(2):
                    if k == 1:
                        dve.wait_ge(raw_ready[s], it + 1)
                    dve.tensor_reduce(nm[s][:], sm[s][:], X, ALU.max, negate=True)
                for s in range(2):
                    dve.drain()
                    dve.tensor_tensor(sm[s][:], sm[s][:], nm[s][:].unsqueeze(2).to_broadcast([P, H, S]), ALU.add)\
                       .then_inc(shifted[s], 1)
                for s in range(2):
                    dve.drain()
                    dve.wait_ge(exp_done[s], 2 * it + k + 1)
                    dve.tensor_reduce(rs[s][:], sm[s][:], X, ALU.add)
                    dve.drain()
                    dve.reciprocal(ri[s][:], rs[s][:])
                    dve.drain()
                    dve.tensor_tensor(sm[s][:], sm[s][:], ri[s][:].unsqueeze(2).to_broadcast([P, H, S]), ALU.mult)
                    dve.drain()
                    dve.transpose(pT[s][:].rearrange("p h q -> p (h q)"), sm[s][:].rearrange("p h q -> p (h q)")).then_inc(pT_ready[s], 1)

            for s in range(2):
                last = dve.memset(qpad[s][:], 0.0)
            last.then_inc(qpad_zero, 1)
            for free in r_free[0] + r_free[1]:
                dve.sem_inc(free, 1)
            dve.sem_inc(at_free, 4)
            with dve.Fori(0, T // 2) as it:
                norm(it, 0)
                for s in range(2):
                    dve.drain()
                    ready(dve, s, it, UQ)
                    dve.transpose(qT[s][:].rearrange("p h q -> p (h q)"), R[s][UQ % 2][:]).then_inc(r_free[s][UQ % 2], 1)
                for s in range(2):
                    dve.wait_ge(at_ready, at_use(it, SCORE0, s) + 1)
                    dve.tensor_tensor(sm[s][:], AT_of(SCORE0, s).rearrange("p (h k) -> p h k", h=H),
                                      tab("tril").unsqueeze(1).to_broadcast([P, H, S]), ALU.mult).then_inc(at_free, 1)
                for s in range(2):
                    dve.drain()
                    dve.tensor_tensor(sm[s][:], sm[s][:], tab("untril").unsqueeze(1).to_broadcast([P, H, S]), ALU.add)
                dve.drain()
                softmax(it, 0)
                for s in range(2):
                    dve.drain()
                    dve.wait_ge(at_ready, at_use(it, PV0, s) + 1)
                    dve.tensor_tensor(tile(it, s), tile(it, s), AT_of(PV0, s), ALU.add).then_inc(at_free, 1)
                norm(it, 1)
                for s in range(2):
                    dve.drain()
                    dve.tensor_tensor(tile(it, s), tile(it, s), xn[s][:], ALU.add)
                for s in range(2):
                    ready(dve, s, it, ULQK)
                    q = R[s][ULQK % 2][:, 0:LAT].rearrange("p (h e k) -> p h e k", e=2, k=KPH)
                    bias = latb[:, 0:LAT].rearrange("p (h e k) -> p h e k", e=2, k=KPH)
                    pad = qpad[s][:].rearrange("p (h e) k -> p h e k", e=2)
                    for e in range(2):
                        dve.tensor_tensor(pad[:, :, e, KPH * e:KPH * e + KPH], q[:, :, e, :], bias[:, :, e, :], ALU.add)
                    dve.tensor_tensor(kn[s][:, 0:LAT], R[s][ULQK % 2][:, LAT:2 * LAT], latb[:, LAT:2 * LAT], ALU.add)\
                       .then_inc(r_free[s][ULQK % 2], 1)
                    dve.drain()
                    dve.transpose(qT[s][:].rearrange("p h q -> p (h q)"), qpad[s][:].rearrange("p h q -> p (h q)"))
                    dve.transpose(kT[s][:], kn[s][:, 0:LAT]).then_inc(qT_ready[s], 1)
                    ready(dve, s, it, ULV)
                    dve.tensor_tensor(vn[s][:, 0:LAT], R[s][ULV % 2][:, 0:LAT], latb[:, 2 * LAT:LC], ALU.add)\
                       .then_inc(r_free[s][ULV % 2], 1)
                softmax(it, 1)
                for s in range(2):
                    dve.drain()
                    dve.wait_ge(at_ready, at_use(it, PV1, s) + 1)
                    dve.tensor_copy(ao[s][:], AT_of(PV1, s)[:, 0:LAT]).then_inc(at_free, 1)
                    dve.drain()
                    dve.sem_inc(ao_ready[s], 1)
                for s in range(2):
                    ready(dve, s, it, UO)
                    dve.tensor_tensor(xn[s][:], R[s][UO % 2][:], latob[:], ALU.add).then_inc(xn_ready[s], 1)
                for s in range(2):
                    dve.drain()
                    ready(dve, s, it, ULOG)
                    dve.tensor_tensor(lg[s][:], R[s][ULOG % 2][:, 0:E], rb[:], ALU.add).then_inc(r_free[s][ULOG % 2], 1)
                    dve.drain()
                    dve.tensor_reduce(lmax[s][:], lg[s][:], X, ALU.max, negate=True).then_inc(lshift[s], 1)
                for s in range(2):
                    dve.drain()
                    dve.wait_ge(lexp[s], it + 1)
                    dve.reciprocal(linv[s][:], lsum[s][:])
                    dve.drain()
                    dve.tensor_scalar(core.probs[:, ds(2 * it + s, 1), :].rearrange("p a e -> p (a e)"), lg[s][:],
                                      linv[s][:, 0:1], None, ALU.mult)

        @block.scalar
        def _(act):
            act.wait_ge(weights_in, WEIGHTS)
            def copy(s, it, n, out, w, free=True, done=None):
                ready(act, s, it, n)
                act.activation(out, R[s][n % 2][:, 0:w], ACT.Copy).then_inc(r_free[s][n % 2], 1)

            def exps(it, k):
                for s in range(2):
                    act.wait_ge(shifted[s], 2 * it + k + 1)
                    act.activation(sm[s][:], sm[s][:], ACT.Exp).then_inc(exp_done[s], 1)

            with act.Fori(0, T // 2) as it:
                for s in range(2):
                    copy(s, it, XT0, xT[s][:].rearrange("p k n -> p (k n)"), D)
                for s in range(2):
                    copy(s, it, UK, kn[s][:], D)
                    copy(s, it, UV, vn[s][:], D)
                exps(it, 0)
                for s in range(2):
                    copy(s, it, XT1, xT[s][:].rearrange("p k n -> p (k n)"), D)
                for s in range(2):
                    act.wait_ge(at_ready, at_use(it, SCORE1, s) + 1)
                    act.activation(sm[s][:], AT_of(SCORE1, s).rearrange("p (h k) -> p h k", h=H), ACT.Copy,
                                   scale=float(KPH) ** -0.5).then_inc(at_free, 1)
                    act.drain()
                    act.sem_inc(raw_ready[s], 1)
                exps(it, 1)
                for s in range(2):
                    copy(s, it, UAO, aoT[s][:].rearrange("p k n -> p (k n)"), LAT)
                for s in range(2):
                    copy(s, it, XT2, xT[s][:].rearrange("p k n -> p (k n)"), D)
                for s in range(2):
                    act.wait_ge(lshift[s], it + 1)
                    act.activation(lg[s][:], lg[s][:], ACT.Exp, bias=lmax[s][:, 0:1], accum_out=lsum[s][:]).then_inc(lexp[s], 1)

        @block.tensor
        def _(pe):
            pe.wait_ge(weights_in, WEIGHTS)
            def free(s, it, n):
                pe.wait_ge(r_free[s][n % 2], READS * it + n // 2 - (n == ULOG) + 1)

            def read(s, it, n):
                pe.wait_ge(r_free[s][n % 2], READS * it + n // 2 - (n == ULOG) + 2)

            def transposes(s, it, n, src, count):
                free(s, it, n)
                for k in range(count):
                    op = pe.transpose(R[s][n % 2][:, P * k:P * k + P], src[:, P * k:P * k + P], tab("ident"))
                op.then_inc(r_ready[s], 1)

            def product(s, it, n, lhs, rhs, w):
                free(s, it, n)
                for k in range(len(lhs)):
                    op = pe.matmul(R[s][n % 2][:, 0:w], lhs[k], rhs[k], start=(k == 0), stop=(k == len(lhs) - 1))
                op.then_inc(r_ready[s], 1)

            def heads(it, n, s, lhs, rhs, w):
                pe.wait_ge(at_free, at_use(it, n, s) + 1)
                pe.sem_inc(heads_begun, 1)
                for h in range(H):
                    for b in range(NB):
                        rows = slice(S * b, S * b + S)
                        op = pe.matmul(AT_of(n, s)[rows, w * h:w * h + w], lhs(rows, h), rhs(rows, h), start=(h == 0), stop=(h == H - 1),
                                       skip_group_check=True)
                op.then_inc(at_ready, 1)

            with pe.Fori(0, T // 2) as it:
                for s in range(2):
                    pe.wait_ge(xn_ready[s], 3 * it + 1)
                    transposes(s, it, XT0, xn[s], K)
                for s in range(2):
                    read(s, it, XT0)
                    for n, c in ((UQ, 0), (UK, 1), (UV, 2)):
                        product(s, it, n, [xT[s][:, k, :] for k in range(K)],
                                [wqkv[:, k, D * c:D * c + D] for k in range(K)], D)
                for s in range(2):
                    read(s, it, UQ)
                    read(s, it, UK)
                    heads(it, SCORE0, s, lambda r, h: qT[s][r, h, :], lambda r, h: kn[s][r, 32 * h:32 * h + 32], 32)
                for s in range(2):
                    read(s, it, UV)
                    pe.wait_ge(pT_ready[s], 2 * it + 1)
                    heads(it, PV0, s, lambda r, h: pT[s][r, h, :], lambda r, h: vn[s][r, 32 * h:32 * h + 32], 32)
                for s in range(2):
                    pe.wait_ge(xn_ready[s], 3 * it + 2)
                    transposes(s, it, XT1, xn[s], K)
                for s in range(2):
                    read(s, it, XT1)
                    for n, c, w in ((ULQK, 0, 2 * LAT), (ULV, 2 * LAT, LAT)):
                        product(s, it, n, [xT[s][:, k, :] for k in range(K)],
                                [latw[:, k, c:c + w] for k in range(K)], w)
                for s in range(2):
                    pe.wait_ge(qT_ready[s], it + 1)
                    heads(it, SCORE1, s, lambda r, h: qT[s][r, h, :], lambda r, h: kT[s][r, 32 * (h // 2):32 * (h // 2) + 32], 32)
                for s in range(2):
                    read(s, it, ULV)
                    pe.wait_ge(pT_ready[s], 2 * it + 2)
                    heads(it, PV1, s, lambda r, h: pT[s][r, h, :], lambda r, h: vn[s][r, KPH * h:KPH * h + KPH], KPH)
                for s in range(2):
                    pe.wait_ge(ao_ready[s], it + 1)
                    transposes(s, it, UAO, ao[s], 2)
                for s in range(2):
                    read(s, it, UAO)
                    product(s, it, UO, [aoT[s][:, k, :] for k in range(2)], [latow[:, k, :] for k in range(2)], D)
                for s in range(2):
                    pe.wait_ge(xn_ready[s], 3 * it + 3)
                    transposes(s, it, XT2, xn[s], K)
                for s in range(2):
                    read(s, it, XT2)
                    product(s, it, ULOG, [xT[s][:, k, :] for k in range(K)], [rw[:, k, :] for k in range(K)], E)


def phase_mixture(nc, core, n, F, biased, eps, scale):
    A, tab, probs, x = core.A, core.tab, core.probs, core.x
    TE = T * E
    NF, NC = F // P, F // 512
    HALF = 2
    PIECES = 2 * NC * HALF
    RING = 4
    w1d, w2d = A[f"w1_{n}"], A[f"w2_{n}"]
    with ExitStack() as ctx:
        sb = lambda name, shape, dt=F32: ctx.enter_context(nc.sbuf_tensor(f"x{n}_{name}", shape, dt))
        sem = semaphores(nc, ctx, f"x{n}_")
        psum = lambda name, banks: ctx.enter_context(nc.psum_tensor(f"x{n}_{name}", [P, banks, 512], F32))
        top, idx = sb("top", [P, T, E]), sb("idx", [P, T, E], U32)
        idxf = sb("idxf", [P, T, 2])
        pick = sb("pick", [P, 2, T, E])
        both = sb("both", [P, T, E])
        wsum, winv = sb("wsum", [P, T]), sb("winv", [P, T])
        off = sb("off", [P, T + 1, E])
        over = sb("over", [P, E, E])
        tiles = sb("tiles", [P, E])
        upto, first = sb("upto", [P, E]), sb("first", [P, E])
        pos, posk = sb("pos", [P, T, E]), sb("posk", [P, T, E])
        slotf = sb("slotf", [P, 2, T])
        cmp = sb("cmp", [1, ST, E])
        owner = sb("owner", [1, ST])
        if biased:
            b1 = sb("b1", [P, E, NF])
            b2 = sb("b2", [E, D])
            mix = sb("mix", [P, T, E])
            mixT = sb("mixT", [E, T, P])
        w1h, w1l = sb("w1h", [P, K, F], F32R), sb("w1l", [P, K, F], F32R)
        w2h, w2l = sb("w2h", [P, NF, D], F32R), sb("w2l", [P, NF, D], F32R)
        stage = sb("stage", [P, RING, HALF, 512])
        xh, xl = sb("xh", [P, K, P], F32R), sb("xl", [P, K, P], F32R)
        hh, hl = sb("hh", [P, NF, P], F32R), sb("hl", [P, NF, P], F32R)
        h = [core.rows[:, c, :] for c in range(2)]
        g = [core.rows[:, 2 + c, :] for c in range(2)]
        xf, xg, y = (core.rows[:, c, :] for c in (4, 5, 6))

        RP, HP, TP, XP, YP = psum("RP", 2), psum("HP", 2), psum("TP", 2), psum("XP", 1), psum("YP", 1)

        picked, counted, routed, sent = sem("picked"), sem("counted"), sem("routed"), sem("sent")
        bias_in, mixed, mixT_made, mixT_copied, b2_made, b2_added = (
            sem(a) for a in ("bias_in", "mixed", "mixT_made", "mixT_copied", "b2_made", "b2_added"))
        piece_in = [sem(f"piece_in{r}") for r in range(RING)]
        split = sem("split")
        rows_in, xT_made, xh_made, xl_made = sem("rows_in"), sem("xT_made"), sem("xh_made"), sem("xl_made")
        xf_made = sem("xf_made")
        h_made = sem("h_made")
        h_copied, hT_made, g_made, hh_made, hl_made = (sem(a) for a in ("h_copied", "hT_made", "g_made", "hh_made", "hl_made"))
        y_part = sem("y_part")
        y_copied, y_stored = sem("y_copied"), sem("y_stored")
        come = [sem(f"come{r}") for r in range(2 * RING)]
        weighed = sem("weighed")

        block = ctx.enter_context(nc.Block())

        def peel(eng, step):
            step(0, True, False)
            with eng.Fori(1, ST - 1) as m:
                step(m, False, False)
            step(ST - 1, False, True)

        def piece(q):
            chunk = q // HALF % NC
            half = q % HALF * (4 // HALF)
            return q < NC * HALF, chunk, half

        @block.sync
        def _(sp):
            if biased:
                sp.dma_start(b1[:], A["b1T"]).then_inc(bias_in, 16)
                sp.dma_start(b2[:], A["b2_0"]).then_inc(bias_in, 16)

            def loads(e, first):
                for q in range(PIECES):
                    if not (first and q < RING):
                        sp.wait_ge(split, PIECES * e + q - RING + 1)
                    is_w1, c, k = piece(q)
                    if is_w1:
                        src = w1d[ds(e, 1)].rearrange("a (k p) f -> p (a k) f", p=P)[:, k:k + 2, 512 * c:512 * c + 512]
                    else:
                        src = w2d[ds(e, 1)].rearrange("a (k p) d -> p (a k) d", p=P)[:, 4 * c + k:4 * c + k + 2, :]
                    sp.dma_start(stage[:, q % RING], src).then_inc(piece_in[q % RING], 16)
            loads(0, True)
            with sp.Fori(1, E) as e:
                loads(e, False)

        @block.vector
        def _(dve):
            for t in range(T):
                dve.max(top[:, t, :], probs[:, t, :])
            dve.drain()
            for t in range(T):
                dve.max_index(idx[:, t, :], top[:, t, :], probs[:, t, :])
            dve.drain()
            dve.tensor_copy(idxf[:], idx[:, :, 0:2])
            dve.tensor_tensor(wsum[:], top[:, :, 0], top[:, :, 1], ALU.add)
            dve.drain()
            if eps:
                dve.tensor_scalar(wsum[:], wsum[:], eps, None, ALU.add)
                dve.drain()
            dve.reciprocal(winv[:], wsum[:])
            for k in range(2):
                dve.tensor_tensor(pick[:, k], tab("expert_id").unsqueeze(1).to_broadcast([P, T, E]),
                                  idxf[:, :, k:k + 1].to_broadcast([P, T, E]), ALU.is_equal)
            dve.drain()
            dve.tensor_tensor(both[:], pick[:, 0], pick[:, 1], ALU.add).then_inc(picked, 1)
            dve.tensor_tensor(core.gate[:], top[:, :, 0:2], winv[:].unsqueeze(2).to_broadcast([P, T, 2]), ALU.mult)
            if scale != 1.0:
                dve.drain()
                dve.tensor_scalar(core.gate[:], core.gate[:], scale, None, ALU.mult)
            dve.memset(off[:, 0, :], 0.0)
            dve.wait_ge(counted, 1)
            for t in range(T):
                dve.drain()
                dve.tensor_tensor(off[:, t + 1, :], off[:, t, :], RP[:, 1, E * t:E * t + E], ALU.add)
            dve.drain()
            dve.tensor_tensor(over[:], off[:, T, :].unsqueeze(2).to_broadcast([P, E, E]),
                              tab("step128").unsqueeze(1).to_broadcast([P, E, E]), ALU.is_gt)
            dve.tensor_tensor(pos[:], off[:, 0:T, :], RP[:, 0, 0:TE].rearrange("p (t e) -> p t e", e=E), ALU.add)
            dve.drain()
            dve.tensor_reduce(tiles[:], over[:], X, ALU.add)
            dve.drain()
            dve.tensor_tensor(over[:], tab("upto").rearrange("p (a b) -> p a b", a=E),
                              tiles[:].unsqueeze(1).to_broadcast([P, E, E]), ALU.mult)
            dve.drain()
            dve.tensor_reduce(upto[:], over[:], X, ALU.add)
            dve.drain()
            dve.tensor_tensor(first[:], upto[:], tiles[:], ALU.subtract)
            dve.tensor_tensor(cmp[:], upto[0:1, :].unsqueeze(1).to_broadcast([1, ST, E]),
                              tab("tile_id")[0:1, :].unsqueeze(2).to_broadcast([1, ST, E]), ALU.is_le)
            dve.drain()
            dve.tensor_reduce(owner[:], cmp[:], X, ALU.add)
            dve.tensor_copy(core.tiles_before[:], first[0:1, :])
            dve.drain()
            dve.tensor_scalar(first[:], first[:], float(P), None, ALU.mult)
            dve.tensor_scalar(core.expert_of[:], owner[:], float(E - 1), None, ALU.min)
            dve.drain()
            dve.tensor_tensor(pos[:], pos[:], first[:].unsqueeze(1).to_broadcast([P, T, E]), ALU.add)
            for k in range(2):
                dve.drain()
                dve.tensor_tensor(posk[:], pos[:], pick[:, k], ALU.mult)
                dve.drain()
                dve.tensor_reduce(slotf[:, k, :], posk[:], X, ALU.add)
            dve.drain()
            dve.tensor_copy(core.slot[:], slotf[:]).then_inc(routed, 1)
            if biased:
                for k in range(2):
                    dve.tensor_tensor(pick[:, k], pick[:, k], core.gate[:, :, k:k + 1].to_broadcast([P, T, E]), ALU.mult)
                dve.drain()
                dve.tensor_tensor(mix[:], pick[:, 0], pick[:, 1], ALU.add).then_inc(mixed, 1)
                for c in range(2):
                    dve.wait_ge(mixT_made, c + 1)
                    dve.tensor_copy(mixT[:, 4 * c:4 * c + 4, :].rearrange("p t n -> p (t n)"), TP[0:E, c, :]).then_inc(mixT_copied, 1)
                for t in range(T):
                    dve.drain()
                    dve.wait_ge(b2_made, t + 1)
                    dve.tensor_tensor(x[:, t, :], x[:, t, :], RP[:, t % 2, :], ALU.add).then_inc(b2_added, 1)

            def splits(e, first):
                if not first:
                    before = dve.value_load(core.tiles_before[0:1, ds(e, 1)], min_val=0, max_val=ST)
                for q in range(PIECES):
                    is_w1, c, k = piece(q)
                    if is_w1:
                        high, low = (w[:, k:k + 2, 512 * c:512 * c + 512] for w in (w1h, w1l))
                    else:
                        high, low = (w[:, 4 * c + k:4 * c + k + 2, :] for w in (w2h, w2l))
                    dve.wait_ge(piece_in[q % RING], 16 * (PIECES // RING) * e + 16 * (q // RING) + 16)
                    if not first and q % HALF == 0:
                        dve.wait_ge(h_made if is_w1 else y_part, before * NC + (c + 1))
                    dve.tensor_copy(high, stage[:, q % RING])
                    dve.drain()
                    dve.tensor_tensor(low, stage[:, q % RING], high.bitcast(F32), ALU.subtract).then_inc(split, 1)
            splits(0, True)
            with dve.Fori(1, E) as e:
                splits(e, False)
            for t in range(T):
                for k in range(2):
                    r = (2 * t + k) % (2 * RING)
                    dve.drain()
                    dve.wait_ge(come[r], 16 * ((2 * t + k) // (2 * RING)) + 16)
                    dve.scalar_tensor_tensor(x[:, t, :], stage[:, r // 2, r % 2, :], core.gate[:, t, k:k + 1], x[:, t, :],
                                             ALU.mult, ALU.add).then_inc(weighed, 1)

        @block.gpsimd
        def _(pool):
            pool.wait_ge(routed, 1)
            for t in range(T):
                for k in range(2):
                    pool.indirect_dma_start(core.sent[n], bass.IndirectOffsetOnAxis(ap=core.slot[:, k, t:t + 1], axis=0),
                                            core.rows[:, t, :], None).then_inc(sent, 16)

            def low_x(m):
                pool.wait_ge(xh_made, m + 1)
                pool.tensor_tensor(xl[:].rearrange("p k n -> p (k n)"), xf, xh[:].rearrange("p k n -> p (k n)").bitcast(F32),
                                   ALU.subtract).then_inc(xl_made, 1)
            low_x(0)

            def step(m, first, last):
                for c in range(NC):
                    pool.wait_ge(hh_made, NC * m + c + 1)
                    pool.tensor_tensor(hl[:, 4 * c:4 * c + 4, :].rearrange("p k n -> p (k n)"), g[c % 2],
                                       hh[:, 4 * c:4 * c + 4, :].rearrange("p k n -> p (k n)").bitcast(F32), ALU.subtract)\
                        .then_inc(hl_made, 1)
                    if c == NC - 2 and not last:
                        low_x(m + 1)
            peel(pool, step)
            pool.wait_ge(y_stored, 16 * ST)
            pool.wait_ge(split, PIECES * E)
            for i in range(2 * T):
                r = i % (2 * RING)
                if i >= 2 * RING:
                    pool.wait_ge(weighed, i - 2 * RING + 1)
                pool.indirect_dma_start(stage[:, r // 2, r % 2, :], None, core.back[n],
                                        bass.IndirectOffsetOnAxis(ap=core.slot[:, i % 2, i // 2:i // 2 + 1], axis=0)).then_inc(come[r], 16)

        @block.scalar
        def _(act):
            def fetch(m):
                act.dma_start(xg, core.sent[n][ds(m * P, P), :]).then_inc(rows_in, 16)

            def split_x(m):
                act.wait_ge(xT_made, m + 1)
                act.activation(xf, XP[:, 0, :], ACT.Copy).then_inc(xf_made, 1)
                act.wait_ge(xf_made, m + 1)
                act.activation(xh[:].rearrange("p k n -> p (k n)"), xf, ACT.Copy).then_inc(xh_made, 1)

            act.wait_ge(sent, 16 * 2 * T)
            if biased:
                act.wait_ge(bias_in, 32)
            act.sem_inc(y_copied, 1)
            fetch(0)
            split_x(0)
            fetch(1)

            def step(m, first, last):
                if biased:
                    e = act.value_load(core.expert_of[0:1, ds(m, 1)], min_val=0, max_val=E - 1)

                def copy_h(c):
                    act.wait_ge(h_made, NC * m + c + 1 + NC)
                    act.activation(h[c % 2], HP[:, c % 2, :], ACT.Copy).then_inc(h_copied, 1)

                def gelu(c):
                    act.wait_ge(hT_made, NC * m + c + 1)
                    if not (first and c < 2):
                        act.wait_ge(hl_made, NC * m + c - 1)
                    if biased:
                        for k in range(4):
                            op = act.activation(g[c % 2][:, P * k:P * k + P], TP[:, c % 2, P * k:P * k + P], ACT.Gelu,
                                                bias=b1[:, ds(e, 1), 4 * c + k:4 * c + k + 1].rearrange("p a b -> p (a b)"))
                    else:
                        op = act.activation(g[c % 2], TP[:, c % 2, :], ACT.Gelu)
                    op.then_inc(g_made, 1)
                    act.wait_ge(g_made, NC * m + c + 1)
                    act.activation(hh[:, 4 * c:4 * c + 4, :].rearrange("p k n -> p (k n)"), g[c % 2], ACT.Copy).then_inc(hh_made, 1)
                copy_h(0)
                for c in range(1, NC):
                    copy_h(c)
                    gelu(c - 1)
                if not last:
                    split_x(m + 1)
                gelu(NC - 1)
                if not last:
                    act.wait_ge(xT_made, m + 2)
                    fetch(m + 2)
                if not first:
                    act.wait_ge(y_stored, 16 * m)
                act.wait_ge(y_part, NC * m + 2 * NC)
                act.activation(y, YP[:, 0, :], ACT.Copy).then_inc(y_copied, 1)
                act.wait_ge(y_copied, m + 2)
                act.dma_start(core.back[n][ds(m * P, P), :], y).then_inc(y_stored, 16)
            peel(act, step)
            act.wait_ge(y_stored, 16 * ST)
            act.wait_ge(rows_in, 16 * (ST + 1))

        @block.tensor
        def _(pe):
            pe.wait_ge(picked, 1)
            flat = both[:].rearrange("p t e -> p (t e)")
            pe.matmul(RP[:, 0, 0:TE], tab("before"), flat, start=True, stop=True)
            pe.matmul(RP[:, 1, 0:TE], tab("ones"), flat, start=True, stop=True).then_inc(counted, 1)
            pe.sem_inc(h_made, NC)
            pe.sem_inc(y_part, NC)
            if biased:
                pe.wait_ge(mixed, 1)
                pe.wait_ge(bias_in, 32)
                for c in range(2):
                    for t in range(4):
                        op = pe.transpose(TP[0:E, c, P * t:P * t + P], mix[:, 4 * c + t, :], tab("ident"))
                    op.then_inc(mixT_made, 1)
                pe.wait_ge(mixT_copied, 2)
                for t in range(T):
                    if t >= 2:
                        pe.wait_ge(b2_added, t - 1)
                    pe.matmul(RP[:, t % 2, :], mixT[:, t, :], b2[:], start=True, stop=True).then_inc(b2_made, 1)

            def rows_T(m):
                pe.wait_ge(rows_in, 16 * m + 16)
                for k in range(K):
                    op = pe.transpose(XP[:, 0, P * k:P * k + P], xg[:, P * k:P * k + P], tab("ident"))
                op.then_inc(xT_made, 1)

            def hidden(m, e, c, first):
                pe.wait_ge(split, e * PIECES + HALF * (c + 1))
                if not (first and c < 2):
                    pe.wait_ge(h_copied, NC * m + c - 1)
                for k in range(K):
                    cols = slice(512 * c, 512 * c + 512)
                    op = passes(pe, HP[:, c % 2, :], (xh[:, k, :], xl[:, k, :]), (w1h[:, k, cols], w1l[:, k, cols]), k == 0, k == K - 1)
                op.then_inc(h_made, 1)

            def hidden_T(m, c, first):
                pe.wait_ge(h_copied, NC * m + c + 1)
                if not (first and c < 2):
                    pe.wait_ge(g_made, NC * m + c - 1)
                for k in range(4):
                    op = pe.transpose(TP[:, c % 2, P * k:P * k + P], h[c % 2][:, P * k:P * k + P], tab("ident"))
                op.then_inc(hT_made, 1)

            def step(m, first, last):
                e = pe.value_load(core.expert_of[0:1, ds(m, 1)], min_val=0, max_val=E - 1)
                pe.wait_ge(xl_made, m + 1)
                hidden(m, e, 0, first)
                for c in range(1, NC):
                    hidden(m, e, c, first)
                    hidden_T(m, c - 1, first)
                if not last:
                    rows_T(m + 1)
                hidden_T(m, NC - 1, first)
                pe.wait_ge(y_copied, m + 1)
                for c in range(NC):
                    pe.wait_ge(split, e * PIECES + HALF * (NC + c + 1))
                    pe.wait_ge(hl_made, NC * m + c + 1)
                    for k in range(4 * c, 4 * c + 4):
                        op = passes(pe, YP[:, 0, :], (hh[:, k, :], hl[:, k, :]), (w2h[:, k, :], w2l[:, k, :]), k == 0, k == NF - 1)
                    op.then_inc(y_part, 1)
            rows_T(0)
            peel(pe, step)


def phase_layer1(nc, core):
    A, x, tab = core.A, core.x, core.tab
    with ExitStack() as ctx:
        sb = lambda name, shape, dt=F32: ctx.enter_context(nc.sbuf_tensor("l1_" + name, shape, dt))
        sem = semaphores(nc, ctx, "l1_")
        sems = lambda name: [sem(f"{name}{s}") for s in range(2)]
        two = lambda name, shape: [sb(f"{name}{s}", shape) for s in range(2)]
        W3 = 3 * HS

        wqkv, wo, rw = sb("wqkv", [P, K, 4 * HS]), sb("wo", [P, 2, D]), sb("rw", [P, K, E])
        ctxT = sb("ctxT", [P, NB, K, SKP])
        ctxn = sb("ctxn", [P, NB, 2, D])
        ctxl = sb("ctxl", [B, D])
        stats, mv, veps, rstd = two("stats", [P, 6]), two("mv", [P, 2]), two("veps", [P, 1]), two("rstd", [P, 1])
        mhalf = sb("mhalf", [P, 1])
        xn, xT = two("xn", [P, D]), two("xT", [P, K, P])
        ls, lsl, lT = two("ls", [P, SK]), two("lsl", [P, 32]), two("lT", [P, 3, P])
        nm, rs, ri = two("nm", [P, 2]), two("rs", [P, 2]), two("ri", [P, 2])
        ex = two("ex", [P, D])
        t1, t2, r, v, rT = (two(a, s) for a, s in (("t1", [P, W3]), ("t2", [P, W3]), ("r", [P, W3]), ("v", [P, HS]), ("rT", [P, 3, P])))
        sm, pT = two("sm", [P, 2, P]), two("pT", [P, 2, P])
        o, oT = two("o", [P, 2 * HS]), two("oT", [P, 2, P])
        lg = two("lg", [P, E])

        R = [[ctx.enter_context(nc.psum_tensor(f"l1_R{s}{k}", [P, 512], F32)) for k in range(2)] for s in range(2)]
        LS = ctx.enter_context(nc.psum_tensor("l1_LS", [P, NB, 512], F32))

        weights_in, ctxl_in = sem("weights_in"), sem("ctxl_in")
        WEIGHTS = 16 * 4
        ctxT_in, ctxn_in = [sem(f"ctxT_in{b}") for b in range(NB)], [sem(f"ctxn_in{b}") for b in range(NB)]
        mhalf_set = sem("mhalf_set")
        var_ready, rstd_ready, xn_ready, rows_kept = sems("var_ready"), sems("rstd_ready"), sems("xn_ready"), sems("rows_kept")
        r_ready = sems("r_ready")
        r_free = [sems(f"r_free{s}_") for s in range(2)]
        ls_ready, ls_free, lin_used = sem("ls_ready"), sem("ls_free"), sem("lin_used")
        lsl_ready = sems("lsl_ready")
        fmax, fexp = sems("fmax"), sems("fexp")
        r_made, p_made, shifted, exp_done = sems("r_made"), sems("p_made"), sems("shifted"), sems("exp_done")
        o_made = sems("o_made")
        lshift, lexp = sems("lshift"), sems("lexp")

        XT0, LT, LO, XT1, QKV, RT, SC, PTT, PV, OT, WO, XT2, LOG = range(13)
        USES, OF_BANK = 13, (7, 6)
        block = ctx.enter_context(nc.Block())

        def ready(eng, s, it, n):
            eng.wait_ge(r_ready[s], USES * it + n + 1)

        @block.sync
        def _(sp):
            sp.dma_start(wqkv[:], A["wqkv1"].rearrange("(k p) n -> p k n", p=P)).then_inc(weights_in, 16)
            sp.dma_start(wo[:], A["wo1"].rearrange("(k p) n -> p k n", p=P)).then_inc(weights_in, 16)
            sp.dma_start(rw[:], A["rw1"].rearrange("(k p) n -> p k n", p=P)).then_inc(weights_in, 16)
            sp.dma_start(ctxl[:], A["ctx"].rearrange("b k d -> b (k d)")[:, (SK - 1) * D:SK * D]).then_inc(weights_in, 16)

            def loads(j, first):
                for b in range(NB):
                    if not first:
                        sp.wait_ge(ls_ready, NB * j - NB + b + 1)
                    sp.dma_start(ctxT[:, b], A["ctxT"][ds(j * NB + b, 1), :, :]
                                 .rearrange("a p n -> p (a n)").rearrange("p (k n) -> p k n", k=K)).then_inc(ctxT_in[b], 16)
                for b in range(NB):
                    if not first:
                        sp.wait_ge(lin_used, NB * j - NB + b + 1)
                    sp.dma_start(ctxn[:, b], A["ctx"][ds(j * NB + b, 1), 0:2 * P, :]
                                 .rearrange("a (k p) d -> p (a k) d", p=P)).then_inc(ctxn_in[b], 16)
            loads(0, True)
            with sp.Fori(1, T) as j:
                loads(j, False)

        @block.gpsimd
        def _(pool):
            pool.memset(mhalf[:], -0.5).then_inc(mhalf_set, 1)
            pool.wait_ge(mhalf_set, 1)
            for kept in rows_kept:
                pool.sem_inc(kept, 1)
            with pool.Fori(0, T // 2) as it:
                for k in range(3):
                    for s in range(2):
                        pool.drain()
                        pool.wait_ge(var_ready[s], 3 * it + k + 1)
                        pool.tensor_tensor(rstd[s][:], veps[s][:], mhalf[:], ALU.pow).then_inc(rstd_ready[s], 1)
                for s in range(2):
                    pool.wait_ge(xn_ready[s], 3 * it + 3)
                    pool.wait_ge(mhalf_set, 1)
                    pool.tensor_copy(core.rows[:, ds(2 * it + s, 1), :].rearrange("p a d -> p (a d)"), xn[s][:])\
                        .then_inc(rows_kept[s], 1)

        @block.vector
        def _(dve):
            dve.wait_ge(weights_in, WEIGHTS)
            def tile(it, s):
                return x[:, ds(2 * it + s, 1), :].rearrange("p a d -> p (a d)")

            def norm(it, k):
                for s in range(2):
                    dve.drain()
                    dve.bn_stats(stats[s][:], tile(it, s))
                for s in range(2):
                    dve.drain()
                    dve.bn_aggr(mv[s][:], stats[s][:])
                for s in range(2):
                    dve.drain()
                    dve.tensor_scalar(veps[s][:], mv[s][:, 1:2], EPS, None, ALU.add).then_inc(var_ready[s], 1)
                for s in range(2):
                    dve.wait_ge(rstd_ready[s], 3 * it + k + 1)
                    if k == 0:
                        dve.wait_ge(rows_kept[s], it + 1)
                    if k > 0:
                        ready(dve, s, it, (XT0, XT1)[k - 1])
                    dve.tensor_scalar(xn[s][:], tile(it, s), mv[s][:, 0:1], rstd[s][:, 0:1],
                                      ALU.subtract, ALU.mult).then_inc(xn_ready[s], 1)

            for free in r_free[0] + r_free[1]:
                dve.sem_inc(free, 1)
            with dve.Fori(0, T // 2) as it:
                norm(it, 0)
                for s in range(2):
                    dve.drain()
                    dve.wait_ge(ls_free, NB * (2 * it + s) + NB)
                    dve.tensor_scalar(lsl[s][:], tab("eye_tile").rearrange("p (t n) -> p t n", n=32)[:, ds(2 * it + s, 1), :]
                                      .rearrange("p a n -> p (a n)"), ls[s][:, SK - 1:SK], None, ALU.mult).then_inc(lsl_ready[s], 1)
                for s in range(2):
                    dve.drain()
                    ready(dve, s, it, LO)
                    dve.tensor_reduce(nm[s][:, 0:1], R[s][LO % 2][:], X, ALU.max, negate=True).then_inc(fmax[s], 1)
                for s in range(2):
                    dve.wait_ge(fexp[s], it + 1)
                    dve.reciprocal(ri[s][:, 0:1], rs[s][:, 0:1])
                    dve.drain()
                    dve.scalar_tensor_tensor(tile(it, s), ex[s][:], ri[s][:, 0:1], tile(it, s), ALU.mult, ALU.add)
                norm(it, 1)
                for s in range(2):
                    dve.drain()
                    ready(dve, s, it, QKV)
                    q = R[s][QKV % 2][:, 0:W3]
                    pair = lambda a: a.rearrange("p (h i c) -> p h i c", h=3, c=2)
                    wide = lambda name: tab(name).rearrange("p (i c) -> p i c", c=2).unsqueeze(1)
                    dve.tensor_tensor(t1[s][:].rearrange("p (h i) -> p h i", h=3), q.rearrange("p (h i) -> p h i", h=3),
                                      tab("cos").unsqueeze(1).to_broadcast([P, 3, HS]), ALU.mult)
                    for c in range(2):
                        dve.tensor_tensor(pair(t2[s][:])[:, :, :, c], pair(q)[:, :, :, 1 - c],
                                               wide("sin")[:, :, :, c].to_broadcast([P, 3, HS // 2]), ALU.mult)
                    dve.tensor_copy(v[s][:], R[s][QKV % 2][:, W3:W3 + HS]).then_inc(r_free[s][QKV % 2], 1)
                    dve.drain()
                    dve.tensor_tensor(r[s][:], t1[s][:], t2[s][:], ALU.add).then_inc(r_made[s], 1)
                for s in range(2):
                    dve.drain()
                    ready(dve, s, it, SC)
                    dve.scalar_tensor_tensor(sm[s][:], R[s][SC % 2][:, 0:2 * P].rearrange("p (h k) -> p h k", h=2), float(HS) ** -0.5,
                                             tab("block_causal").unsqueeze(1).to_broadcast([P, 2, P]), ALU.mult, ALU.add)\
                       .then_inc(r_free[s][SC % 2], 1)
                    dve.drain()
                    dve.tensor_reduce(nm[s][:], sm[s][:], X, ALU.max, negate=True)
                    dve.drain()
                    dve.tensor_tensor(sm[s][:], sm[s][:], nm[s][:].unsqueeze(2).to_broadcast([P, 2, P]), ALU.add)\
                       .then_inc(shifted[s], 1)
                for s in range(2):
                    dve.drain()
                    dve.wait_ge(exp_done[s], it + 1)
                    dve.tensor_reduce(rs[s][:], sm[s][:], X, ALU.add)
                    dve.drain()
                    dve.reciprocal(ri[s][:], rs[s][:])
                    dve.drain()
                    dve.tensor_tensor(sm[s][:], sm[s][:], ri[s][:].unsqueeze(2).to_broadcast([P, 2, P]), ALU.mult).then_inc(p_made[s], 1)
                for s in range(2):
                    ready(dve, s, it, PV)
                    dve.tensor_copy(o[s][:], R[s][PV % 2][:, 0:2 * HS]).then_inc(r_free[s][PV % 2], 1)
                for s in range(2):
                    ready(dve, s, it, WO)
                    dve.tensor_tensor(tile(it, s), tile(it, s), R[s][WO % 2][:], ALU.add).then_inc(r_free[s][WO % 2], 1)
                norm(it, 2)
                for s in range(2):
                    dve.drain()
                    ready(dve, s, it, LOG)
                    dve.tensor_copy(lg[s][:], R[s][LOG % 2][:, 0:E]).then_inc(r_free[s][LOG % 2], 1)
                    dve.drain()
                    dve.tensor_reduce(nm[s][:, 0:1], lg[s][:], X, ALU.max, negate=True).then_inc(lshift[s], 1)
                for s in range(2):
                    dve.drain()
                    dve.wait_ge(lexp[s], it + 1)
                    dve.reciprocal(ri[s][:, 0:1], rs[s][:, 0:1])
                    dve.drain()
                    dve.tensor_scalar(core.probs[:, ds(2 * it + s, 1), :].rearrange("p a e -> p (a e)"), lg[s][:],
                                      ri[s][:, 0:1], None, ALU.mult)

        @block.scalar
        def _(act):
            act.wait_ge(weights_in, WEIGHTS)
            def copy(s, it, n, out, w):
                ready(act, s, it, n)
                act.activation(out, R[s][n % 2][:, 0:w], ACT.Copy).then_inc(r_free[s][n % 2], 1)

            flat = lambda a: a[:].rearrange("p k n -> p (k n)")
            with act.Fori(0, T // 2) as it:
                for s in range(2):
                    copy(s, it, XT0, flat(xT[s]), D)
                for s in range(2):
                    for b in range(NB):
                        rows = slice(S * b, S * b + S)
                        act.wait_ge(ls_ready, NB * (2 * it + s) + b + 1)
                        act.activation(ls[s][rows], LS[rows, b, 0:SK], ACT.Copy, scale=float(D) ** -0.5).then_inc(ls_free, 1)
                for s in range(2):
                    ready(act, s, it, LT)
                    act.activation(lT[s][0:32, 2, :], R[s][LT % 2][0:32, 2 * P:3 * P], ACT.Copy)
                    act.activation(lT[s][:, 0:2, :].rearrange("p k n -> p (k n)"), R[s][LT % 2][:, 0:2 * P], ACT.Copy)\
                       .then_inc(r_free[s][LT % 2], 1)
                for s in range(2):
                    act.wait_ge(fmax[s], it + 1)
                    act.activation(ex[s][:], R[s][LO % 2][:], ACT.Exp, bias=nm[s][:, 0:1], accum_out=rs[s][:, 0:1]).then_inc(r_free[s][LO % 2], 1)
                    act.drain()
                    act.sem_inc(fexp[s], 1)
                for s in range(2):
                    copy(s, it, XT1, flat(xT[s]), D)
                for s in range(2):
                    copy(s, it, RT, flat(rT[s]), 3 * P)
                for s in range(2):
                    act.wait_ge(shifted[s], it + 1)
                    act.activation(sm[s][:], sm[s][:], ACT.Exp).then_inc(exp_done[s], 1)
                for s in range(2):
                    copy(s, it, PTT, flat(pT[s]), 2 * P)
                for s in range(2):
                    copy(s, it, OT, flat(oT[s]), 2 * P)
                for s in range(2):
                    copy(s, it, XT2, flat(xT[s]), D)
                for s in range(2):
                    act.wait_ge(lshift[s], it + 1)
                    act.activation(lg[s][:], lg[s][:], ACT.Exp, bias=nm[s][:, 0:1], accum_out=rs[s][:, 0:1]).then_inc(lexp[s], 1)

        @block.tensor
        def _(pe):
            pe.wait_ge(weights_in, WEIGHTS)
            def free(s, it, n):
                pe.wait_ge(r_free[s][n % 2], OF_BANK[n % 2] * it + n // 2 + 1)

            def read(s, it, n):
                pe.wait_ge(r_free[s][n % 2], OF_BANK[n % 2] * it + n // 2 + 2)

            def transposes(s, it, n, src, count):
                free(s, it, n)
                for k in range(count):
                    op = pe.transpose(R[s][n % 2][:, P * k:P * k + P], src[:, P * k:P * k + P], tab("ident"))
                op.then_inc(r_ready[s], 1)

            def product(s, it, n, lhs, rhs, w):
                free(s, it, n)
                for k in range(len(lhs)):
                    op = pe.matmul(R[s][n % 2][:, 0:w], lhs[k], rhs[k], start=(k == 0), stop=(k == len(lhs) - 1))
                op.then_inc(r_ready[s], 1)

            with pe.Fori(0, T // 2) as it:
                for s in range(2):
                    pe.wait_ge(xn_ready[s], 3 * it + 1)
                    transposes(s, it, XT0, xn[s][:], K)
                for s in range(2):
                    read(s, it, XT0)
                    for b in range(NB):
                        pe.wait_ge(ctxT_in[b], 16 * (2 * it + s) + 16)
                        if s:
                            pe.wait_ge(ls_free, 8 * it + b + 1)
                        for k in range(K):
                            op = pe.matmul(LS[:, b, 0:SK], xT[s][:, k, :], ctxT[:, b, k, 0:SK], start=(k == 0), stop=(k == K - 1))
                        op.then_inc(ls_ready, 1)
                for s in range(2):
                    pe.wait_ge(lsl_ready[s], it + 1)
                    free(s, it, LT)
                    for k in range(2):
                        pe.transpose(R[s][LT % 2][:, P * k:P * k + P], ls[s][:, P * k:P * k + P], tab("ident"))
                    pe.transpose(R[s][LT % 2][0:32, 2 * P:3 * P], lsl[s][:], tab("ident")).then_inc(r_ready[s], 1)
                for s in range(2):
                    free(s, it, LO)
                    read(s, it, LT)
                    pe.matmul(R[s][LO % 2][:], lT[s][0:32, 2, :], ctxl[:], start=True, stop=True, skip_group_check=True)
                    for b in range(NB):
                        rows = slice(S * b, S * b + S)
                        pe.wait_ge(ctxn_in[b], 16 * (2 * it + s) + 16)
                        for k in range(2):
                            op = pe.matmul(R[s][LO % 2][rows, :], lT[s][:, k, rows], ctxn[:, b, k, :], start=False, stop=(k == 1),
                                           skip_group_check=True)
                        op.then_inc(lin_used, 1)
                    pe.drain()
                    pe.sem_inc(r_ready[s], 1)
                for s in range(2):
                    pe.wait_ge(xn_ready[s], 3 * it + 2)
                    transposes(s, it, XT1, xn[s][:], K)
                for s in range(2):
                    read(s, it, XT1)
                    product(s, it, QKV, [xT[s][:, k, :] for k in range(K)], [wqkv[:, k, :] for k in range(K)], 4 * HS)
                for s in range(2):
                    pe.wait_ge(r_made[s], it + 1)
                    transposes(s, it, RT, r[s][:], 3)
                for s in range(2):
                    read(s, it, RT)
                    free(s, it, SC)
                    for hd in range(2):
                        op = pe.matmul(R[s][SC % 2][:, P * hd:P * hd + P], rT[s][:, hd, :], rT[s][:, 2, :], start=True, stop=True)
                    op.then_inc(r_ready[s], 1)
                for s in range(2):
                    pe.wait_ge(p_made[s], it + 1)
                    transposes(s, it, PTT, sm[s][:].rearrange("p h k -> p (h k)"), 2)
                for s in range(2):
                    read(s, it, PTT)
                    free(s, it, PV)
                    for hd in range(2):
                        op = pe.matmul(R[s][PV % 2][:, HS * hd:HS * hd + HS], pT[s][:, hd, :], v[s][:], start=True, stop=True)
                    op.then_inc(r_ready[s], 1)
                for s in range(2):
                    read(s, it, PV)
                    transposes(s, it, OT, o[s][:], 2)
                for s in range(2):
                    read(s, it, OT)
                    product(s, it, WO, [oT[s][:, k, :] for k in range(2)], [wo[:, k, :] for k in range(2)], D)
                for s in range(2):
                    pe.wait_ge(xn_ready[s], 3 * it + 3)
                    transposes(s, it, XT2, xn[s][:], K)
                for s in range(2):
                    read(s, it, XT2)
                    product(s, it, LOG, [xT[s][:, k, :] for k in range(K)], [rw[:, k, :] for k in range(K)], E)


def build(nc, A, out, stop=5):
    with ExitStack() as ctx:
        core = Core(nc, ctx, A)
        phase_cross0(nc, core)
        if stop >= 1:
            phase_self0(nc, core)
        if stop >= 2:
            phase_mixture(nc, core, 0, F0, True, 1e-8, 0.3)
        if stop >= 3:
            phase_layer1(nc, core)
        if stop >= 5:
            phase_mixture(nc, core, 1, F1, False, 0.0, 1.0)
        finish(nc, core, out)


def finish(nc, core, out):
    with ExitStack() as ctx:
        stored = ctx.enter_context(nc.semaphore("stored"))
        block = ctx.enter_context(nc.Block())

        @block.sync
        def _(sp):
            sp.dma_start(out.rearrange("b s d -> (b s) d").rearrange("(t p) d -> p t d", p=P), core.x[:]).then_inc(stored, 16)
            sp.wait_ge(stored, 16)


def layout(**inputs):
    a = {k: np.asarray(v) for k, v in inputs.items()}
    c = np.ascontiguousarray
    rowvec = lambda v: c(v.reshape(1, -1))
    ctx = a["ctx_1024"]
    ctxT = np.zeros((B, D, SKP), ctx.dtype)
    ctxT[:, :, :SK] = ctx.transpose(0, 2, 1)
    heads = lambda w: w.reshape(w.shape[:-1] + (H, DH))[..., :KPH].reshape(w.shape[:-1] + (LAT,))
    d = {
        "tables": tables(),
        "x": c(a["x"].reshape(B * S, D)),
        "ctx": c(ctx),
        "ctxT": c(ctxT.reshape(B, K, P, SKP).transpose(0, 2, 1, 3).reshape(B, P, K * SKP)),
        "ctx_lastT": c(ctx[::-1, SK - 1, :].T.reshape(K, P, B).transpose(1, 0, 2)),
        "mask": c(a["mask_Bx1xS2_if1"].reshape(T, NB * SK)),
        "wq": a["L0_xattn_Wq"], "wk": a["L0_xattn_Wk"], "wv": a["L0_xattn_Wv"], "wo": a["L0_xattn_Wo"],
        "bqT": c(a["L0_xattn_bq"].reshape(G, P).T), "bkT": c(a["L0_xattn_bk"].reshape(G, P).T),
        "bv": a["L0_xattn_bv"], "bo": a["L0_xattn_bo"],
        "wqkv": a["L0_attn_qkv_weights"],
        "lat_w": c(np.concatenate([heads(a["L0_ffn_q_w"]), a["L0_ffn_k_w"], a["L0_ffn_v_w"]], axis=1)),
        "lat_b": c(np.concatenate([heads(a["L0_ffn_q_b"]), a["L0_ffn_k_b"], a["L0_ffn_v_b"]])),
        "lat_ow": c(a["L0_ffn_o_w"][:LAT]), "lat_ob": a["L0_ffn_o_b"],
        "rw0": a["L0_ffn_router_w"], "rb0": a["L0_ffn_router_b"],
        "w1_0": a["L0_ffn_w1"], "b1T": c(a["L0_ffn_b1"].reshape(E, F0 // P, P).transpose(2, 0, 1)), "w2_0": a["L0_ffn_w2"], "b2_0": a["L0_ffn_b2"],
        "wqkv1": c(np.concatenate([a["L1_attn_Wq"].reshape(2 * HS, D), a["L1_attn_Wk"], a["L1_attn_Wv"]], axis=0).T),
        "wo1": c(a["L1_attn_Wo"].T),
        "rw1": c(a["L1_ffn_router_w"].T),
        "w1_1": a["L1_ffn_w1"], "w2_1": a["L1_ffn_w2"],
    }
    return {k: c(v) for k, v in d.items()}


def kernel(**inputs):
    import concourse.bacc as bacc
    from concourse.bass_utils import run_bass_kernel_spmd

    nc = bacc.Bacc("TRN2", target_bir_lowering=False, num_devices=1)
    arrays = {f"in_{k}": v for k, v in layout(**inputs).items()}
    A = {k[3:]: nc.dram_tensor(k, v.shape, mybir.dt.from_np(v.dtype), kind="ExternalInput").ap() for k, v in arrays.items()}
    out = nc.dram_tensor("out", (B, S, D), F32, kind="ExternalOutput").ap()
    build(nc, A, out)
    r = run_bass_kernel_spmd(nc, [arrays], core_ids=[0])
    return r.results[0]["out"]
```

```python
from contextlib import ExitStack

import numpy as np

import concourse.bass as bass
from concourse import mybir

F32 = mybir.dt.float32
F32R = mybir.dt.float32r
I32 = mybir.dt.int32
U32 = mybir.dt.uint32
ALU = mybir.AluOpType
ACT = mybir.ActivationFunctionType
X = mybir.AxisListType.X
ds = bass.ds

P = 128
B, S, D = 32, 32, 512
SK = 257
SKP = SK + 1
K = D // P
T = B * S // P
NB = P // S
SL = 4
H, DH = 16, 32
G = 4
LAT, KPH = 256, 16
E = 8
ST = 2 * B * S // P + E - 1
F0, F1 = 1024, 2048
HS = 128
EPS = 1e-5
NEG = -1e9
BIG = 3e38

TABLES = {}
_at = 0
for _name, _n in (("ident", P), ("ones", P), ("before", P), ("eye_tile", T * 32),
                  ("causal", S), ("cos", HS), ("sin", HS), ("block_causal", P),
                  ("expert_id", E), ("step128", E), ("upto", E * E), ("tile_id", ST)):
    TABLES[_name] = (_at, _n)
    _at += _n
TABLE = _at


def tables():
    p = np.arange(P)
    t = {}
    t["ident"] = np.eye(P)
    t["ones"] = np.ones((P, P))
    t["before"] = p[:, None] < p[None, :]
    t["eye_tile"] = (np.arange(32)[None, None] == NB * np.arange(T)[None, :, None] + (p // S)[:, None, None])
    t["causal"] = np.where(np.tril(np.ones((S, S)))[p % S] > 0, BIG, NEG)
    theta = np.float32(10000.0) ** (np.float32(-2.0) * np.arange(0, HS, 2, dtype=np.float32) / np.float32(HS))
    angle = (p % S).astype(np.float32)[:, None] * theta[None]
    t["cos"] = np.repeat(np.cos(angle), 2, axis=1)
    t["sin"] = np.stack([-np.sin(angle), np.sin(angle)], -1)
    t["block_causal"] = np.where((p[:, None] // S == p[None] // S) & (p[None] <= p[:, None]), 0.0, -1e30)
    t["expert_id"] = np.broadcast_to(np.arange(E), (P, E))
    t["step128"] = np.broadcast_to(np.where(np.arange(E) == 0, -1, P * np.arange(E)), (P, E))
    t["upto"] = np.broadcast_to(np.tril(np.ones((E, E))).reshape(1, -1), (P, E * E))
    t["tile_id"] = np.broadcast_to(np.arange(ST), (P, ST))
    return np.concatenate([np.asarray(t[n], np.float32).reshape(P, -1) for n in TABLES], axis=1)


def semaphores(nc, ctx, prefix):
    taken = []

    def give_back():
        nc.clear_and_free_semaphores(taken)
        nc.all_engine_barrier()
    ctx.callback(give_back)

    def sem(name):
        taken.append(nc.alloc_semaphore(prefix + name))
        return taken[-1]
    return sem


def passes(pe, out, xs, ws, first, last):
    (x_high, x_low), (w_high, w_low) = xs, ws
    pe.matmul(out, x_high, w_low, start=first, stop=False)
    pe.matmul(out, x_low, w_high, start=False, stop=False)
    return pe.matmul(out, x_high, w_high, start=False, stop=last)


def staggered(steps, groups, it):
    for k in range(len(steps) + len(groups) - 1):
        for behind, group in enumerate(groups):
            if 0 <= k - behind < len(steps) and steps[k - behind]:
                steps[k - behind](it, group)


class Core:

    def __init__(self, nc, ctx, A):
        self.nc, self.A = nc, A
        self.sb = lambda name, shape, dt=F32: ctx.enter_context(nc.sbuf_tensor(name, shape, dt))
        self.x = self.sb("x", [P, T, D])
        self.rows = self.sb("rows", [P, T, D])
        self.probs = self.sb("probs", [P, T, E])
        self.table = self.sb("table", [P, TABLE])
        self.slot = self.sb("slot", [P, 2, T], U32)
        self.gate = self.sb("gate", [P, T, 2])
        self.expert_of = self.sb("expert_of", [1, ST], I32)
        self.tiles_before = self.sb("tiles_before", [1, E], I32)
        dram = lambda name, rows: nc.dram_tensor(name, [rows, D], F32, kind="Internal").ap()
        self.sent = [dram(f"sent{n}", (ST + 1) * P) for n in range(2)]
        self.v_last = nc.dram_tensor("v_last", [B, D], F32, kind="Internal").ap()
        self.back = [dram(f"back{n}", ST * P) for n in range(2)]

    def tab(self, name):
        a, n = TABLES[name]
        return self.table[:, a:a + n]


def phase_cross0(nc, core):
    A = core.A
    x, tab = core.x, core.tab
    with ExitStack() as ctx:
        sb = lambda name, shape, dt=F32: ctx.enter_context(nc.sbuf_tensor("c0_" + name, shape, dt))
        sem = semaphores(nc, ctx, "c0_")
        pb = lambda name, banks: ctx.enter_context(nc.psum_tensor("c0_" + name, [P, banks, 512], F32))

        wq, wo = sb("wq", [P, K, D]), sb("wo", [P, K, D])
        wk, wv = core.rows[:, 0:K, :], core.rows[:, K:2 * K, :]
        wkh, wkl, wvh, wvl = (sb(n, [P, K, D], F32R) for n in ("wkh", "wkl", "wvh", "wvl"))
        zero = sb("zero", [P, D])
        bq, bk = sb("bq", [P, G]), sb("bk", [P, G])
        bv, bo = sb("bv", [P, D]), sb("bo", [P, D])
        ctxT = sb("ctxT", [P, NB, K, SKP])
        ctxh, ctxl = sb("ctxh", [P, 2, K, SKP], F32R), sb("ctxl", [P, 2, K, SKP], F32R)
        lastT = sb("lastT", [P, K, B])
        maskt = sb("maskt", [P, NB, SK], I32)
        keep = sb("keep", [P, NB, SK])
        bound = sb("bound", [P, NB, SK])
        stats = sb("stats", [P, 6])
        mv = sb("mv", [P, 2])
        mhalf = sb("mhalf", [P, 1])
        veps = sb("veps", [P, 1])
        rstd = sb("rstd", [P, 1])
        xn = sb("xn", [P, D])
        xT = sb("xT", [P, K, P])
        qbd = sb("qbd", [P, NB, G, NB, S])
        kT = sb("kT", [P, 2, G, SK])
        v = sb("v", [P, 2, 2, D])
        vlast = sb("vlast", [B, D])
        vspread = sb("vspread", [P, NB, D])
        sm = sb("sm", [P, 2, G, SK])
        nmax = sb("nmax", [P, 2, G])
        rsum = sb("rsum", [P, 2, G])
        rinv = sb("rinv", [P, 2, G])
        plast = sb("plast", [P, G])
        olast = sb("olast", [P, D])
        on = sb("on", [P, D])
        pT = sb("pT", [P, 2 * G, P])
        o = sb("o", [P, D])
        oT = sb("oT", [P, K, P])

        KV = pb("KV", 3)
        SC = pb("SC", 2)
        TB = pb("TB", 2)
        O = pb("O", 1)

        wkv_in, weights_in, wo_in = sem("wkv_in"), sem("weights_in"), sem("wo_in")
        w_high, w_split = sem("w_high"), sem("w_split")
        ctx_high, ctx_split = sem("ctx_high"), sem("ctx_split")
        zero_made, rows_cleared = sem("zero_made"), sem("rows_cleared")
        ctx_in = [sem(f"ctx_in{b}") for b in range(NB)]
        mask_in = sem("mask_in")
        keep_made = sem("keep_made")
        bound_made = sem("bound_made")
        mhalf_set = sem("mhalf_set")
        var_ready = sem("var_ready")
        rstd_ready = sem("rstd_ready")
        xn_ready = sem("xn_ready")
        t_ready = sem("t_ready")
        t_free = [sem("t_free0"), sem("t_free1")]
        kv_ready = sem("kv_ready")
        kT_ready = sem("kT_ready")
        v_ready = sem("v_ready")
        vlast_done, vlast_ready, vlast_stored = sem("vlast_done"), sem("vlast_ready"), sem("vlast_stored")
        vspread_in = [sem(f"vspread_in{b}") for b in range(NB)]
        scores_ready = sem("scores_ready")
        masked = sem("masked")
        max_ready = sem("max_ready")
        exp_done = sem("exp_done")
        pv_ready = sem("pv_ready")
        o_ready = sem("o_ready")

        OT_USE, OUT_USE, PT_USE, XT_USE, Q_USE, USES = 0, 1, (2, 4, 6, 10), 8, 9, 12
        FINAL_OT, FINAL_OUT = 10, 11

        def use(n, last):
            return n - 2 if last and n > Q_USE else n

        block = ctx.enter_context(nc.Block())

        @block.sync
        def _(sp):
            def load_ctx(j, b):
                sp.dma_start(ctxT[:, b], A["ctxT"][ds(j * NB + b, 1), :, :]
                             .rearrange("a p n -> p (a n)").rearrange("p (k n) -> p k n", k=K)).then_inc(ctx_in[b], 16)

            def spread_v(j, b):
                sp.dma_start(vspread[:, b, :], core.v_last[ds(j * NB + b, 1), :].partition_broadcast(P)
                             .rearrange("p a d -> p (a d)")).then_inc(vspread_in[b], 16)

            for t, a in ((wk, "wk"), (wv, "wv")):
                sp.dma_start(t, A[a].rearrange("(k p) n -> p k n", p=P)).then_inc(wkv_in, 16)
            for t, a in ((bq, "bqT"), (bk, "bkT")):
                sp.dma_start(t[:], A[a]).then_inc(wkv_in, 16)
            sp.dma_start(bv[:], A["bv"].partition_broadcast(P)).then_inc(wkv_in, 16)
            load_ctx(0, 0)
            load_ctx(0, 1)
            sp.dma_start(wq[:], A["wq"].rearrange("(k p) n -> p k n", p=P)).then_inc(weights_in, 16)
            sp.dma_start(core.table[:], A["tables"]).then_inc(weights_in, 16)
            sp.dma_start(x[:], A["x"].rearrange("(t p) d -> p t d", p=P)).then_inc(weights_in, 16)
            sp.dma_start(lastT[:], A["ctx_lastT"]).then_inc(weights_in, 16)

            def load_mask(j):
                sp.dma_start(maskt[:], A["mask"][ds(j, 1), :].partition_broadcast(P)
                             .rearrange("p a (b k) -> p (a b) k", b=NB)).then_inc(mask_in, 16)
            load_mask(0)
            load_ctx(0, 2)
            load_ctx(0, 3)
            sp.dma_start(wo[:], A["wo"].rearrange("(k p) n -> p k n", p=P)).then_inc(wo_in, 16)
            sp.dma_start(bo[:], A["bo"].partition_broadcast(P)).then_inc(wo_in, 16)
            sp.wait_ge(vlast_ready, 1)
            sp.dma_start(core.v_last, vlast[:]).then_inc(vlast_stored, 16)
            sp.wait_ge(vlast_stored, 16)
            for b in range(NB):
                spread_v(0, b)
            sp.wait_ge(zero_made, 1)
            for sent in core.sent:
                sp.dma_start(sent.rearrange("(t p) d -> p t d", p=P),
                             zero[:].unsqueeze(1).to_broadcast([P, ST + 1, D])).then_inc(rows_cleared, 16)
            with sp.Fori(1, T) as j:
                sp.wait_ge(bound_made, j)
                load_mask(j)
                for b in range(NB):
                    sp.wait_ge(ctx_split, NB * j - NB + b + 1)
                    load_ctx(j, b)
                    sp.wait_ge(o_ready, NB * j - NB + b + 2)
                    spread_v(j, b)
            sp.wait_ge(rows_cleared, 32)

        WKV, WEIGHTS = 16 * 5, 16 * 4

        @block.gpsimd
        def _(pool):
            pool.memset(zero[:], 0.0).then_inc(zero_made, 1)
            pool.memset(mhalf[:], -0.5).then_inc(mhalf_set, 1)
            pool.wait_ge(mhalf_set, 1)

            def rsqrt(j):
                pool.drain()
                pool.wait_ge(var_ready, j + 1)
                pool.tensor_tensor(rstd[:], veps[:], mhalf[:], ALU.pow).then_inc(rstd_ready, 1)
            with pool.Fori(0, T) as j:
                rsqrt(j)

        @block.vector
        def _(dve):
            dve.wait_ge(wkv_in, WKV)
            def norm(j):
                dve.drain()
                dve.bn_stats(stats[:], x[:, ds(j, 1), :].rearrange("p a d -> p (a d)"))
                dve.drain()
                dve.bn_aggr(mv[:], stats[:])
                dve.drain()
                dve.tensor_scalar(veps[:], mv[:, 1:2], EPS, None, ALU.add).then_inc(var_ready, 1)

            def normed(j):
                dve.drain()
                dve.wait_ge(rstd_ready, j + 1)
                dve.tensor_scalar(xn[:], x[:, ds(j, 1), :].rearrange("p a d -> p (a d)"), mv[:, 0:1],
                                  rstd[:, 0:1], ALU.subtract, ALU.mult).then_inc(xn_ready, 1)

            def spread_q(u):
                dve.drain()
                dve.wait_ge(t_ready, u)
                for h in range(NB):
                    rows = slice(S * h, S * h + S)
                    last = dve.tensor_tensor(
                        qbd[rows, :, :, h, :].rearrange("p b g q -> p g b q"),
                        TB[rows, 1, :].rearrange("p (g b q) -> p g b q", g=G, b=NB),
                        bq[rows, :].unsqueeze(2).unsqueeze(3).to_broadcast([S, G, NB, S]), ALU.add)
                last.then_inc(t_free[1], 1)

            def copy_v(i, p, kt):
                dve.wait_ge(kv_ready, 6 * i + G + kt + 1)
                dve.tensor_tensor(v[:, p, kt, :], KV[:, 1 + kt, :], bv[:], ALU.add).then_inc(v_ready, 1)

            def low_ctx(i, b):
                dve.wait_ge(ctx_high, i + 1)
                dve.tensor_tensor(ctxl[:, b % 2], ctxT[:, b], ctxh[:, b % 2].bitcast(F32), ALU.subtract).then_inc(ctx_split, 1)

            dve.sem_inc(masked, 1)
            dve.sem_inc(o_ready, 1)
            for n, (w, high, low) in enumerate(((wk, wkh, wkl), (wv, wvh, wvl))):
                dve.wait_ge(w_high, n + 1)
                dve.tensor_tensor(low[:], w, high[:].bitcast(F32), ALU.subtract).then_inc(w_split, 1)
            for b in range(2):
                low_ctx(b, b)
            dve.memset(qbd[:], 0.0)
            copy_v(0, 0, 0)
            copy_v(0, 0, 1)
            dve.wait_ge(weights_in, WEIGHTS)
            norm(0)
            normed(0)
            dve.wait_ge(vlast_done, 1)
            dve.tensor_tensor(vlast[:], O[0:B, 0, :], bv[0:B, :], ALU.add).then_inc(vlast_ready, 1)
            spread_q(2)

            def grouped(a):
                return a[:].rearrange("p (g c) -> p g c", g=G)

            def add_output(j, u):
                dve.drain()
                dve.wait_ge(t_ready, u)
                xt = x[:, ds(j, 1), :].rearrange("p a d -> p (a d)")
                dve.tensor_tensor(xt, xt, TB[:, 1, :], ALU.add).then_inc(t_free[1], 1)
                dve.drain()
                dve.wait_ge(wo_in, 32)
                dve.tensor_tensor(xt, xt, bo[:], ALU.add)

            def tile(j, first=False, last=False):
                dve.drain()
                dve.wait_ge(mask_in, 16 * j + 16)
                dve.tensor_scalar(keep[:], maskt[:], 0, BIG, ALU.not_equal, ALU.mult).then_inc(keep_made, 1)
                dve.drain()
                dve.tensor_scalar(bound[:], keep[:], NEG, None, ALU.add).then_inc(bound_made, 1)
                for b in range(NB):
                    i = NB * j + b
                    for hf in range(2):
                        groups = slice(2 * hf, 2 * hf + 2)
                        dve.drain()
                        dve.wait_ge(scores_ready, 2 * i + hf + 1)
                        dve.scalar_tensor_tensor(sm[:, b % 2, groups, :], SC[:, :, 0:SK], float(DH) ** -0.5,
                                                 bound[:, b:b + 1, :].to_broadcast([P, 2, SK]), ALU.mult, ALU.min)\
                           .then_inc(masked, 1)
                        dve.drain()
                        dve.tensor_reduce(nmax[:, b % 2, groups], sm[:, b % 2, groups, :], X, ALU.max, negate=True)\
                           .then_inc(max_ready, 1)
                    if b == NB - 1 and not last:
                        spread_q(USES * j + Q_USE + 1)
                    dve.drain()
                    dve.wait_ge(exp_done, 2 * i + 2)
                    dve.reciprocal(rinv[:, b % 2, :], rsum[:, b % 2, :])
                    dve.drain()
                    dve.tensor_tensor(plast[:], sm[:, b % 2, :, SK - 1], rinv[:, b % 2, :], ALU.mult)
                    dve.drain()
                    dve.wait_ge(vspread_in[b], 16 * j + 16)
                    dve.tensor_tensor(grouped(olast), grouped(vspread[:, b, :]), plast[:].unsqueeze(2).to_broadcast([P, G, P]), ALU.mult)
                    if b == 0 and not first:
                        add_output(j - 1, USES * j + OUT_USE + 1)
                    if not (last and b == NB - 1):
                        copy_v(i + 1, (b + 1) % 2, 0)
                    if not (last and b + 2 >= NB):
                        low_ctx(i + 2, (b + 2) % NB)
                    if not (last and b == NB - 1):
                        copy_v(i + 1, (b + 1) % 2, 1)
                    if b == 0 and not last:
                        norm(j + 1)
                    if b == 1 and not last:
                        normed(j + 1)
                    dve.drain()
                    dve.wait_ge(pv_ready, i + 1)
                    dve.tensor_tensor(grouped(on), grouped(O[:, 0, :]), rinv[:, b % 2, :].unsqueeze(2).to_broadcast([P, G, P]), ALU.mult)
                    dve.drain()
                    for h in range(NB):
                        rows, cols = slice(S * h, S * h + S), slice(S * h, S * h + S)
                        op = dve.tensor_tensor(grouped(o)[S * b:S * b + S, :, cols], grouped(on)[rows, :, cols],
                                               grouped(olast)[rows, :, cols], ALU.add)
                    op.then_inc(o_ready, 1)
            tile(0, first=True)
            with dve.Fori(1, T - 1) as j:
                tile(j)
            tile(T - 1, last=True)
            add_output(T - 1, USES * (T - 1) + FINAL_OUT + 1)

        @block.scalar
        def _(act):
            act.wait_ge(wkv_in, WKV)
            def copy_k(i, p, g):
                act.wait_ge(kv_ready, 6 * i + g + 1)
                act.activation(kT[:, p, g, :], KV[:, g % 3, 0:SK], ACT.Identity, bias=bk[:, g:g + 1]).then_inc(kT_ready, 1)

            def copy_t(out, u, bank):
                act.wait_ge(t_ready, u)
                act.activation(out, TB[:, bank, 0:out.free_size()], ACT.Copy).then_inc(t_free[bank], 1)

            def high_ctx(i, b, j, first=False):
                act.wait_ge(ctx_in[b], 16 * j + 16)
                if not first:
                    act.wait_ge(kv_ready, 6 * i - 6)
                act.activation(ctxh[:, b % 2], ctxT[:, b], ACT.Copy).then_inc(ctx_high, 1)

            for w, high in ((wk, wkh), (wv, wvh)):
                act.activation(high[:], w, ACT.Copy).then_inc(w_high, 1)
            for b in range(2):
                high_ctx(b, b, 0, first=True)
            for g in range(G):
                copy_k(0, 0, g)
            copy_t(xT[:].rearrange("p k n -> p (k n)"), 1, 0)

            def tile(j, first=False, last=False):
                for b in range(NB):
                    i = NB * j + b
                    for hf in range(2):
                        if not (last and b == NB - 1):
                            copy_k(i + 1, (b + 1) % 2, 2 * hf)
                            copy_k(i + 1, (b + 1) % 2, 2 * hf + 1)
                        if b == hf == 0 and not first:
                            copy_t(oT[:].rearrange("p k n -> p (k n)"), USES * j + OT_USE + 1, 0)
                        act.wait_ge(max_ready, 2 * i + hf + 1)
                        for g in range(2 * hf, 2 * hf + 2):
                            op = act.activation(sm[:, b % 2, g, :], sm[:, b % 2, g, :], ACT.Exp,
                                                bias=nmax[:, b % 2, g:g + 1], accum_out=rsum[:, b % 2, g:g + 1])
                        op.then_inc(exp_done, 1)
                    if not (last and b + 2 >= NB):
                        high_ctx(i + 2, (b + 2) % NB, j + (b + 2) // NB)
                    n = use(PT_USE[b], last)
                    for c in range(2):
                        copy_t(pT[:, 4 * c:4 * c + 4, :].rearrange("p a n -> p (a n)"), USES * j + n + c + 1, (n + c) % 2)
                    if b == 2 and not last:
                        copy_t(xT[:].rearrange("p k n -> p (k n)"), USES * j + XT_USE + 1, 0)

            tile(0, first=True)
            with act.Fori(1, T - 1) as j:
                tile(j)
            tile(T - 1, last=True)
            copy_t(oT[:].rearrange("p k n -> p (k n)"), USES * (T - 1) + FINAL_OT + 1, 0)

        @block.tensor
        def _(pe):
            def free(bank, v):
                pe.wait_ge(t_free[bank], v)

            def make_xT(j):
                pe.wait_ge(xn_ready, j + 1)
                for k in range(K):
                    op = pe.transpose(TB[:, 0, P * k:P * k + P], xn[:, P * k:P * k + P], tab("ident"))
                op.then_inc(t_ready, 1)

            def make_q(v):
                free(0, v)
                for g in range(G):
                    for k in range(K):
                        op = pe.matmul(TB[:, 1, P * g:P * g + P], wq[:, k, P * g:P * g + P], xT[:, k, :],
                                       start=(k == 0), stop=(k == K - 1))
                op.then_inc(t_ready, 1)

            def make_k(i, b, g, first=False):
                if g == 0:
                    pe.wait_ge(ctx_split, i + 1)
                    if not first:
                        pe.wait_ge(kT_ready, 4 * i)
                if g == 1 and not first:
                    pe.wait_ge(v_ready, 2 * i - 1)
                if g == 2 and not first:
                    pe.wait_ge(v_ready, 2 * i)
                if g == 3:
                    pe.wait_ge(kT_ready, 4 * i + 1)
                for k in range(K):
                    op = passes(pe, KV[:, g % 3, 0:SKP], [w[:, k, P * g:P * g + P] for w in (wkh, wkl)],
                                [c[:, b % 2, k, :] for c in (ctxh, ctxl)], k == 0, k == K - 1)
                op.then_inc(kv_ready, 1)

            def make_v(i, b, kt):
                pe.wait_ge(kT_ready, 4 * i + 2 + kt)
                for k in range(K):
                    op = passes(pe, KV[:, 1 + kt, :], [c[:, b % 2, k, P * kt:P * kt + P] for c in (ctxh, ctxl)],
                                [w[:, k, :] for w in (wvh, wvl)], k == 0, k == K - 1)
                op.then_inc(kv_ready, 1)

            def scores(i, b, hf):
                pe.wait_ge(kT_ready, 4 * i + 2 * hf + 2)
                pe.wait_ge(masked, 2 * i + hf + 1)
                for g in range(2 * hf, 2 * hf + 2):
                    op = pe.matmul(SC[:, g % 2, 0:SK], qbd[:, b, g].rearrange("p h q -> p (h q)"), kT[:, b % 2, g, :],
                                   start=True, stop=True)
                op.then_inc(scores_ready, 1)

            pe.wait_ge(w_split, 2)
            for g in range(G):
                make_k(0, 0, g, first=True)
            make_v(0, 0, 0)
            make_v(0, 0, 1)
            pe.wait_ge(weights_in, WEIGHTS)
            for k in range(K):
                op = pe.matmul(O[0:B, 0, :], lastT[:, k, :], wv[:, k, :], start=(k == 0), stop=(k == K - 1))
            op.then_inc(vlast_done, 1)
            make_xT(0)
            make_q(1)
            pe.wait_ge(t_free[1], 1)

            def turn(j, n):
                free(n % 2, USES // 2 * j + n // 2)

            def output_T(j, n, o_done):
                pe.wait_ge(o_ready, o_done)
                turn(j, n)
                for k in range(K):
                    op = pe.transpose(TB[:, 0, P * k:P * k + P], o[:, P * k:P * k + P], tab("ident"))
                op.then_inc(t_ready, 1)

            def output(j, n):
                turn(j, n)
                free(0, USES // 2 * j + (n - 1) // 2 + 1)
                pe.wait_ge(wo_in, 32)
                for k in range(K):
                    op = pe.matmul(TB[:, 1, :], oT[:, k, :], wo[:, k, :], start=(k == 0), stop=(k == K - 1))
                op.then_inc(t_ready, 1)

            def tile(j, first=False, last=False):
                for b in range(NB):
                    i = NB * j + b
                    nb = (b + 1) % NB
                    more = not (last and b == NB - 1)
                    if b == NB - 1 and not last:
                        turn(j, Q_USE)
                        make_q(USES // 2 * j + XT_USE // 2 + 1)
                    scores(i, b, 0)
                    if more:
                        make_k(i + 1, nb, 0)
                        make_k(i + 1, nb, 1)
                    if b == 0 and not first:
                        output_T(j, OT_USE, NB * j + 1)
                    scores(i, b, 1)
                    if more:
                        make_k(i + 1, nb, 2)
                        make_k(i + 1, nb, 3)
                    if b == 0 and not first:
                        output(j, OUT_USE)
                    if more:
                        make_v(i + 1, nb, 0)
                    n = use(PT_USE[b], last)
                    pe.wait_ge(exp_done, 2 * i + 2)
                    for c in range(2):
                        turn(j, n + c)
                        for m in range(4):
                            g, kt = 2 * c + m // 2, m % 2
                            op = pe.transpose(TB[:, (n + c) % 2, P * m:P * m + P], sm[:, b % 2, g, P * kt:P * kt + P], tab("ident"))
                        op.then_inc(t_ready, 1)
                    if more:
                        make_v(i + 1, nb, 1)
                    pe.wait_ge(v_ready, 2 * i + 2)
                    if first and b == 0:
                        pe.wait_ge(vlast_ready, 1)
                    pe.wait_ge(o_ready, i + 1)
                    turn(j, n + 2)
                    turn(j, n + 3)
                    for g in range(G):
                        for kt in range(2):
                            op = pe.matmul(O[:, 0, P * g:P * g + P], pT[:, 2 * g + kt, :], v[:, b % 2, kt, P * g:P * g + P],
                                           start=(kt == 0), stop=(kt == 1), skip_group_check=True)
                    op.then_inc(pv_ready, 1)
                    if b == 2 and not last:
                        turn(j, XT_USE)
                        make_xT(j + 1)

            tile(0, first=True)
            with pe.Fori(1, T - 1) as j:
                tile(j)
            tile(T - 1, last=True)
            output_T(T - 1, FINAL_OT, NB * T + 1)
            output(T - 1, FINAL_OUT)


def router_tensor(pe, core, R, xT, rw, logits, r_ready, r_free, uses, rows_made, logits_made):
    for first in range(0, T, SL):
        for s in range(SL):
            rows_made(pe, first + s)
            pe.wait_ge(r_free[s], uses + first // SL + 1)
            for k in range(K):
                op = pe.transpose(R[s][:, P * k:P * k + P], core.rows[:, first + s, P * k:P * k + P], core.tab("ident"))
            op.then_inc(r_ready[s], 1)
        for s in range(SL):
            pe.wait_ge(r_free[s], uses + first // SL + 2)
            for k in range(K):
                op = pe.matmul(logits[:, E * (first + s):E * (first + s) + E], xT[s][:, k, :], rw[:, k, :], start=(k == 0), stop=(k == K - 1))
    op.then_inc(logits_made, 1)


def router_scalar(act, R, xT, lg, r_ready, r_free, uses, shifted, exp_done):
    for t in range(T):
        s = t % SL
        act.wait_ge(r_ready[s], uses + t // SL + 1)
        act.activation(xT[s][:].rearrange("p k n -> p (k n)"), R[s][:], ACT.Copy).then_inc(r_free[s], 1)
    act.wait_ge(shifted, 1)
    act.activation(lg[:], lg[:], ACT.Exp).then_inc(exp_done, 1)


def router_vector(dve, core, lg, lmax, lsum, linv, logits, bias, logits_made, shifted, exp_done):
    wide = lambda a: a[:].unsqueeze(2).to_broadcast([P, T, E])
    dve.drain()
    dve.wait_ge(logits_made, 1)
    made = logits[:, 0:T * E].rearrange("p (t e) -> p t e", e=E)
    if bias is None:
        dve.tensor_copy(lg[:], made)
    else:
        dve.tensor_tensor(lg[:], made, bias[:].unsqueeze(1).to_broadcast([P, T, E]), ALU.add)
    dve.drain()
    dve.tensor_reduce(lmax[:], lg[:], X, ALU.max, negate=True)
    dve.drain()
    dve.tensor_tensor(lg[:], lg[:], wide(lmax), ALU.add).then_inc(shifted, 1)
    dve.wait_ge(exp_done, 1)
    dve.tensor_reduce(lsum[:], lg[:], X, ALU.add)
    dve.drain()
    dve.reciprocal(linv[:], lsum[:])
    dve.drain()
    dve.tensor_tensor(core.probs[:], lg[:], wide(linv), ALU.mult)


def phase_self0(nc, core):
    A, x, tab = core.A, core.x, core.tab
    with ExitStack() as ctx:
        sb = lambda name, shape, dt=F32: ctx.enter_context(nc.sbuf_tensor("s0_" + name, shape, dt))
        sem = semaphores(nc, ctx, "s0_")
        sems = lambda name: [sem(f"{name}{s}") for s in range(SL)]
        LC = 3 * LAT

        wqkv = sb("wqkv", [P, K, 3 * D])
        latw = sb("latw", [P, K, LC])
        latb = sb("latb", [P, LC])
        latow = sb("latow", [P, 2, D])
        latob = sb("latob", [P, D])
        rw = sb("rw", [P, K, E])
        rb = sb("rb", [P, E])
        slots = lambda name, shape: [sb(f"{name}{s}", shape) for s in range(SL)]
        stats, mv, veps, rstd = slots("stats", [P, 6]), slots("mv", [P, 2]), slots("veps", [P, 1]), slots("rstd", [P, 1])
        mhalf = sb("mhalf", [P, 1])
        xn, xT = slots("xn", [P, D]), slots("xT", [P, K, P])
        qT, kT, kn, vn = slots("qT", [P, H, 32]), slots("kT", [P, LAT]), slots("kn", [P, D]), slots("vn", [P, D])
        qpad = slots("qpad", [P, H, 32])
        sm, pT = slots("sm", [P, H, S]), slots("pT", [P, H, S])
        nm, rs, ri = slots("nm", [P, H]), slots("rs", [P, H]), slots("ri", [P, H])
        ao, aoT = slots("ao", [P, LAT]), slots("aoT", [P, 2, P])
        lg, lmax, lsum, linv = sb("lg", [P, T, E]), sb("lmax", [P, T]), sb("lsum", [P, T]), sb("linv", [P, T])

        R = [ctx.enter_context(nc.psum_tensor(f"s0_R{s}", [P, 512], F32)) for s in range(SL)]
        AT = ctx.enter_context(nc.psum_tensor("s0_AT", [P, SL, 512], F32))

        wqkv_in, weights_in = sem("wqkv_in"), sem("weights_in")
        WEIGHTS = 16 * 6
        mhalf_set, qpad_zero = sem("mhalf_set"), sem("qpad_zero")
        var_ready, rstd_ready, xn_ready = sems("var_ready"), sems("rstd_ready"), sems("xn_ready")
        r_ready = sems("r_ready")
        r_free = sems("r_free")
        qT_ready, xn_added = sems("qT_ready"), sems("xn_added")
        heads_begun = sem("heads_begun")
        at_ready, at_free = sems("at_ready"), sems("at_free")
        shifted, exp_done, pT_ready = sems("shifted"), sems("exp_done"), sems("pT_ready")
        ao_ready = sems("ao_ready")
        logits_made, lshift, lexp = sem("logits_made"), sem("lshift"), sem("lexp")

        XT0, UQ, UK, UV, XT1, ULQK, ULV, UAO, UO = range(9)
        USES = 9
        SCORE0, PV0, SCORE1, PV1 = range(4)
        GROUPS = ((0, 1), (2, 3))

        block = ctx.enter_context(nc.Block())

        def ready(eng, s, it, n):
            eng.wait_ge(r_ready[s], USES * it + n + 1)

        def at_made(eng, s, it, n):
            eng.wait_ge(at_ready[s], 4 * it + n + 1)

        @block.sync
        def _(sp):
            sp.dma_start(wqkv[:], A["wqkv"].rearrange("(k p) n -> p k n", p=P)).then_inc(wqkv_in, 16)
            for t, a in ((latw, "lat_w"), (latow, "lat_ow"), (rw, "rw0")):
                sp.dma_start(t[:], A[a].rearrange("(k p) n -> p k n", p=P)).then_inc(weights_in, 16)
            for t, a in ((latb, "lat_b"), (latob, "lat_ob"), (rb, "rb0")):
                sp.dma_start(t[:], A[a].partition_broadcast(P)).then_inc(weights_in, 16)

        @block.gpsimd
        def _(pool):
            pool.memset(mhalf[:], -0.5).then_inc(mhalf_set, 1)
            pool.wait_ge(mhalf_set, 1)

            def rsqrt(k):
                def step(it, slots):
                    for s in slots:
                        pool.drain()
                        pool.wait_ge(var_ready[s], 2 * it + k + 1)
                        pool.tensor_tensor(rstd[s][:], veps[s][:], mhalf[:], ALU.pow).then_inc(rstd_ready[s], 1)
                return step

            def add_normed(it, slots):
                for s in slots:
                    pool.wait_ge(xn_ready[s], 2 * it + 2)
                    pool.tensor_tensor(x[:, ds(SL * it + s, 1), :].rearrange("p a d -> p (a d)"),
                                       x[:, ds(SL * it + s, 1), :].rearrange("p a d -> p (a d)"), xn[s][:], ALU.add).then_inc(xn_added[s], 1)
            for added in xn_added:
                pool.sem_inc(added, 1)
            for s in range(SL):
                last = pool.memset(qpad[s][:], 0.0)
            last.then_inc(qpad_zero, 1)
            with pool.Fori(0, T // SL) as it:
                staggered([rsqrt(0), None, None, rsqrt(1), add_normed, None, None, None, None], GROUPS, it)

        @block.vector
        def _(dve):
            def tile(it, s):
                return x[:, ds(SL * it + s, 1), :].rearrange("p a d -> p (a d)")

            def norm(it, slots, k):
                for s in slots:
                    dve.drain()
                    dve.bn_stats(stats[s][:], tile(it, s))
                for s in slots:
                    dve.drain()
                    dve.bn_aggr(mv[s][:], stats[s][:])
                for s in slots:
                    dve.drain()
                    dve.tensor_scalar(veps[s][:], mv[s][:, 1:2], EPS, None, ALU.add).then_inc(var_ready[s], 1)
                for s in slots:
                    dve.wait_ge(rstd_ready[s], 2 * it + k + 1)
                    if k == 0:
                        dve.wait_ge(xn_added[s], it + 1)
                    if k > 0:
                        ready(dve, s, it, XT0)
                    dve.tensor_scalar(xn[s][:], tile(it, s), mv[s][:, 0:1], rstd[s][:, 0:1],
                                      ALU.subtract, ALU.mult).then_inc(xn_ready[s], 1)

            def exps(it, slots, k):
                for s in slots:
                    dve.drain()
                    dve.wait_ge(exp_done[s], 2 * it + k + 1)
                    dve.transpose(pT[s][:].rearrange("p h q -> p (h q)"), sm[s][:].rearrange("p h q -> p (h q)")).then_inc(pT_ready[s], 1)
                    dve.tensor_reduce(rs[s][:], sm[s][:], X, ALU.add)
                for s in slots:
                    dve.drain()
                    dve.reciprocal(ri[s][:], rs[s][:])

            def norm0(it, slots):
                norm(it, slots, 0)

            def q_T(it, slots):
                for s in slots:
                    dve.drain()
                    ready(dve, s, it, UQ)
                    dve.transpose(qT[s][:].rearrange("p h q -> p (h q)"), R[s][:]).then_inc(r_free[s], 1)

            def softmax0(it, slots):
                for s in slots:
                    at_made(dve, s, it, SCORE0)
                    dve.scalar_tensor_tensor(sm[s][:], AT[:, s, :].rearrange("p (h k) -> p h k", h=H), float(DH) ** -0.5,
                                             tab("causal").unsqueeze(1).to_broadcast([P, H, S]), ALU.mult, ALU.min)\
                       .then_inc(at_free[s], 1)
                for s in slots:
                    dve.drain()
                    dve.tensor_reduce(nm[s][:], sm[s][:], X, ALU.max, negate=True)
                for s in slots:
                    dve.drain()
                    dve.tensor_tensor(sm[s][:], sm[s][:], nm[s][:].unsqueeze(2).to_broadcast([P, H, S]), ALU.add)\
                       .then_inc(shifted[s], 1)
                exps(it, slots, 0)

            def add_heads(it, slots):
                for s in slots:
                    dve.drain()
                    at_made(dve, s, it, PV0)
                    dve.tensor_tensor(sm[s][:], AT[:, s, :].rearrange("p (h k) -> p h k", h=H),
                                      ri[s][:].unsqueeze(2).to_broadcast([P, H, DH]), ALU.mult).then_inc(at_free[s], 1)
                for s in slots:
                    dve.drain()
                    dve.tensor_tensor(tile(it, s), tile(it, s), sm[s][:].rearrange("p h k -> p (h k)"), ALU.add)
                norm(it, slots, 1)

            def latent_qkv(it, slots):
                dve.wait_ge(weights_in, WEIGHTS)
                dve.wait_ge(qpad_zero, 1)
                for s in slots:
                    ready(dve, s, it, ULQK)
                    q = R[s][:, 0:LAT].rearrange("p (h e k) -> p h e k", e=2, k=KPH)
                    bias = latb[:, 0:LAT].rearrange("p (h e k) -> p h e k", e=2, k=KPH)
                    pad = qpad[s][:].rearrange("p (h e) k -> p h e k", e=2)
                    for e in range(2):
                        dve.tensor_tensor(pad[:, :, e, KPH * e:KPH * e + KPH], q[:, :, e, :], bias[:, :, e, :], ALU.add)
                    dve.tensor_tensor(kn[s][:, 0:LAT], R[s][:, LAT:2 * LAT], latb[:, LAT:2 * LAT], ALU.add)\
                       .then_inc(r_free[s], 1)
                    dve.drain()
                    dve.transpose(qT[s][:].rearrange("p h q -> p (h q)"), qpad[s][:].rearrange("p h q -> p (h q)"))
                    dve.transpose(kT[s][:], kn[s][:, 0:LAT]).then_inc(qT_ready[s], 1)
                for s in slots:
                    ready(dve, s, it, ULV)
                    dve.tensor_tensor(vn[s][:, 0:LAT], R[s][:, 0:LAT], latb[:, 2 * LAT:LC], ALU.add)\
                       .then_inc(r_free[s], 1)

            def softmax1(it, slots):
                for s in slots:
                    dve.drain()
                    at_made(dve, s, it, SCORE1)
                    dve.tensor_reduce(nm[s][:], AT[:, s, :].rearrange("p (h k) -> p h k", h=H), X, ALU.max, negate=True)
                for s in slots:
                    dve.drain()
                    dve.tensor_tensor(sm[s][:], AT[:, s, :].rearrange("p (h k) -> p h k", h=H),
                                      nm[s][:].unsqueeze(2).to_broadcast([P, H, S]), ALU.add).then_inc(at_free[s], 1)
                    dve.drain()
                    dve.sem_inc(shifted[s], 1)
                exps(it, slots, 1)

            def latent_out(it, slots):
                for s in slots:
                    dve.drain()
                    at_made(dve, s, it, PV1)
                    dve.tensor_tensor(ao[s][:].rearrange("p (h k) -> p h k", h=H), AT[:, s, 0:LAT].rearrange("p (h k) -> p h k", h=H),
                                      ri[s][:].unsqueeze(2).to_broadcast([P, H, KPH]), ALU.mult).then_inc(at_free[s], 1)
                    dve.drain()
                    dve.sem_inc(ao_ready[s], 1)

            def latent_biased(it, slots):
                for s in slots:
                    ready(dve, s, it, UO)
                    dve.tensor_tensor(core.rows[:, ds(SL * it + s, 1), :].rearrange("p a d -> p (a d)"), R[s][:], latob[:],
                                      ALU.add).then_inc(r_free[s], 1)

            for free in r_free + at_free:
                dve.sem_inc(free, 1)
            with dve.Fori(0, T // SL) as it:
                staggered([norm0, q_T, softmax0, add_heads, None, latent_qkv, softmax1, latent_out, latent_biased], GROUPS, it)
            router_vector(dve, core, lg, lmax, lsum, linv, AT[:, 0, :], rb, logits_made, lshift, lexp)

        @block.scalar
        def _(act):
            def copy(s, it, n, out, w):
                ready(act, s, it, n)
                act.activation(out, R[s][:, 0:w], ACT.Copy).then_inc(r_free[s], 1)

            def x_T(n):
                def step(it, slots):
                    for s in slots:
                        copy(s, it, n, xT[s][:].rearrange("p k n -> p (k n)"), D)
                return step

            def k_v(it, slots):
                for s in slots:
                    copy(s, it, UK, kn[s][:], D)
                for s in slots:
                    copy(s, it, UV, vn[s][:], D)

            def exps(k, scale):
                def step(it, slots):
                    for s in slots:
                        act.wait_ge(shifted[s], 2 * it + k + 1)
                        act.activation(sm[s][:], sm[s][:], ACT.Exp, scale=scale).then_inc(exp_done[s], 1)
                return step

            def o_T(it, slots):
                for s in slots:
                    copy(s, it, UAO, aoT[s][:].rearrange("p k n -> p (k n)"), LAT)

            with act.Fori(0, T // SL) as it:
                staggered([x_T(XT0), k_v, exps(0, 1.0), None, x_T(XT1), None, exps(1, float(KPH) ** -0.5), None, o_T], GROUPS, it)
            router_scalar(act, R, xT, lg, r_ready, r_free, USES * (T // SL), lshift, lexp)

        @block.tensor
        def _(pe):
            def free(s, it, n):
                pe.wait_ge(r_free[s], USES * it + n + 1)

            def read(s, it, n):
                pe.wait_ge(r_free[s], USES * it + n + 2)

            def transposes(s, it, n, src, count):
                free(s, it, n)
                for k in range(count):
                    op = pe.transpose(R[s][:, P * k:P * k + P], src[:, P * k:P * k + P], tab("ident"))
                op.then_inc(r_ready[s], 1)

            def product(s, it, n, lhs, rhs, w):
                free(s, it, n)
                for k in range(len(lhs)):
                    op = pe.matmul(R[s][:, 0:w], lhs[k], rhs[k], start=(k == 0), stop=(k == len(lhs) - 1))
                op.then_inc(r_ready[s], 1)

            def heads(it, n, s, lhs, rhs, w):
                pe.wait_ge(at_free[s], 4 * it + n + 1)
                pe.sem_inc(heads_begun, 1)
                for h in range(H):
                    for b in range(NB):
                        rows = slice(S * b, S * b + S)
                        op = pe.matmul(AT[rows, s, w * h:w * h + w], lhs(rows, h), rhs(rows, h), start=(h == 0), stop=(h == H - 1),
                                       skip_group_check=True)
                op.then_inc(at_ready[s], 1)

            def x_T(k, n):
                def step(it, slots):
                    for s in slots:
                        pe.wait_ge(xn_ready[s], 2 * it + k + 1)
                        transposes(s, it, n, xn[s], K)
                return step

            def qkv(it, slots):
                pe.wait_ge(wqkv_in, 16)
                for n, c in ((UQ, 0), (UK, 1), (UV, 2)):
                    for s in slots:
                        product(s, it, n, [xT[s][:, k, :] for k in range(K)],
                                [wqkv[:, k, D * c:D * c + D] for k in range(K)], D)

            def scores0(it, slots):
                for s in slots:
                    read(s, it, UK)
                    heads(it, SCORE0, s, lambda r, h: qT[s][r, h, :], lambda r, h: kn[s][r, 32 * h:32 * h + 32], 32)

            def sum0(it, slots):
                for s in slots:
                    read(s, it, UV)
                    pe.wait_ge(pT_ready[s], 2 * it + 1)
                    heads(it, PV0, s, lambda r, h: pT[s][r, h, :], lambda r, h: vn[s][r, 32 * h:32 * h + 32], 32)

            def latent_qkv(it, slots):
                pe.wait_ge(weights_in, WEIGHTS)
                for n, c, w in ((ULQK, 0, 2 * LAT), (ULV, 2 * LAT, LAT)):
                    for s in slots:
                        product(s, it, n, [xT[s][:, k, :] for k in range(K)],
                                [latw[:, k, c:c + w] for k in range(K)], w)

            def scores1(it, slots):
                for s in slots:
                    pe.wait_ge(qT_ready[s], it + 1)
                    heads(it, SCORE1, s, lambda r, h: qT[s][r, h, :], lambda r, h: kT[s][r, 32 * (h // 2):32 * (h // 2) + 32], 32)

            def sum1(it, slots):
                for s in slots:
                    read(s, it, ULV)
                    pe.wait_ge(pT_ready[s], 2 * it + 2)
                    heads(it, PV1, s, lambda r, h: pT[s][r, h, :], lambda r, h: vn[s][r, KPH * h:KPH * h + KPH], KPH)

            def out(it, slots):
                for s in slots:
                    pe.wait_ge(ao_ready[s], it + 1)
                    transposes(s, it, UAO, ao[s], 2)
                for s in slots:
                    read(s, it, UAO)
                    product(s, it, UO, [aoT[s][:, k, :] for k in range(2)], [latow[:, k, :] for k in range(2)], D)

            with pe.Fori(0, T // SL) as it:
                staggered([x_T(0, XT0), qkv, scores0, sum0, x_T(1, XT1), latent_qkv, scores1, sum1, out], GROUPS, it)

            def rows_made(pe, t):
                pe.wait_ge(r_free[t % SL], USES * (t // SL) + UO + 2)
            pe.wait_ge(at_free[0], 4 * (T // SL) + 1)
            router_tensor(pe, core, R, xT, rw, AT[:, 0, :], r_ready, r_free, USES * (T // SL), rows_made, logits_made)


def phase_mixture(nc, core, n, F, biased, eps, scale, prefetch=None, out=None):
    A, tab, probs, x = core.A, core.tab, core.probs, core.x
    TE = T * E
    NF, NC = F // P, F // 512
    HALF = 2
    PIECES = 2 * NC * HALF
    RING = 4
    w1d, w2d = A[f"w1_{n}"], A[f"w2_{n}"]
    with ExitStack() as ctx:
        sb = lambda name, shape, dt=F32: ctx.enter_context(nc.sbuf_tensor(f"x{n}_{name}", shape, dt))
        sem = semaphores(nc, ctx, f"x{n}_")
        psum = lambda name, banks: ctx.enter_context(nc.psum_tensor(f"x{n}_{name}", [P, banks, 512], F32))
        top, idx = sb("top", [P, T, E]), sb("idx", [P, T, E], U32)
        idxf = sb("idxf", [P, T, 2])
        pick = sb("pick", [P, 2, T, E])
        both = sb("both", [P, T, E])
        wsum, winv = sb("wsum", [P, T]), sb("winv", [P, T])
        off = sb("off", [P, T + 1, E])
        over = sb("over", [P, E, E])
        tiles = sb("tiles", [P, E])
        upto, first = sb("upto", [P, E]), sb("first", [P, E])
        pos, posk = sb("pos", [P, T, E]), sb("posk", [P, T, E])
        slotf = sb("slotf", [P, 2, T])
        cmp = sb("cmp", [1, ST, E])
        owner = sb("owner", [1, ST])
        if biased:
            b1 = sb("b1", [P, E, NF])
            b2 = sb("b2", [E, D])
            mix = sb("mix", [P, T, E])
            mixT = sb("mixT", [E, T, P])
        w1h, w1l = sb("w1h", [P, K, F], F32R), sb("w1l", [P, K, F], F32R)
        w2h, w2l = sb("w2h", [P, NF, D], F32R), sb("w2l", [P, NF, D], F32R)
        stage = sb("stage", [P, RING, HALF, 512])
        xh, xl = sb("xh", [P, K, P], F32R), sb("xl", [P, K, P], F32R)
        hh, hl = sb("hh", [P, NF, P], F32R), sb("hl", [P, NF, P], F32R)
        h = [core.rows[:, c, :] for c in range(2)]
        g = [core.rows[:, 2 + c, :] for c in range(2)]
        xf, xg, y = (core.rows[:, c, :] for c in (4, 5, 6))

        RP, HP, TP, XP, YP = psum("RP", 2), psum("HP", 2), psum("TP", 2), psum("XP", 1), psum("YP", 1)

        picked, counted, routed, sent = sem("picked"), sem("counted"), sem("routed"), sem("sent")
        bias_in, mixed, mixT_made, mixT_copied, b2_made, b2_added = (
            sem(a) for a in ("bias_in", "mixed", "mixT_made", "mixT_copied", "b2_made", "b2_added"))
        piece_in = [sem(f"piece_in{r}") for r in range(RING)]
        split = sem("split")
        rows_in, xT_made, xh_made, xl_made = sem("rows_in"), sem("xT_made"), sem("xh_made"), sem("xl_made")
        xf_made = sem("xf_made")
        h_made = sem("h_made")
        h_copied, hT_made, g_made, hh_made, hl_made = (sem(a) for a in ("h_copied", "hT_made", "g_made", "hh_made", "hl_made"))
        y_part = sem("y_part")
        y_copied, y_stored = sem("y_copied"), sem("y_stored")
        come = [sem(f"come{r}") for r in range(2 * RING)]
        weighed, stored = sem("weighed"), sem("stored")

        block = ctx.enter_context(nc.Block())

        def run_tiles(eng, experts, ahead, middle, end):
            def stage(work, m, c, e):
                work(m + c // NC, c % NC, e[c // NC])

            def step(m, last=False):
                e = (experts(m), None if last else experts(m + 1))
                for c in range(NC):
                    for work, later in ((ahead, 2), (middle, 1), (end, 0)):
                        if not (last and c + later >= NC):
                            stage(work, m, c + later, e)
            e = (experts(0), None)
            ahead(0, 0, e[0])
            ahead(0, 1, e[0])
            middle(0, 0, e[0])
            step(0)
            with eng.Fori(1, ST - 2) as m:
                step(m)
            step(ST - 2)
            step(ST - 1, last=True)

        def opens_next(m, c):
            return c == NC - 1 and not (isinstance(m, int) and m == ST - 1)

        def wait_count(eng, sem, value):
            if not (isinstance(value, int) and value < 1):
                eng.wait_ge(sem, value)

        def piece(q):
            chunk = q // HALF % NC
            half = q % HALF * (4 // HALF)
            return q < NC * HALF, chunk, half

        @block.sync
        def _(sp):
            if biased:
                sp.dma_start(b1[:], A["b1T"]).then_inc(bias_in, 16)
                sp.dma_start(b2[:], A["b2_0"]).then_inc(bias_in, 16)

            def loads(e, first):
                for q in range(PIECES):
                    if not (first and q < RING):
                        sp.wait_ge(split, PIECES * e + q - RING + 1)
                    is_w1, c, k = piece(q)
                    if is_w1:
                        src = w1d[ds(e, 1)].rearrange("a (k p) f -> p (a k) f", p=P)[:, k:k + 2, 512 * c:512 * c + 512]
                    else:
                        src = w2d[ds(e, 1)].rearrange("a (k p) d -> p (a k) d", p=P)[:, 4 * c + k:4 * c + k + 2, :]
                    sp.dma_start(stage[:, q % RING], src).then_inc(piece_in[q % RING], 16)
            loads(0, True)
            sp.wait_ge(sent, 16 * 2 * T)
            with sp.Fori(1, E) as e:
                loads(e, False)
            if prefetch:
                prefetch(sp)
            if out is not None:
                for t in range(T):
                    sp.wait_ge(weighed, 2 * t + 2)
                    sp.dma_start(out[t * P:t * P + P, :], x[:, t, :]).then_inc(stored, 16)
                sp.wait_ge(stored, 16 * T)

        @block.vector
        def _(dve):
            for t in range(T):
                dve.max(top[:, t, :], probs[:, t, :])
            dve.drain()
            for t in range(T):
                dve.max_index(idx[:, t, :], top[:, t, :], probs[:, t, :])
            dve.drain()
            dve.tensor_copy(idxf[:], idx[:, :, 0:2])
            dve.tensor_tensor(wsum[:], top[:, :, 0], top[:, :, 1], ALU.add)
            dve.drain()
            if eps:
                dve.tensor_scalar(wsum[:], wsum[:], eps, None, ALU.add)
                dve.drain()
            dve.reciprocal(winv[:], wsum[:])
            for k in range(2):
                dve.tensor_tensor(pick[:, k], tab("expert_id").unsqueeze(1).to_broadcast([P, T, E]),
                                  idxf[:, :, k:k + 1].to_broadcast([P, T, E]), ALU.is_equal)
            dve.drain()
            dve.tensor_tensor(both[:], pick[:, 0], pick[:, 1], ALU.add).then_inc(picked, 1)
            dve.tensor_tensor(core.gate[:], top[:, :, 0:2], winv[:].unsqueeze(2).to_broadcast([P, T, 2]), ALU.mult)
            if scale != 1.0:
                dve.drain()
                dve.tensor_scalar(core.gate[:], core.gate[:], scale, None, ALU.mult)
            dve.memset(off[:, 0, :], 0.0)
            dve.wait_ge(counted, 1)
            for t in range(T):
                dve.drain()
                dve.tensor_tensor(off[:, t + 1, :], off[:, t, :], RP[:, 1, E * t:E * t + E], ALU.add)
            dve.drain()
            dve.tensor_tensor(over[:], off[:, T, :].unsqueeze(2).to_broadcast([P, E, E]),
                              tab("step128").unsqueeze(1).to_broadcast([P, E, E]), ALU.is_gt)
            dve.tensor_tensor(pos[:], off[:, 0:T, :], RP[:, 0, 0:TE].rearrange("p (t e) -> p t e", e=E), ALU.add)
            dve.drain()
            dve.tensor_reduce(tiles[:], over[:], X, ALU.add)
            dve.drain()
            dve.tensor_tensor(over[:], tab("upto").rearrange("p (a b) -> p a b", a=E),
                              tiles[:].unsqueeze(1).to_broadcast([P, E, E]), ALU.mult)
            dve.drain()
            dve.tensor_reduce(upto[:], over[:], X, ALU.add)
            dve.drain()
            dve.tensor_tensor(first[:], upto[:], tiles[:], ALU.subtract)
            dve.tensor_tensor(cmp[:], upto[0:1, :].unsqueeze(1).to_broadcast([1, ST, E]),
                              tab("tile_id")[0:1, :].unsqueeze(2).to_broadcast([1, ST, E]), ALU.is_le)
            dve.drain()
            dve.tensor_reduce(owner[:], cmp[:], X, ALU.add)
            dve.tensor_copy(core.tiles_before[:], first[0:1, :])
            dve.drain()
            dve.tensor_scalar(first[:], first[:], float(P), None, ALU.mult)
            dve.tensor_scalar(core.expert_of[:], owner[:], float(E - 1), None, ALU.min)
            dve.drain()
            dve.tensor_tensor(pos[:], pos[:], first[:].unsqueeze(1).to_broadcast([P, T, E]), ALU.add)
            for k in range(2):
                dve.drain()
                dve.tensor_tensor(posk[:], pos[:], pick[:, k], ALU.mult)
                dve.drain()
                dve.tensor_reduce(slotf[:, k, :], posk[:], X, ALU.add)
            dve.drain()
            dve.tensor_copy(core.slot[:], slotf[:]).then_inc(routed, 1)
            if biased:
                for k in range(2):
                    dve.tensor_tensor(pick[:, k], pick[:, k], core.gate[:, :, k:k + 1].to_broadcast([P, T, E]), ALU.mult)
                dve.drain()
                dve.tensor_tensor(mix[:], pick[:, 0], pick[:, 1], ALU.add).then_inc(mixed, 1)

            def splits(e, first):
                if not first:
                    before = dve.value_load(core.tiles_before[0:1, ds(e, 1)], min_val=0, max_val=ST)
                for q in range(PIECES):
                    is_w1, c, k = piece(q)
                    if is_w1:
                        high, low = (w[:, k:k + 2, 512 * c:512 * c + 512] for w in (w1h, w1l))
                    else:
                        high, low = (w[:, 4 * c + k:4 * c + k + 2, :] for w in (w2h, w2l))
                    dve.wait_ge(piece_in[q % RING], 16 * (PIECES // RING) * e + 16 * (q // RING) + 16)
                    if not first and q % HALF == 0:
                        dve.wait_ge(h_made if is_w1 else y_part, before * NC + (c + 1))
                    dve.tensor_copy(high, stage[:, q % RING])
                    dve.drain()
                    dve.tensor_tensor(low, stage[:, q % RING], high.bitcast(F32), ALU.subtract).then_inc(split, 1)
            splits(0, True)
            with dve.Fori(1, E) as e:
                splits(e, False)
            if biased:
                for c in range(2):
                    dve.wait_ge(mixT_made, c + 1)
                    dve.tensor_copy(mixT[:, 4 * c:4 * c + 4, :].rearrange("p t n -> p (t n)"), TP[0:E, c, :]).then_inc(mixT_copied, 1)
            for t in range(T):
                if biased:
                    dve.drain()
                    dve.wait_ge(b2_made, t + 1)
                    dve.tensor_tensor(x[:, t, :], x[:, t, :], RP[:, t % 2, :], ALU.add).then_inc(b2_added, 1)
                for k in range(2):
                    r = (2 * t + k) % (2 * RING)
                    dve.drain()
                    dve.wait_ge(come[r], 16 * ((2 * t + k) // (2 * RING)) + 16)
                    dve.scalar_tensor_tensor(x[:, t, :], stage[:, r // 2, r % 2, :], core.gate[:, t, k:k + 1], x[:, t, :],
                                             ALU.mult, ALU.add).then_inc(weighed, 1)

        @block.gpsimd
        def _(pool):
            pool.wait_ge(routed, 1)
            for t in range(T):
                for k in range(2):
                    pool.indirect_dma_start(core.sent[n], bass.IndirectOffsetOnAxis(ap=core.slot[:, k, t:t + 1], axis=0),
                                            core.rows[:, t, :], None).then_inc(sent, 16)

            def low_x(m):
                pool.wait_ge(xh_made, m + 1)
                pool.tensor_tensor(xl[:].rearrange("p k n -> p (k n)"), xf, xh[:].rearrange("p k n -> p (k n)").bitcast(F32),
                                   ALU.subtract).then_inc(xl_made, 1)

            def ahead(m, c, e):
                if opens_next(m, c):
                    low_x(m + 1)

            def middle(m, c, e):
                pool.wait_ge(hh_made, NC * m + c + 1)
                pool.tensor_tensor(hl[:, 4 * c:4 * c + 4, :].rearrange("p k n -> p (k n)"), g[c % 2],
                                   hh[:, 4 * c:4 * c + 4, :].rearrange("p k n -> p (k n)").bitcast(F32), ALU.subtract)\
                    .then_inc(hl_made, 1)
            low_x(0)
            run_tiles(pool, lambda m: None, ahead, middle, lambda m, c, e: None)
            pool.wait_ge(y_stored, 16 * ST)
            pool.wait_ge(split, PIECES * E)
            for i in range(2 * T):
                r = i % (2 * RING)
                if i >= 2 * RING:
                    pool.wait_ge(weighed, i - 2 * RING + 1)
                pool.indirect_dma_start(stage[:, r // 2, r % 2, :], None, core.back[n],
                                        bass.IndirectOffsetOnAxis(ap=core.slot[:, i % 2, i // 2:i // 2 + 1], axis=0)).then_inc(come[r], 16)

        @block.scalar
        def _(act):
            def fetch(m):
                act.dma_start(xg, core.sent[n][ds(m * P, P), :]).then_inc(rows_in, 16)

            def x_T(m):
                act.wait_ge(xT_made, m + 1)
                act.activation(xf, XP[:, 0, :], ACT.Copy).then_inc(xf_made, 1)
                fetch(m + 1)

            def high_x(m):
                act.wait_ge(xf_made, m + 1)
                act.activation(xh[:].rearrange("p k n -> p (k n)"), xf, ACT.Copy).then_inc(xh_made, 1)

            def ahead(m, c, e):
                if opens_next(m, c):
                    x_T(m + 1)
                act.wait_ge(h_made, NC * m + c + 1 + NC)
                act.activation(h[c % 2], HP[:, c % 2, :], ACT.Copy).then_inc(h_copied, 1)
                if opens_next(m, c):
                    high_x(m + 1)

            def middle(m, c, e):
                act.wait_ge(hT_made, NC * m + c + 1)
                wait_count(act, hl_made, NC * m + c - 1)
                if biased:
                    for k in range(4):
                        op = act.activation(g[c % 2][:, P * k:P * k + P], TP[:, c % 2, P * k:P * k + P], ACT.Gelu,
                                            bias=b1[:, ds(e, 1), 4 * c + k:4 * c + k + 1].rearrange("p a b -> p (a b)"))
                else:
                    op = act.activation(g[c % 2], TP[:, c % 2, :], ACT.Gelu)
                op.then_inc(g_made, 1)
                act.wait_ge(g_made, NC * m + c + 1)
                act.activation(hh[:, 4 * c:4 * c + 4, :].rearrange("p k n -> p (k n)"), g[c % 2], ACT.Copy).then_inc(hh_made, 1)

            def end(m, c, e):
                if c == NC - 1:
                    wait_count(act, y_stored, 16 * m)
                    act.wait_ge(y_part, NC * m + 2 * NC)
                    act.activation(y, YP[:, 0, :], ACT.Copy).then_inc(y_copied, 1)
                    act.wait_ge(y_copied, m + 2)
                    act.dma_start(core.back[n][ds(m * P, P), :], y).then_inc(y_stored, 16)

            act.wait_ge(sent, 16 * 2 * T)
            if biased:
                act.wait_ge(bias_in, 32)
            act.sem_inc(y_copied, 1)
            fetch(0)
            x_T(0)
            high_x(0)
            run_tiles(act, lambda m: act.value_load(core.expert_of[0:1, ds(m, 1)], min_val=0, max_val=E - 1) if biased else None,
                      ahead, middle, end)
            act.wait_ge(y_stored, 16 * ST)
            act.wait_ge(rows_in, 16 * (ST + 1))

        @block.tensor
        def _(pe):
            pe.wait_ge(picked, 1)
            flat = both[:].rearrange("p t e -> p (t e)")
            pe.matmul(RP[:, 0, 0:TE], tab("before"), flat, start=True, stop=True)
            pe.matmul(RP[:, 1, 0:TE], tab("ones"), flat, start=True, stop=True).then_inc(counted, 1)
            pe.sem_inc(h_made, NC)
            pe.sem_inc(y_part, NC)
            def rows_T(m):
                pe.wait_ge(rows_in, 16 * m + 16)
                for k in range(K):
                    op = pe.transpose(XP[:, 0, P * k:P * k + P], xg[:, P * k:P * k + P], tab("ident"))
                op.then_inc(xT_made, 1)

            def ahead(m, c, e):
                if opens_next(m, c):
                    rows_T(m + 1)
                cols = slice(512 * c, 512 * c + 512)
                pe.wait_ge(split, e * PIECES + HALF * (c + 1))
                wait_count(pe, h_copied, NC * m + c - 1)
                if c == 0:
                    pe.wait_ge(xh_made, m + 1)
                for k in range(K):
                    pe.matmul(HP[:, c % 2, :], xh[:, k, :], w1l[:, k, cols], start=(k == 0), stop=False)
                    pe.matmul(HP[:, c % 2, :], xh[:, k, :], w1h[:, k, cols], start=False, stop=False)
                if c == 0:
                    pe.wait_ge(xl_made, m + 1)
                for k in range(K):
                    op = pe.matmul(HP[:, c % 2, :], xl[:, k, :], w1h[:, k, cols], start=False, stop=(k == K - 1))
                op.then_inc(h_made, 1)

            def middle(m, c, e):
                pe.wait_ge(h_copied, NC * m + c + 1)
                wait_count(pe, g_made, NC * m + c - 1)
                for k in range(4):
                    op = pe.transpose(TP[:, c % 2, P * k:P * k + P], h[c % 2][:, P * k:P * k + P], tab("ident"))
                op.then_inc(hT_made, 1)

            def end(m, c, e):
                if c == 0:
                    pe.wait_ge(y_copied, m + 1)
                pe.wait_ge(split, e * PIECES + HALF * (NC + c + 1))
                pe.wait_ge(hh_made, NC * m + c + 1)
                for k in range(4 * c, 4 * c + 4):
                    pe.matmul(YP[:, 0, :], hh[:, k, :], w2l[:, k, :], start=(k == 0), stop=False)
                    pe.matmul(YP[:, 0, :], hh[:, k, :], w2h[:, k, :], start=False, stop=False)
                pe.wait_ge(hl_made, NC * m + c + 1)
                for k in range(4 * c, 4 * c + 4):
                    op = pe.matmul(YP[:, 0, :], hl[:, k, :], w2h[:, k, :], start=False, stop=(k == NF - 1))
                op.then_inc(y_part, 1)

            rows_T(0)
            run_tiles(pe, lambda m: pe.value_load(core.expert_of[0:1, ds(m, 1)], min_val=0, max_val=E - 1), ahead, middle, end)
            if biased:
                pe.wait_ge(mixed, 1)
                pe.wait_ge(bias_in, 32)
                for c in range(2):
                    for t in range(4):
                        op = pe.transpose(TP[0:E, c, P * t:P * t + P], mix[:, 4 * c + t, :], tab("ident"))
                    op.then_inc(mixT_made, 1)
                pe.wait_ge(mixT_copied, 2)
                for t in range(T):
                    if t >= 2:
                        pe.wait_ge(b2_added, t - 1)
                    pe.matmul(RP[:, t % 2, :], mixT[:, t, :], b2[:], start=True, stop=True).then_inc(b2_made, 1)


class ContextInputs:

    def __init__(self, nc, ctx, A):
        sb = lambda name, shape: ctx.enter_context(nc.sbuf_tensor("l1_" + name, shape, F32))
        sem = semaphores(nc, ctx, "l1in_")
        self.A = A
        self.wqkv, self.wo, self.rw = sb("wqkv", [P, K, 4 * HS]), sb("wo", [P, 2, D]), sb("rw", [P, K, E])
        self.ctxl = sb("ctxl", [B, D])
        self.ctxT = sb("ctxT", [P, 2, NB, K, SKP])
        self.weights_in = sem("weights_in")
        self.ctxT_in = [[sem(f"ctxT_in{e}{b}") for b in range(NB)] for e in range(2)]

    def load_ctxT(self, sp, j, e, b):
        sp.dma_start(self.ctxT[:, e, b], self.A["ctxT"][ds(j * NB + b, 1), :, :]
                     .rearrange("a p n -> p (a n)").rearrange("p (k n) -> p k n", k=K)).then_inc(self.ctxT_in[e][b], 16)

    def load(self, sp):
        for t, a in ((self.wqkv, "wqkv1"), (self.wo, "wo1"), (self.rw, "rw1")):
            sp.dma_start(t[:], self.A[a].rearrange("(k p) n -> p k n", p=P)).then_inc(self.weights_in, 16)
        sp.dma_start(self.ctxl[:], self.A["ctx"].rearrange("b k d -> b (k d)")[:, (SK - 1) * D:SK * D]).then_inc(self.weights_in, 16)
        for j in range(2):
            for b in range(NB):
                self.load_ctxT(sp, j, j, b)


def phase_layer1(nc, core, inputs):
    A, x, tab = core.A, core.x, core.tab
    with ExitStack() as ctx:
        sb = lambda name, shape, dt=F32: ctx.enter_context(nc.sbuf_tensor("l1_" + name, shape, dt))
        sem = semaphores(nc, ctx, "l1_")
        sems = lambda name: [sem(f"{name}{s}") for s in range(SL)]
        slots = lambda name, shape: [sb(f"{name}{s}", shape) for s in range(SL)]
        W3 = 3 * HS

        wqkv, wo, rw, ctxT, ctxl = inputs.wqkv, inputs.wo, inputs.rw, inputs.ctxT, inputs.ctxl
        ctxn = sb("ctxn", [P, 2, NB, 2, D])
        stats, mv, veps, rstd = slots("stats", [P, 6]), slots("mv", [P, 2]), slots("veps", [P, 1]), slots("rstd", [P, 1])
        mhalf = sb("mhalf", [P, 1])
        xn, xT = slots("xn", [P, D]), slots("xT", [P, K, P])
        ls, lsl, lT = slots("ls", [P, SK]), slots("lsl", [P, 32]), slots("lT", [P, 3, P])
        nm, rs, ri = slots("nm", [P, 2]), slots("rs", [P, 2]), slots("ri", [P, 2])
        ex = slots("ex", [P, D])
        t1, t2, r, v, rT = (slots(a, s) for a, s in (("t1", [P, W3]), ("t2", [P, W3]), ("r", [P, W3]), ("v", [P, HS]), ("rT", [P, 3, P])))
        sm, pT = slots("sm", [P, 2, P]), slots("pT", [P, 2, P])
        o, oT = slots("o", [P, 2 * HS]), slots("oT", [P, 2, P])
        lg, lmax, lsum, linv = sb("lg", [P, T, E]), sb("lmax", [P, T]), sb("lsum", [P, T]), sb("linv", [P, T])

        R = [ctx.enter_context(nc.psum_tensor(f"l1_R{s}", [P, 512], F32)) for s in range(SL)]
        LS = ctx.enter_context(nc.psum_tensor("l1_LS", [P, SL, 512], F32))

        weights_in, ctxT_in = inputs.weights_in, inputs.ctxT_in
        WEIGHTS = 16 * 4
        ctxn_in = [[sem(f"ctxn_in{e}{b}") for b in range(NB)] for e in range(2)]
        mhalf_set = sem("mhalf_set")
        var_ready, rstd_ready, xn_ready, rows_made = sems("var_ready"), sems("rstd_ready"), sems("xn_ready"), sems("rows_made")
        r_ready = sems("r_ready")
        r_free = sems("r_free")
        ls_ready, ls_free, lin_used = sem("ls_ready"), sem("ls_free"), sem("lin_used")
        lsl_ready = sems("lsl_ready")
        fmax, fexp = sems("fmax"), sems("fexp")
        r_made, shifted, exp_done = sems("r_made"), sems("shifted"), sems("exp_done")
        logits_made, lshift, lexp = sem("logits_made"), sem("lshift"), sem("lexp")

        XT0, LT, LO, XT1, QKV, RT, SC, PTT, PV, OT, WO = range(11)
        USES = 11
        GROUPS = ((0,), (1,), (2, 3))
        block = ctx.enter_context(nc.Block())

        def ready(eng, s, it, n):
            eng.wait_ge(r_ready[s], USES * it + n + 1)

        @block.sync
        def _(sp):
            def load_ctxT(j, e):
                for b in range(NB):
                    sp.wait_ge(ls_ready, NB * (j - 2) + b + 1)
                    inputs.load_ctxT(sp, j, e, b)

            def load_ctxn(j, e, first=False):
                for b in range(NB):
                    if not first:
                        sp.wait_ge(lin_used, NB * (j - 2) + b + 1)
                    sp.dma_start(ctxn[:, e, b], A["ctx"][ds(j * NB + b, 1), 0:2 * P, :]
                                 .rearrange("a (k p) d -> p (a k) d", p=P)).then_inc(ctxn_in[e][b], 16)

            def loads(q, first=False, last=False):
                for e in range(2):
                    load_ctxn(2 * q + e, e, first)
                if not last:
                    for e in range(2):
                        load_ctxT(2 * q + 2 + e, e)
            loads(0, first=True)
            with sp.Fori(1, T // 2 - 1) as q:
                loads(q)
            loads(T // 2 - 1, last=True)

        @block.gpsimd
        def _(pool):
            pool.memset(mhalf[:], -0.5).then_inc(mhalf_set, 1)
            pool.wait_ge(mhalf_set, 1)
            def rsqrt(k):
                def step(it, slots):
                    for s in slots:
                        pool.drain()
                        pool.wait_ge(var_ready[s], 3 * it + k + 1)
                        pool.tensor_tensor(rstd[s][:], veps[s][:], mhalf[:], ALU.pow).then_inc(rstd_ready[s], 1)
                return step

            with pool.Fori(0, T // SL) as it:
                staggered([rsqrt(0), None, None, rsqrt(1), None, None, None, None, None, None, None, rsqrt(2)], GROUPS, it)

        @block.vector
        def _(dve):
            def tile(it, s):
                return x[:, ds(SL * it + s, 1), :].rearrange("p a d -> p (a d)")

            def norm(it, slots, k):
                for s in slots:
                    dve.drain()
                    dve.bn_stats(stats[s][:], tile(it, s))
                for s in slots:
                    dve.drain()
                    dve.bn_aggr(mv[s][:], stats[s][:])
                for s in slots:
                    dve.drain()
                    dve.tensor_scalar(veps[s][:], mv[s][:, 1:2], EPS, None, ALU.add).then_inc(var_ready[s], 1)
                for s in slots:
                    dve.wait_ge(rstd_ready[s], 3 * it + k + 1)
                    if k == 1:
                        ready(dve, s, it, XT0)
                    normed = xn[s][:] if k < 2 else core.rows[:, ds(SL * it + s, 1), :].rearrange("p a d -> p (a d)")
                    dve.tensor_scalar(normed, tile(it, s), mv[s][:, 0:1], rstd[s][:, 0:1],
                                      ALU.subtract, ALU.mult).then_inc(xn_ready[s] if k < 2 else rows_made[s], 1)

            def norm0(it, slots):
                norm(it, slots, 0)

            def last_score(it, slots):
                for s in slots:
                    dve.drain()
                    dve.wait_ge(ls_free, SL * it + s + 1)
                    dve.tensor_scalar(lsl[s][:], tab("eye_tile").rearrange("p (t n) -> p t n", n=32)[:, ds(SL * it + s, 1), :]
                                      .rearrange("p a n -> p (a n)"), ls[s][:, SK - 1:SK], None, ALU.mult).then_inc(lsl_ready[s], 1)

            def feature_softmax(it, slots):
                for s in slots:
                    dve.drain()
                    ready(dve, s, it, LO)
                    dve.tensor_reduce(nm[s][:, 0:1], R[s][:], X, ALU.max, negate=True).then_inc(fmax[s], 1)
                for s in slots:
                    dve.wait_ge(fexp[s], it + 1)
                    dve.reciprocal(ri[s][:, 0:1], rs[s][:, 0:1])
                for s in slots:
                    dve.drain()
                    dve.scalar_tensor_tensor(tile(it, s), ex[s][:], ri[s][:, 0:1], tile(it, s), ALU.mult, ALU.add)
                norm(it, slots, 1)

            def rotate(it, slots):
                for s in slots:
                    dve.drain()
                    ready(dve, s, it, QKV)
                    q = R[s][:, 0:W3]
                    pair = lambda a: a.rearrange("p (h i c) -> p h i c", h=3, c=2)
                    wide = lambda name: tab(name).rearrange("p (i c) -> p i c", c=2).unsqueeze(1)
                    dve.tensor_tensor(t1[s][:].rearrange("p (h i) -> p h i", h=3), q.rearrange("p (h i) -> p h i", h=3),
                                      tab("cos").unsqueeze(1).to_broadcast([P, 3, HS]), ALU.mult)
                    for c in range(2):
                        dve.tensor_tensor(pair(t2[s][:])[:, :, :, c], pair(q)[:, :, :, 1 - c],
                                          wide("sin")[:, :, :, c].to_broadcast([P, 3, HS // 2]), ALU.mult)
                    dve.tensor_copy(v[s][:], R[s][:, W3:W3 + HS]).then_inc(r_free[s], 1)
                    dve.drain()
                    dve.tensor_tensor(r[s][:], t1[s][:], t2[s][:], ALU.add).then_inc(r_made[s], 1)

            def softmax(it, slots):
                for s in slots:
                    dve.drain()
                    ready(dve, s, it, SC)
                    dve.scalar_tensor_tensor(sm[s][:], R[s][:, 0:2 * P].rearrange("p (h k) -> p h k", h=2), float(HS) ** -0.5,
                                             tab("block_causal").unsqueeze(1).to_broadcast([P, 2, P]), ALU.mult, ALU.add)\
                       .then_inc(r_free[s], 1)
                for s in slots:
                    dve.drain()
                    dve.tensor_reduce(nm[s][:], sm[s][:], X, ALU.max, negate=True)
                for s in slots:
                    dve.drain()
                    dve.tensor_tensor(sm[s][:], sm[s][:], nm[s][:].unsqueeze(2).to_broadcast([P, 2, P]), ALU.add)\
                       .then_inc(shifted[s], 1)
                for s in slots:
                    dve.drain()
                    dve.wait_ge(exp_done[s], it + 1)
                    dve.tensor_reduce(rs[s][:], sm[s][:], X, ALU.add)
                for s in slots:
                    dve.drain()
                    dve.reciprocal(ri[s][:], rs[s][:])

            def heads(it, slots):
                for s in slots:
                    dve.drain()
                    ready(dve, s, it, PV)
                    dve.tensor_tensor(o[s][:].rearrange("p (h c) -> p h c", h=2), R[s][:, 0:2 * HS].rearrange("p (h c) -> p h c", h=2),
                                      ri[s][:].unsqueeze(2).to_broadcast([P, 2, HS]), ALU.mult).then_inc(r_free[s], 1)

            def add_heads(it, slots):
                for s in slots:
                    ready(dve, s, it, WO)
                    dve.tensor_tensor(tile(it, s), tile(it, s), R[s][:], ALU.add).then_inc(r_free[s], 1)
                norm(it, slots, 2)

            for free in r_free:
                dve.sem_inc(free, 1)
            with dve.Fori(0, T // SL) as it:
                staggered([norm0, last_score, None, feature_softmax, None, rotate, None, softmax, None, heads, None, add_heads], GROUPS, it)
            router_vector(dve, core, lg, lmax, lsum, linv, LS[:, 0, :], None, logits_made, lshift, lexp)

        @block.scalar
        def _(act):
            def copy(s, it, n, out, w):
                ready(act, s, it, n)
                act.activation(out, R[s][:, 0:w], ACT.Copy).then_inc(r_free[s], 1)

            def copies(n, out, w):
                def step(it, slots):
                    for s in slots:
                        copy(s, it, n, out[s][:].rearrange("p k n -> p (k n)"), w)
                return step

            def scores(it, slots):
                for s in slots:
                    act.wait_ge(ls_ready, NB * (SL * it + s) + NB)
                    act.activation(ls[s][:], LS[:, s, 0:SK], ACT.Copy, scale=float(D) ** -0.5).then_inc(ls_free, 1)

            def scores_T(it, slots):
                for s in slots:
                    ready(act, s, it, LT)
                    act.activation(lT[s][0:32, 2, :], R[s][0:32, 2 * P:3 * P], ACT.Copy)
                    act.activation(lT[s][:, 0:2, :].rearrange("p k n -> p (k n)"), R[s][:, 0:2 * P], ACT.Copy)\
                       .then_inc(r_free[s], 1)

            def feature_exp(it, slots):
                for s in slots:
                    act.wait_ge(fmax[s], it + 1)
                    act.activation(ex[s][:], R[s][:], ACT.Exp, bias=nm[s][:, 0:1], accum_out=rs[s][:, 0:1]).then_inc(r_free[s], 1)
                    act.drain()
                    act.sem_inc(fexp[s], 1)

            def exps(it, slots):
                for s in slots:
                    act.wait_ge(shifted[s], it + 1)
                    act.activation(sm[s][:], sm[s][:], ACT.Exp).then_inc(exp_done[s], 1)

            with act.Fori(0, T // SL) as it:
                staggered([copies(XT0, xT, D), scores, scores_T, feature_exp, copies(XT1, xT, D), None, copies(RT, rT, 3 * P), exps,
                           copies(PTT, pT, 2 * P), None, copies(OT, oT, 2 * P), None], GROUPS, it)
            router_scalar(act, R, xT, lg, r_ready, r_free, USES * (T // SL), lshift, lexp)

        @block.tensor
        def _(pe):
            def free(s, it, n):
                pe.wait_ge(r_free[s], USES * it + n + 1)

            def read(s, it, n):
                pe.wait_ge(r_free[s], USES * it + n + 2)

            def transposes(s, it, n, src, count):
                free(s, it, n)
                for k in range(count):
                    op = pe.transpose(R[s][:, P * k:P * k + P], src[:, P * k:P * k + P], tab("ident"))
                op.then_inc(r_ready[s], 1)

            def product(s, it, n, lhs, rhs, w):
                free(s, it, n)
                for k in range(len(lhs)):
                    op = pe.matmul(R[s][:, 0:w], lhs[k], rhs[k], start=(k == 0), stop=(k == len(lhs) - 1))
                op.then_inc(r_ready[s], 1)

            def x_T(k, n):
                def step(it, slots):
                    for s in slots:
                        pe.wait_ge(xn_ready[s], 2 * it + k + 1)
                        transposes(s, it, n, xn[s][:], K)
                return step

            def scores(it, slots):
                for s in slots:
                    read(s, it, XT0)
                    for b in range(NB):
                        pe.wait_ge(ctxT_in[s % 2][b], 16 * (SL // 2 * it + s // 2) + 16)
                        rows = slice(S * b, S * b + S)
                        for k in range(K):
                            op = pe.matmul(LS[rows, s, 0:SK], xT[s][:, k, rows], ctxT[:, s % 2, b, k, 0:SK], start=(k == 0), stop=(k == K - 1))
                        op.then_inc(ls_ready, 1)

            def scores_T(it, slots):
                for s in slots:
                    pe.wait_ge(lsl_ready[s], it + 1)
                    free(s, it, LT)
                    for k in range(2):
                        pe.transpose(R[s][:, P * k:P * k + P], ls[s][:, P * k:P * k + P], tab("ident"))
                    pe.transpose(R[s][0:32, 2 * P:3 * P], lsl[s][:], tab("ident")).then_inc(r_ready[s], 1)

            def linear(it, slots):
                pe.wait_ge(weights_in, WEIGHTS)
                for s in slots:
                    read(s, it, LT)
                    pe.matmul(R[s][:], lT[s][0:32, 2, :], ctxl[:], start=True, stop=True, skip_group_check=True)
                    for b in range(NB):
                        rows = slice(S * b, S * b + S)
                        pe.wait_ge(ctxn_in[s % 2][b], 16 * (SL // 2 * it + s // 2) + 16)
                        for k in range(2):
                            op = pe.matmul(R[s][rows, :], lT[s][:, k, rows], ctxn[:, s % 2, b, k, :], start=False, stop=(k == 1),
                                           skip_group_check=True)
                        op.then_inc(lin_used, 1)
                    pe.drain()
                    pe.sem_inc(r_ready[s], 1)

            def qkv(it, slots):
                for s in slots:
                    product(s, it, QKV, [xT[s][:, k, :] for k in range(K)], [wqkv[:, k, :] for k in range(K)], 4 * HS)

            def rotated_T(it, slots):
                for s in slots:
                    pe.wait_ge(r_made[s], it + 1)
                    transposes(s, it, RT, r[s][:], 3)

            def head_scores(it, slots):
                for s in slots:
                    free(s, it, SC)
                    for hd in range(2):
                        op = pe.matmul(R[s][:, P * hd:P * hd + P], rT[s][:, hd, :], rT[s][:, 2, :], start=True, stop=True)
                    op.then_inc(r_ready[s], 1)

            def exps_T(it, slots):
                for s in slots:
                    pe.wait_ge(exp_done[s], it + 1)
                    transposes(s, it, PTT, sm[s][:].rearrange("p h k -> p (h k)"), 2)

            def sums(it, slots):
                for s in slots:
                    free(s, it, PV)
                    for hd in range(2):
                        op = pe.matmul(R[s][:, HS * hd:HS * hd + HS], pT[s][:, hd, :], v[s][:], start=True, stop=True)
                    op.then_inc(r_ready[s], 1)

            def heads_T(it, slots):
                for s in slots:
                    transposes(s, it, OT, o[s][:], 2)

            def out(it, slots):
                for s in slots:
                    product(s, it, WO, [oT[s][:, k, :] for k in range(2)], [wo[:, k, :] for k in range(2)], D)

            with pe.Fori(0, T // SL) as it:
                staggered([x_T(0, XT0), scores, scores_T, linear, x_T(1, XT1), qkv, rotated_T, head_scores, exps_T, sums, heads_T, out], GROUPS, it)
            pe.wait_ge(ls_free, T)
            router_tensor(pe, core, R, xT, rw, LS[:, 0, :], r_ready, r_free, USES * (T // SL),
                          lambda pe, t: pe.wait_ge(rows_made[t % SL], t // SL + 1), logits_made)


def build(nc, A, out):
    with ExitStack() as ctx:
        core = Core(nc, ctx, A)
        phase_cross0(nc, core)
        phase_self0(nc, core)
        with ExitStack() as early:
            inputs = ContextInputs(nc, early, A)
            phase_mixture(nc, core, 0, F0, True, 1e-8, 0.3, prefetch=inputs.load)
            phase_layer1(nc, core, inputs)
        phase_mixture(nc, core, 1, F1, False, 0.0, 1.0, out=out.rearrange("b s d -> (b s) d"))


def layout(**inputs):
    a = {k: np.asarray(v) for k, v in inputs.items()}
    c = np.ascontiguousarray
    rowvec = lambda v: c(v.reshape(1, -1))
    ctx = a["ctx_1024"]
    ctxT = np.zeros((B, D, SKP), ctx.dtype)
    ctxT[:, :, :SK] = ctx.transpose(0, 2, 1)
    heads = lambda w: w.reshape(w.shape[:-1] + (H, DH))[..., :KPH].reshape(w.shape[:-1] + (LAT,))
    d = {
        "tables": tables(),
        "x": c(a["x"].reshape(B * S, D)),
        "ctx": c(ctx),
        "ctxT": c(ctxT.reshape(B, K, P, SKP).transpose(0, 2, 1, 3).reshape(B, P, K * SKP)),
        "ctx_lastT": c(ctx[:, SK - 1, :].T.reshape(K, P, B).transpose(1, 0, 2)),
        "mask": c(a["mask_Bx1xS2_if1"].reshape(T, NB * SK)),
        "wq": a["L0_xattn_Wq"], "wk": a["L0_xattn_Wk"], "wv": a["L0_xattn_Wv"], "wo": a["L0_xattn_Wo"],
        "bqT": c(a["L0_xattn_bq"].reshape(G, P).T), "bkT": c(a["L0_xattn_bk"].reshape(G, P).T),
        "bv": a["L0_xattn_bv"], "bo": a["L0_xattn_bo"],
        "wqkv": a["L0_attn_qkv_weights"],
        "lat_w": c(np.concatenate([heads(a["L0_ffn_q_w"]), a["L0_ffn_k_w"], a["L0_ffn_v_w"]], axis=1)),
        "lat_b": c(np.concatenate([heads(a["L0_ffn_q_b"]), a["L0_ffn_k_b"], a["L0_ffn_v_b"]])),
        "lat_ow": c(a["L0_ffn_o_w"][:LAT]), "lat_ob": a["L0_ffn_o_b"],
        "rw0": a["L0_ffn_router_w"], "rb0": a["L0_ffn_router_b"],
        "w1_0": a["L0_ffn_w1"], "b1T": c(a["L0_ffn_b1"].reshape(E, F0 // P, P).transpose(2, 0, 1)), "w2_0": a["L0_ffn_w2"], "b2_0": a["L0_ffn_b2"],
        "wqkv1": c(np.concatenate([a["L1_attn_Wq"].reshape(2 * HS, D), a["L1_attn_Wk"], a["L1_attn_Wv"]], axis=0).T),
        "wo1": c(a["L1_attn_Wo"].T),
        "rw1": c(a["L1_ffn_router_w"].T),
        "w1_1": a["L1_ffn_w1"], "w2_1": a["L1_ffn_w2"],
    }
    return {k: c(v) for k, v in d.items()}


def kernel(**inputs):
    import concourse.bacc as bacc
    from concourse.bass_utils import run_bass_kernel_spmd

    nc = bacc.Bacc("TRN2", target_bir_lowering=False, num_devices=1)
    arrays = {f"in_{k}": v for k, v in layout(**inputs).items()}
    A = {k[3:]: nc.dram_tensor(k, v.shape, mybir.dt.from_np(v.dtype), kind="ExternalInput").ap() for k, v in arrays.items()}
    out = nc.dram_tensor("out", (B, S, D), F32, kind="ExternalOutput").ap()
    build(nc, A, out)
    r = run_bass_kernel_spmd(nc, [arrays], core_ids=[0])
    return r.results[0]["out"]
```
